# Optimizing a Trainium2 kernel written in Bass

```python
import numpy as np
import jax
import jax.numpy as jnp

def _softmax(x, axis=-1):
    return jax.nn.softmax(x, axis=axis)

def _gelu(x):
    return jax.nn.gelu(x, approximate=True)

def _silu(x):
    return jax.nn.silu(x)

def _sigmoid(x):
    return jax.nn.sigmoid(x)

def _layernorm(x, axis=-1, eps=1e-05):
    m = jnp.mean(x, axis=axis, keepdims=True)
    v = jnp.var(x, axis=axis, keepdims=True)
    return (x - m) / jnp.sqrt(v + eps)

def _scatter_add(tgt, idx, src, axis=0):
    return tgt.at[idx].add(src)

def _segment_sum(src, seg, n):
    return jax.ops.segment_sum(src, seg, n)
kernel_name = 'mk_adaln_d4_jaxref_r8_b19b7d'

def setup_inputs(seed: int=0):
    np.random.seed(seed)
    _w = jnp.asarray

    def _L0_attn_setup():
        import jax, jax.numpy as jnp
        import numpy as np
        E = 128
        D = 64
        H = E // D
        EPS = 1e-05
        key = jax.random.key(seed)
        ks = jax.random.split(key, 8)
        std = 0.02
        x = jax.random.normal(ks[0], (2, 128, E), jnp.float32)
        Wq = jax.random.normal(ks[1], (E, E), jnp.float32) * std
        Wk = jax.random.normal(ks[2], (E, E), jnp.float32) * std
        Wv = jax.random.normal(ks[3], (E, E), jnp.float32) * std
        Wo = jax.random.normal(ks[4], (E, E), jnp.float32) * std
        delta = jnp.full((E,), float(np.log(0.99 / 0.01)), jnp.float32)
        G1 = jax.random.normal(ks[5], (E, D), jnp.float32) * std
        G2 = jax.random.normal(ks[6], (D, E), jnp.float32) * std
        norm_w = jnp.ones((E,), jnp.float32)
        return {'x': x, 'Wq': Wq, 'Wk': Wk, 'Wv': Wv, 'Wo': Wo, 'delta': delta, 'G1': G1, 'G2': G2, 'norm_w': norm_w}
    _L0_attn_in = _L0_attn_setup()

    def _L0_ffn_setup():
        import jax, jax.numpy as jnp
        import numpy as np
        D_IN, D_HID = (128, 512)

        def _ternary(key, shape):
            return jax.random.randint(key, shape, -1, 2).astype(jnp.float32)

        def _tlin(x, w, s):
            return jnp.einsum('bsi,oi->bso', x, w) * s
        key = jax.random.key(seed)
        ks = jax.random.split(key, 12)
        inv = lambda fan: 1.0 / np.sqrt(fan).astype(np.float32)
        return {'x': jax.random.normal(ks[0], (4, 256, D_IN), dtype=jnp.float32), 'w1_w': _ternary(ks[1], (D_HID, D_IN)), 'w1_s': jax.random.uniform(ks[2], (D_HID,), dtype=jnp.float32) * inv(D_IN), 'w2_w': _ternary(ks[3], (D_HID, D_IN)), 'w2_s': jax.random.uniform(ks[4], (D_HID,), dtype=jnp.float32) * inv(D_IN), 'h1_w': _ternary(ks[5], (D_HID, D_HID)), 'h1_s': jax.random.uniform(ks[6], (D_HID,), dtype=jnp.float32) * inv(D_HID), 'h2_w': _ternary(ks[7], (D_HID, D_HID)), 'h2_s': jax.random.uniform(ks[8], (D_HID,), dtype=jnp.float32) * inv(D_HID), 'w3_w': _ternary(ks[9], (D_IN, D_HID)), 'w3_s': jax.random.uniform(ks[10], (D_IN,), dtype=jnp.float32) * inv(D_HID)}
    _L0_ffn_in = _L0_ffn_setup()
    _L0_c = _w((lambda *s: np.random.randn(*s).astype(np.float32) * 0.05)(2, 128))
    _L0_wmod = _w((lambda *s: np.random.randn(*s).astype(np.float32) * 0.05)(128, 6 * 128) * 128 ** (-0.5))

    def _L1_attn_setup():
        import jax, jax.numpy as jnp
        import numpy as np
        D_MODEL = 128
        N_HEADS = 4
        KEY_DIM = 128
        VALUE_DIM = 256
        DK = KEY_DIM // N_HEADS
        DV = VALUE_DIM // N_HEADS
        LOW_RANK = 16
        GATE_NORM = 16.0
        EPS = 1e-05

        def _gla_scan(q, k, v, gk):
            B, H, L, dk = q.shape
            dv = v.shape[-1]
            qs = jnp.moveaxis(q, 2, 0)
            ks_ = jnp.moveaxis(k, 2, 0)
            vs = jnp.moveaxis(v, 2, 0)
            gs = jnp.moveaxis(gk, 2, 0)

            def step(S, inp):
                q_t, k_t, v_t, g_t = inp
                S = S * jnp.exp(g_t)[..., None] + k_t[..., None] * v_t[..., None, :]
                o_t = jnp.einsum('bhk,bhkv->bhv', q_t, S)
                return (S, o_t)
            S0 = jnp.zeros((B, H, dk, dv), q.dtype)
            _, os = jax.lax.scan(step, S0, (qs, ks_, vs, gs))
            return jnp.moveaxis(os, 0, 2)
        key = jax.random.key(seed)
        ks = jax.random.split(key, 10)
        B, L = (2, 256)
        gain = 2.0 ** (-2.5)

        def xavier(k, shape, g=gain):
            fan_in, fan_out = (shape[0], shape[1])
            a = g * np.sqrt(6.0 / (fan_in + fan_out))
            return jax.random.uniform(k, shape, jnp.float32, -a, a)
        return {'x': jax.random.normal(ks[0], (B, L, D_MODEL), jnp.float32), 'Wq': xavier(ks[1], (D_MODEL, KEY_DIM)), 'Wk': xavier(ks[2], (D_MODEL, KEY_DIM)), 'Wv': xavier(ks[3], (D_MODEL, VALUE_DIM)), 'Wg': xavier(ks[4], (D_MODEL, VALUE_DIM)), 'gk_w1': xavier(ks[5], (D_MODEL, LOW_RANK)), 'gk_w2': xavier(ks[6], (LOW_RANK, KEY_DIM)), 'gk_b2': jnp.zeros((KEY_DIM,), jnp.float32), 'g_norm_w': jnp.ones((DV,), jnp.float32), 'Wo': xavier(ks[7], (VALUE_DIM, D_MODEL))}
    _L1_attn_in = _L1_attn_setup()

    def _L1_ffn_setup():
        import jax, jax.numpy as jnp
        import numpy as np
        B, S, D, H = (8, 128, 128, 512)
        E, R = (3, 8)
        SCALING = 1.0 / R

        def _mole(x, W, b, A, Bm, Rw):
            gates = jax.nn.softmax(jnp.einsum('bsd,de->bse', x, Rw), axis=-1)
            base = jnp.einsum('bsd,dh->bsh', x, W) + b
            z = jnp.einsum('bsd,edr->ebsr', x, A)
            zg = z * jnp.transpose(gates, (2, 0, 1))[..., None]
            lora = jnp.einsum('ebsr,erh->bsh', zg, Bm)
            return base + SCALING * lora
        key = jax.random.key(seed)
        ks = jax.random.split(key, 12)
        s = lambda k, shape, scale: jax.random.normal(k, shape, dtype=jnp.float32) * scale
        return {'x': s(ks[0], (B, S, D), 1.0), 'W1': s(ks[1], (D, H), D ** (-0.5)), 'b1': jnp.zeros((H,), jnp.float32), 'A1': s(ks[2], (E, D, R), D ** (-0.5)), 'B1': s(ks[3], (E, R, H), 0.0) + s(ks[4], (E, R, H), R ** (-0.5)), 'R1': s(ks[5], (D, E), D ** (-0.5)), 'W2': s(ks[6], (H, D), H ** (-0.5)), 'b2': jnp.zeros((D,), jnp.float32), 'A2': s(ks[7], (E, H, R), H ** (-0.5)), 'B2': s(ks[8], (E, R, D), R ** (-0.5)), 'R2': s(ks[9], (H, E), H ** (-0.5))}
    _L1_ffn_in = _L1_ffn_setup()
    _L1_c = _w((lambda *s: np.random.randn(*s).astype(np.float32) * 0.05)(2, 128))
    _L1_wmod = _w((lambda *s: np.random.randn(*s).astype(np.float32) * 0.05)(128, 6 * 128) * 128 ** (-0.5))

    def _L2_attn_setup():
        import jax, jax.numpy as jnp
        from jax import lax
        import numpy as np
        INPUT_DIM, STATE_DIM, CONV_K, EXPAND = (128, 16, 4, 2)
        INNER = INPUT_DIM * EXPAND
        BATCH, SEQ = (2, 256)
        key = jax.random.key(seed)
        ks = jax.random.split(key, 6)
        x = jax.random.normal(ks[0], (BATCH, SEQ, INPUT_DIM), jnp.float32)
        W_in = jax.random.normal(ks[1], (2 * INNER, INPUT_DIM), jnp.float32) * 0.02
        conv_w = jax.random.normal(ks[2], (INNER, 1, CONV_K), jnp.float32) * 0.1
        conv_b = jnp.zeros((INNER,), jnp.float32)
        A_log = jax.random.normal(ks[3], (INNER, STATE_DIM), jnp.float32)
        D = jnp.ones((INNER,), jnp.float32)
        W_out = jax.random.normal(ks[4], (INPUT_DIM, INNER), jnp.float32) * 0.02
        return {'x': x, 'W_in': W_in, 'conv_w': conv_w, 'conv_b': conv_b, 'A_log': A_log, 'D': D, 'W_out': W_out}
    _L2_attn_in = _L2_attn_setup()

    def _L2_ffn_setup():
        import jax, jax.numpy as jnp
        import numpy as np
        D_IN, D_HID = (128, 512)

        def _ternary(key, shape):
            return jax.random.randint(key, shape, -1, 2).astype(jnp.float32)

        def _tlin(x, w, s):
            return jnp.einsum('bsi,oi->bso', x, w) * s
        key = jax.random.key(seed)
        ks = jax.random.split(key, 12)
        inv = lambda fan: 1.0 / np.sqrt(fan).astype(np.float32)
        return {'x': jax.random.normal(ks[0], (4, 256, D_IN), dtype=jnp.float32), 'w1_w': _ternary(ks[1], (D_HID, D_IN)), 'w1_s': jax.random.uniform(ks[2], (D_HID,), dtype=jnp.float32) * inv(D_IN), 'w2_w': _ternary(ks[3], (D_HID, D_IN)), 'w2_s': jax.random.uniform(ks[4], (D_HID,), dtype=jnp.float32) * inv(D_IN), 'h1_w': _ternary(ks[5], (D_HID, D_HID)), 'h1_s': jax.random.uniform(ks[6], (D_HID,), dtype=jnp.float32) * inv(D_HID), 'h2_w': _ternary(ks[7], (D_HID, D_HID)), 'h2_s': jax.random.uniform(ks[8], (D_HID,), dtype=jnp.float32) * inv(D_HID), 'w3_w': _ternary(ks[9], (D_IN, D_HID)), 'w3_s': jax.random.uniform(ks[10], (D_IN,), dtype=jnp.float32) * inv(D_HID)}
    _L2_ffn_in = _L2_ffn_setup()
    _L2_c = _w((lambda *s: np.random.randn(*s).astype(np.float32) * 0.05)(2, 128))
    _L2_wmod = _w((lambda *s: np.random.randn(*s).astype(np.float32) * 0.05)(128, 6 * 128) * 128 ** (-0.5))

    def _L3_attn_setup():
        import jax, jax.numpy as jnp
        import numpy as np
        N_HEADS = 16
        INPUT_DIM = 128
        EMBED_DIM = 128
        KEY_DIM = EMBED_DIM // N_HEADS
        BATCH = 4
        SEQ = 256

        def _uniform(key, shape, bound):
            return jax.random.uniform(key, shape, jnp.float32, -bound, bound)
        key = jax.random.key(seed)
        kq, k1, k2, k3, k4 = jax.random.split(key, 5)
        stdv_k = 1.0 / np.sqrt(KEY_DIM)
        stdv_e = 1.0 / np.sqrt(EMBED_DIM)
        return {'q': jax.random.normal(kq, (BATCH, SEQ, INPUT_DIM), jnp.float32), 'W_query': _uniform(k1, (N_HEADS, INPUT_DIM, KEY_DIM), stdv_k), 'W_key': _uniform(k2, (N_HEADS, INPUT_DIM, KEY_DIM), stdv_k), 'W_val': _uniform(k3, (N_HEADS, INPUT_DIM, KEY_DIM), stdv_k), 'W_out': _uniform(k4, (N_HEADS, KEY_DIM, EMBED_DIM), stdv_e)}
    _L3_attn_in = _L3_attn_setup()

    def _L3_ffn_setup():
        import jax, jax.numpy as jnp
        import numpy as np
        DIM = 128
        DEPTH = 6
        HEADS = 16
        DIM_HEAD = 64
        WINDOW = 32
        INNER = HEADS * DIM_HEAD
        DIM_INNER = int(DIM * 4 * 2 / 3)
        QK_SCALE = 8.0

        def shift_tokens(t):
            a, s = jnp.split(t, 2, -1)
            s = jnp.pad(s, ((0, 0), (1, 0), (0, 0)))[:, :-1]
            return jnp.concatenate([a, s], -1)

        def l2norm(t):
            return t / jnp.maximum(jnp.linalg.norm(t, axis=-1, keepdims=True), 1e-12)

        def rotate_half(x):
            x1, x2 = jnp.split(x, 2, -1)
            return jnp.concatenate([-x2, x1], -1)

        def rotary_tables(n):
            half = jnp.arange(0, DIM_HEAD, 2, dtype=jnp.float32)
            inv_freq = 1.0 / 10000.0 ** (half / DIM_HEAD)
            t = jnp.arange(n, dtype=jnp.float32)
            freqs = t[:, None] * inv_freq[None, :]
            freqs = jnp.concatenate([freqs, freqs], -1)
            base_scale = (half + 0.4 * DIM_HEAD) / (1.4 * DIM_HEAD)
            power = (t - n // 2) / (WINDOW // 2)
            scale = base_scale[None, :] ** power[:, None]
            scale = jnp.concatenate([scale, scale], -1)
            return (freqs, scale)

        def local_attention(q, k, v):
            b, h, n, d = q.shape
            w = WINDOW
            nw = n // w
            bq = q.reshape(b, h, nw, w, d)
            bk = k.reshape(b, h, nw, w, d)
            bv = v.reshape(b, h, nw, w, d)

            def look(t):
                p = jnp.pad(t, ((0, 0), (0, 0), (1, 0), (0, 0), (0, 0)))
                return jnp.concatenate([p[:, :, :nw], p[:, :, 1:]], axis=3)
            bk2, bv2 = (look(bk), look(bv))
            seq = jnp.arange(n).reshape(nw, w)
            seq_p = jnp.pad(seq, ((1, 0), (0, 0)), constant_values=-1)
            jt = jnp.concatenate([seq_p[:nw], seq_p[1:]], axis=1)
            it = seq[:, :, None]
            jb = jt[:, None, :]
            mask = (it < jb) | (it > jb + w) | (jb == -1)
            sim = jnp.einsum('bhwie,bhwje->bhwij', bq, bk2) * QK_SCALE
            sim = jnp.where(mask, -jnp.finfo(sim.dtype).max, sim)
            attn = jax.nn.softmax(sim, -1)
            out = jnp.einsum('bhwij,bhwje->bhwie', attn, bv2)
            return out.reshape(b, h, n, d)

        def attn_layer(x, Wqkv, qs, ksc, Wo):
            b, n, _ = x.shape
            qkv = x @ Wqkv
            q, k, v = jnp.split(qkv, 3, -1)
            sh = lambda t: t.reshape(b, n, HEADS, DIM_HEAD).transpose(0, 2, 1, 3)
            q, k, v = (sh(q), sh(k), sh(v))
            q = l2norm(q) * qs
            k = l2norm(k) * ksc
            freqs, scale = rotary_tables(n)
            cos, sin = (jnp.cos(freqs), jnp.sin(freqs))
            q = q * cos * scale + rotate_half(q) * sin * scale
            inv = 1.0 / scale
            k = k * cos * inv + rotate_half(k) * sin * inv
            out = local_attention(q, k, v)
            out = out.transpose(0, 2, 1, 3).reshape(b, n, INNER)
            return out @ Wo

        def ffn_layer(x, g, bln, W1, b1, W2, b2):
            mu = x.mean(-1, keepdims=True)
            var = ((x - mu) ** 2).mean(-1, keepdims=True)
            xn = (x - mu) / jnp.sqrt(var + 1e-05) * g + bln
            hg = xn @ W1 + b1
            a, gate = jnp.split(hg, 2, -1)
            return a * jax.nn.gelu(gate, approximate=False) @ W2 + b2
        key = jax.random.key(seed)
        ks = jax.random.split(key, 8)
        B, N = (2, 256)
        init = lambda k, shape: jax.random.normal(k, shape, jnp.float32) * 0.02
        return {'x': jax.random.normal(ks[0], (B, N, DIM), jnp.float32), 'Wqkv': init(ks[1], (DEPTH, DIM, 3 * INNER)), 'q_scale': jnp.ones((DEPTH, DIM_HEAD), jnp.float32), 'k_scale': jnp.ones((DEPTH, DIM_HEAD), jnp.float32), 'Wo': init(ks[2], (DEPTH, INNER, DIM)), 'ln_g': jnp.ones((DEPTH, DIM), jnp.float32), 'ln_b': jnp.zeros((DEPTH, DIM), jnp.float32), 'W1': init(ks[3], (DEPTH, DIM, 2 * DIM_INNER)), 'b1': jnp.zeros((DEPTH, 2 * DIM_INNER), jnp.float32), 'W2': init(ks[4], (DEPTH, DIM_INNER, DIM)), 'b2': jnp.zeros((DEPTH, DIM), jnp.float32)}
    _L3_ffn_in = _L3_ffn_setup()
    _L3_c = _w((lambda *s: np.random.randn(*s).astype(np.float32) * 0.05)(2, 128))
    _L3_wmod = _w((lambda *s: np.random.randn(*s).astype(np.float32) * 0.05)(128, 6 * 128) * 128 ** (-0.5))
    _d = {'L0_attn_x': _L0_attn_in['x'], 'L0_attn_Wq': _L0_attn_in['Wq'], 'L0_attn_Wk': _L0_attn_in['Wk'], 'L0_attn_Wv': _L0_attn_in['Wv'], 'L0_attn_Wo': _L0_attn_in['Wo'], 'L0_attn_delta': _L0_attn_in['delta'], 'L0_attn_G1': _L0_attn_in['G1'], 'L0_attn_G2': _L0_attn_in['G2'], 'L0_attn_norm_w': _L0_attn_in['norm_w'], 'L0_ffn_w1_w': _L0_ffn_in['w1_w'], 'L0_ffn_w1_s': _L0_ffn_in['w1_s'], 'L0_ffn_w2_w': _L0_ffn_in['w2_w'], 'L0_ffn_w2_s': _L0_ffn_in['w2_s'], 'L0_ffn_h1_w': _L0_ffn_in['h1_w'], 'L0_ffn_h1_s': _L0_ffn_in['h1_s'], 'L0_ffn_h2_w': _L0_ffn_in['h2_w'], 'L0_ffn_h2_s': _L0_ffn_in['h2_s'], 'L0_ffn_w3_w': _L0_ffn_in['w3_w'], 'L0_ffn_w3_s': _L0_ffn_in['w3_s'], 'L0_c': _L0_c, 'L0_wmod': _L0_wmod, 'L1_attn_Wq': _L1_attn_in['Wq'], 'L1_attn_Wk': _L1_attn_in['Wk'], 'L1_attn_Wv': _L1_attn_in['Wv'], 'L1_attn_Wg': _L1_attn_in['Wg'], 'L1_attn_gk_w1': _L1_attn_in['gk_w1'], 'L1_attn_gk_w2': _L1_attn_in['gk_w2'], 'L1_attn_gk_b2': _L1_attn_in['gk_b2'], 'L1_attn_g_norm_w': _L1_attn_in['g_norm_w'], 'L1_attn_Wo': _L1_attn_in['Wo'], 'L1_ffn_W1': _L1_ffn_in['W1'], 'L1_ffn_b1': _L1_ffn_in['b1'], 'L1_ffn_A1': _L1_ffn_in['A1'], 'L1_ffn_B1': _L1_ffn_in['B1'], 'L1_ffn_R1': _L1_ffn_in['R1'], 'L1_ffn_W2': _L1_ffn_in['W2'], 'L1_ffn_b2': _L1_ffn_in['b2'], 'L1_ffn_A2': _L1_ffn_in['A2'], 'L1_ffn_B2': _L1_ffn_in['B2'], 'L1_ffn_R2': _L1_ffn_in['R2'], 'L1_c': _L1_c, 'L1_wmod': _L1_wmod, 'L2_attn_W_in': _L2_attn_in['W_in'], 'L2_attn_conv_w': _L2_attn_in['conv_w'], 'L2_attn_conv_b': _L2_attn_in['conv_b'], 'L2_attn_A_log': _L2_attn_in['A_log'], 'L2_attn_D': _L2_attn_in['D'], 'L2_attn_W_out': _L2_attn_in['W_out'], 'L2_ffn_w1_w': _L2_ffn_in['w1_w'], 'L2_ffn_w1_s': _L2_ffn_in['w1_s'], 'L2_ffn_w2_w': _L2_ffn_in['w2_w'], 'L2_ffn_w2_s': _L2_ffn_in['w2_s'], 'L2_ffn_h1_w': _L2_ffn_in['h1_w'], 'L2_ffn_h1_s': _L2_ffn_in['h1_s'], 'L2_ffn_h2_w': _L2_ffn_in['h2_w'], 'L2_ffn_h2_s': _L2_ffn_in['h2_s'], 'L2_ffn_w3_w': _L2_ffn_in['w3_w'], 'L2_ffn_w3_s': _L2_ffn_in['w3_s'], 'L2_c': _L2_c, 'L2_wmod': _L2_wmod, 'L3_attn_W_query': _L3_attn_in['W_query'], 'L3_attn_W_key': _L3_attn_in['W_key'], 'L3_attn_W_val': _L3_attn_in['W_val'], 'L3_attn_W_out': _L3_attn_in['W_out'], 'L3_ffn_Wqkv': _L3_ffn_in['Wqkv'], 'L3_ffn_q_scale': _L3_ffn_in['q_scale'], 'L3_ffn_k_scale': _L3_ffn_in['k_scale'], 'L3_ffn_Wo': _L3_ffn_in['Wo'], 'L3_ffn_ln_g': _L3_ffn_in['ln_g'], 'L3_ffn_ln_b': _L3_ffn_in['ln_b'], 'L3_ffn_W1': _L3_ffn_in['W1'], 'L3_ffn_b1': _L3_ffn_in['b1'], 'L3_ffn_W2': _L3_ffn_in['W2'], 'L3_ffn_b2': _L3_ffn_in['b2'], 'L3_c': _L3_c, 'L3_wmod': _L3_wmod}
    _x0 = _d['L0_attn_x']
    _d['L0_attn_x'] = jax.random.normal(jax.random.fold_in(jax.random.key(seed), 1), (2, 1024, 128), dtype=_x0.dtype)
    del _x0
    return _d

def reference(L0_attn_x, L0_attn_Wq, L0_attn_Wk, L0_attn_Wv, L0_attn_Wo, L0_attn_delta, L0_attn_G1, L0_attn_G2, L0_attn_norm_w, L0_ffn_w1_w, L0_ffn_w1_s, L0_ffn_w2_w, L0_ffn_w2_s, L0_ffn_h1_w, L0_ffn_h1_s, L0_ffn_h2_w, L0_ffn_h2_s, L0_ffn_w3_w, L0_ffn_w3_s, L0_c, L0_wmod, L1_attn_Wq, L1_attn_Wk, L1_attn_Wv, L1_attn_Wg, L1_attn_gk_w1, L1_attn_gk_w2, L1_attn_gk_b2, L1_attn_g_norm_w, L1_attn_Wo, L1_ffn_W1, L1_ffn_b1, L1_ffn_A1, L1_ffn_B1, L1_ffn_R1, L1_ffn_W2, L1_ffn_b2, L1_ffn_A2, L1_ffn_B2, L1_ffn_R2, L1_c, L1_wmod, L2_attn_W_in, L2_attn_conv_w, L2_attn_conv_b, L2_attn_A_log, L2_attn_D, L2_attn_W_out, L2_ffn_w1_w, L2_ffn_w1_s, L2_ffn_w2_w, L2_ffn_w2_s, L2_ffn_h1_w, L2_ffn_h1_s, L2_ffn_h2_w, L2_ffn_h2_s, L2_ffn_w3_w, L2_ffn_w3_s, L2_c, L2_wmod, L3_attn_W_query, L3_attn_W_key, L3_attn_W_val, L3_attn_W_out, L3_ffn_Wqkv, L3_ffn_q_scale, L3_ffn_k_scale, L3_ffn_Wo, L3_ffn_ln_g, L3_ffn_ln_b, L3_ffn_W1, L3_ffn_b1, L3_ffn_W2, L3_ffn_b2, L3_c, L3_wmod):

    def _L0_attn_ref(x, Wq, Wk, Wv, Wo, delta, G1, G2, norm_w):
        import jax, jax.numpy as jnp
        import numpy as np
        E = 128
        D = 64
        H = E // D
        EPS = 1e-05
        B, T, _ = x.shape
        q = jax.nn.silu(x @ Wq)
        v = x @ Wv
        log_f = jax.nn.log_sigmoid(x @ Wk + delta)
        k = -jnp.expm1(log_f)

        def to_tbhd(a):
            return a.reshape(B, T, H, D).transpose(1, 0, 2, 3)
        qh, kh, vh, gh = map(to_tbhd, (q, k, v, log_f))
        S0 = jnp.zeros((B, H, D, D), x.dtype)

        def step(S, inp):
            q_t, k_t, v_t, g_t = inp
            S = S * jnp.exp(g_t)[..., None] + k_t[..., None] * v_t[..., None, :]
            o_t = jnp.einsum('bhk,bhkv->bhv', q_t, S)
            return (S, o_t)
        _, o = jax.lax.scan(step, S0, (qh, kh, vh, gh))
        o = o.transpose(1, 0, 2, 3).reshape(B, T, E)
        gate = x @ G1 @ G2
        o = o * jax.nn.sigmoid(gate)
        og = o.reshape(B, T, H, D)
        og = og * jax.lax.rsqrt(jnp.mean(og * og, axis=-1, keepdims=True) + EPS)
        o = og.reshape(B, T, E) * norm_w
        return o @ Wo

    def _L0_ffn_ref(x, w1_w, w1_s, w2_w, w2_s, h1_w, h1_s, h2_w, h2_s, w3_w, w3_s):
        import jax, jax.numpy as jnp
        import numpy as np
        D_IN, D_HID = (128, 512)

        def _ternary(key, shape):
            return jax.random.randint(key, shape, -1, 2).astype(jnp.float32)

        def _tlin(x, w, s):
            return jnp.einsum('bsi,oi->bso', x, w) * s
        h = jax.nn.silu(_tlin(x, w1_w, w1_s)) * _tlin(x, w2_w, w2_s)
        h = jax.nn.gelu(_tlin(h, h1_w, h1_s), approximate=False)
        h = jax.nn.gelu(_tlin(h, h2_w, h2_s), approximate=False)
        return _tlin(h, w3_w, w3_s)

    def _L1_attn_ref(x, Wq, Wk, Wv, Wg, gk_w1, gk_w2, gk_b2, g_norm_w, Wo):
        import jax, jax.numpy as jnp
        import numpy as np
        D_MODEL = 128
        N_HEADS = 4
        KEY_DIM = 128
        VALUE_DIM = 256
        DK = KEY_DIM // N_HEADS
        DV = VALUE_DIM // N_HEADS
        LOW_RANK = 16
        GATE_NORM = 16.0
        EPS = 1e-05

        def _gla_scan(q, k, v, gk):
            B, H, L, dk = q.shape
            dv = v.shape[-1]
            qs = jnp.moveaxis(q, 2, 0)
            ks_ = jnp.moveaxis(k, 2, 0)
            vs = jnp.moveaxis(v, 2, 0)
            gs = jnp.moveaxis(gk, 2, 0)

            def step(S, inp):
                q_t, k_t, v_t, g_t = inp
                S = S * jnp.exp(g_t)[..., None] + k_t[..., None] * v_t[..., None, :]
                o_t = jnp.einsum('bhk,bhkv->bhv', q_t, S)
                return (S, o_t)
            S0 = jnp.zeros((B, H, dk, dv), q.dtype)
            _, os = jax.lax.scan(step, S0, (qs, ks_, vs, gs))
            return jnp.moveaxis(os, 0, 2)
        B, L, _ = x.shape
        scale = DK ** (-0.5)

        def heads(t, d):
            return t.reshape(B, L, N_HEADS, d).transpose(0, 2, 1, 3)
        q = heads(x @ Wq, DK) * scale
        k = heads(x @ Wk, DK)
        v = heads(x @ Wv, DV)
        gk = heads(jax.nn.log_sigmoid(x @ gk_w1 @ gk_w2 + gk_b2) / GATE_NORM, DK)
        o = _gla_scan(q, k, v, gk)
        o = o.transpose(0, 2, 1, 3)
        g = (x @ Wg).reshape(B, L, N_HEADS, DV)
        rms = o * jax.lax.rsqrt(jnp.mean(o * o, axis=-1, keepdims=True) + EPS)
        o = rms * g_norm_w * (g * jax.nn.sigmoid(g))
        o = o.reshape(B, L, VALUE_DIM)
        return o @ Wo

    def _L1_ffn_ref(x, W1, b1, A1, B1, R1, W2, b2, A2, B2, R2):
        import jax, jax.numpy as jnp
        import numpy as np
        B, S, D, H = (8, 128, 128, 512)
        E, R = (3, 8)
        SCALING = 1.0 / R

        def _mole(x, W, b, A, Bm, Rw):
            gates = jax.nn.softmax(jnp.einsum('bsd,de->bse', x, Rw), axis=-1)
            base = jnp.einsum('bsd,dh->bsh', x, W) + b
            z = jnp.einsum('bsd,edr->ebsr', x, A)
            zg = z * jnp.transpose(gates, (2, 0, 1))[..., None]
            lora = jnp.einsum('ebsr,erh->bsh', zg, Bm)
            return base + SCALING * lora
        h = _mole(x, W1, b1, A1, B1, R1)
        h = jax.nn.relu(h)
        return _mole(h, W2, b2, A2, B2, R2)

    def _L2_attn_ref(x, W_in, conv_w, conv_b, A_log, D, W_out):
        import jax, jax.numpy as jnp
        from jax import lax
        import numpy as np
        INPUT_DIM, STATE_DIM, CONV_K, EXPAND = (128, 16, 4, 2)
        INNER = INPUT_DIM * EXPAND
        BATCH, SEQ = (2, 256)
        b, s, _ = x.shape
        inner = W_in.shape[0] // 2
        K = conv_w.shape[-1]
        state = A_log.shape[1]
        xr = x @ W_in.T
        x_ssm, res = (xr[..., :inner], xr[..., inner:])
        xc = jnp.transpose(x_ssm, (0, 2, 1))
        xc = jnp.pad(xc, ((0, 0), (0, 0), (K - 1, 0)))
        xc = lax.conv_general_dilated(xc, conv_w, (1,), 'VALID', feature_group_count=inner, dimension_numbers=('NCH', 'OIH', 'NCH'))
        x_conv = jax.nn.silu(jnp.transpose(xc, (0, 2, 1)) + conv_b)
        delta = jax.nn.softplus(x_conv)
        A = -jnp.exp(A_log)
        A_d = jnp.exp(delta[..., None] * A)
        Bx = x_conv * x_conv

        def step(h, inp):
            a_t, bx_t, c_t = inp
            h = a_t * h + bx_t[..., None]
            y = c_t * jnp.sum(h, axis=-1)
            return (h, y)
        h0 = jnp.zeros((b, inner, state), x.dtype)
        _, ys = lax.scan(step, h0, (jnp.moveaxis(A_d, 1, 0), jnp.moveaxis(Bx, 1, 0), jnp.moveaxis(x_conv, 1, 0)))
        y_ssm = jnp.moveaxis(ys, 0, 1)
        y = y_ssm * jax.nn.silu(res) + D * x_conv
        return y @ W_out.T

    def _L2_ffn_ref(x, w1_w, w1_s, w2_w, w2_s, h1_w, h1_s, h2_w, h2_s, w3_w, w3_s):
        import jax, jax.numpy as jnp
        import numpy as np
        D_IN, D_HID = (128, 512)

        def _ternary(key, shape):
            return jax.random.randint(key, shape, -1, 2).astype(jnp.float32)

        def _tlin(x, w, s):
            return jnp.einsum('bsi,oi->bso', x, w) * s
        h = jax.nn.silu(_tlin(x, w1_w, w1_s)) * _tlin(x, w2_w, w2_s)
        h = jax.nn.gelu(_tlin(h, h1_w, h1_s), approximate=False)
        h = jax.nn.gelu(_tlin(h, h2_w, h2_s), approximate=False)
        return _tlin(h, w3_w, w3_s)

    def _L3_attn_ref(q, W_query, W_key, W_val, W_out):
        import jax, jax.numpy as jnp
        import numpy as np
        N_HEADS = 16
        INPUT_DIM = 128
        EMBED_DIM = 128
        KEY_DIM = EMBED_DIM // N_HEADS
        BATCH = 4
        SEQ = 256

        def _uniform(key, shape, bound):
            return jax.random.uniform(key, shape, jnp.float32, -bound, bound)
        norm = 1.0 / np.sqrt(KEY_DIM)
        Q = jnp.einsum('bsd,hdk->hbsk', q, W_query)
        K = jnp.einsum('bsd,hdk->hbsk', q, W_key)
        V = jnp.einsum('bsd,hdv->hbsv', q, W_val)
        scores = norm * jnp.einsum('hbqk,hbnk->hbqn', Q, K)
        attn = jax.nn.softmax(scores, axis=-1)
        heads = jnp.einsum('hbqn,hbnv->hbqv', attn, V)
        out = jnp.einsum('hbqv,hve->bqe', heads, W_out)
        return out

    def _L3_ffn_ref(x, Wqkv, q_scale, k_scale, Wo, ln_g, ln_b, W1, b1, W2, b2):
        import jax, jax.numpy as jnp
        import numpy as np
        DIM = 128
        DEPTH = 6
        HEADS = 16
        DIM_HEAD = 64
        WINDOW = 32
        INNER = HEADS * DIM_HEAD
        DIM_INNER = int(DIM * 4 * 2 / 3)
        QK_SCALE = 8.0

        def shift_tokens(t):
            a, s = jnp.split(t, 2, -1)
            s = jnp.pad(s, ((0, 0), (1, 0), (0, 0)))[:, :-1]
            return jnp.concatenate([a, s], -1)

        def l2norm(t):
            return t / jnp.maximum(jnp.linalg.norm(t, axis=-1, keepdims=True), 1e-12)

        def rotate_half(x):
            x1, x2 = jnp.split(x, 2, -1)
            return jnp.concatenate([-x2, x1], -1)

        def rotary_tables(n):
            half = jnp.arange(0, DIM_HEAD, 2, dtype=jnp.float32)
            inv_freq = 1.0 / 10000.0 ** (half / DIM_HEAD)
            t = jnp.arange(n, dtype=jnp.float32)
            freqs = t[:, None] * inv_freq[None, :]
            freqs = jnp.concatenate([freqs, freqs], -1)
            base_scale = (half + 0.4 * DIM_HEAD) / (1.4 * DIM_HEAD)
            power = (t - n // 2) / (WINDOW // 2)
            scale = base_scale[None, :] ** power[:, None]
            scale = jnp.concatenate([scale, scale], -1)
            return (freqs, scale)

        def local_attention(q, k, v):
            b, h, n, d = q.shape
            w = WINDOW
            nw = n // w
            bq = q.reshape(b, h, nw, w, d)
            bk = k.reshape(b, h, nw, w, d)
            bv = v.reshape(b, h, nw, w, d)

            def look(t):
                p = jnp.pad(t, ((0, 0), (0, 0), (1, 0), (0, 0), (0, 0)))
                return jnp.concatenate([p[:, :, :nw], p[:, :, 1:]], axis=3)
            bk2, bv2 = (look(bk), look(bv))
            seq = jnp.arange(n).reshape(nw, w)
            seq_p = jnp.pad(seq, ((1, 0), (0, 0)), constant_values=-1)
            jt = jnp.concatenate([seq_p[:nw], seq_p[1:]], axis=1)
            it = seq[:, :, None]
            jb = jt[:, None, :]
            mask = (it < jb) | (it > jb + w) | (jb == -1)
            sim = jnp.einsum('bhwie,bhwje->bhwij', bq, bk2) * QK_SCALE
            sim = jnp.where(mask, -jnp.finfo(sim.dtype).max, sim)
            attn = jax.nn.softmax(sim, -1)
            out = jnp.einsum('bhwij,bhwje->bhwie', attn, bv2)
            return out.reshape(b, h, n, d)

        def attn_layer(x, Wqkv, qs, ksc, Wo):
            b, n, _ = x.shape
            qkv = x @ Wqkv
            q, k, v = jnp.split(qkv, 3, -1)
            sh = lambda t: t.reshape(b, n, HEADS, DIM_HEAD).transpose(0, 2, 1, 3)
            q, k, v = (sh(q), sh(k), sh(v))
            q = l2norm(q) * qs
            k = l2norm(k) * ksc
            freqs, scale = rotary_tables(n)
            cos, sin = (jnp.cos(freqs), jnp.sin(freqs))
            q = q * cos * scale + rotate_half(q) * sin * scale
            inv = 1.0 / scale
            k = k * cos * inv + rotate_half(k) * sin * inv
            out = local_attention(q, k, v)
            out = out.transpose(0, 2, 1, 3).reshape(b, n, INNER)
            return out @ Wo

        def ffn_layer(x, g, bln, W1, b1, W2, b2):
            mu = x.mean(-1, keepdims=True)
            var = ((x - mu) ** 2).mean(-1, keepdims=True)
            xn = (x - mu) / jnp.sqrt(var + 1e-05) * g + bln
            hg = xn @ W1 + b1
            a, gate = jnp.split(hg, 2, -1)
            return a * jax.nn.gelu(gate, approximate=False) @ W2 + b2
        for i in range(DEPTH):
            x = attn_layer(shift_tokens(x), Wqkv[i], q_scale[i], k_scale[i], Wo[i]) + x
            x = ffn_layer(shift_tokens(x), ln_g[i], ln_b[i], W1[i], b1[i], W2[i], b2[i]) + x
        return x
    x = L0_attn_x
    mod = (_silu(L0_c) @ L0_wmod).reshape(L0_c.shape[0], 6, 1, -1)
    sa, ca, ga, sb, cb, gb = (mod[:, 0], mod[:, 1], mod[:, 2], mod[:, 3], mod[:, 4], mod[:, 5])
    ga = (2 * (ga >= 0) - 1) * jnp.maximum(jnp.abs(ga), 0.25)
    gb = (2 * (gb >= 0) - 1) * jnp.maximum(jnp.abs(gb), 0.25)
    h = _layernorm(x, axis=-1) * (1 + ca) + sa
    x = x + ga * _L0_attn_ref(h, L0_attn_Wq, L0_attn_Wk, L0_attn_Wv, L0_attn_Wo, L0_attn_delta, L0_attn_G1, L0_attn_G2, L0_attn_norm_w)
    h = _layernorm(x, axis=-1) * (1 + cb) + sb
    x = x + gb * _L0_ffn_ref(h, L0_ffn_w1_w, L0_ffn_w1_s, L0_ffn_w2_w, L0_ffn_w2_s, L0_ffn_h1_w, L0_ffn_h1_s, L0_ffn_h2_w, L0_ffn_h2_s, L0_ffn_w3_w, L0_ffn_w3_s)
    mod = (_silu(L1_c) @ L1_wmod).reshape(L1_c.shape[0], 6, 1, -1)
    sa, ca, ga, sb, cb, gb = (mod[:, 0], mod[:, 1], mod[:, 2], mod[:, 3], mod[:, 4], mod[:, 5])
    ga = (2 * (ga >= 0) - 1) * jnp.maximum(jnp.abs(ga), 0.25)
    gb = (2 * (gb >= 0) - 1) * jnp.maximum(jnp.abs(gb), 0.25)
    h = _layernorm(x, axis=-1) * (1 + ca) + sa
    x = x + ga * _L1_attn_ref(h, L1_attn_Wq, L1_attn_Wk, L1_attn_Wv, L1_attn_Wg, L1_attn_gk_w1, L1_attn_gk_w2, L1_attn_gk_b2, L1_attn_g_norm_w, L1_attn_Wo)
    h = _layernorm(x, axis=-1) * (1 + cb) + sb
    x = x + gb * _L1_ffn_ref(h, L1_ffn_W1, L1_ffn_b1, L1_ffn_A1, L1_ffn_B1, L1_ffn_R1, L1_ffn_W2, L1_ffn_b2, L1_ffn_A2, L1_ffn_B2, L1_ffn_R2)
    mod = (_silu(L2_c) @ L2_wmod).reshape(L2_c.shape[0], 6, 1, -1)
    sa, ca, ga, sb, cb, gb = (mod[:, 0], mod[:, 1], mod[:, 2], mod[:, 3], mod[:, 4], mod[:, 5])
    ga = (2 * (ga >= 0) - 1) * jnp.maximum(jnp.abs(ga), 0.25)
    gb = (2 * (gb >= 0) - 1) * jnp.maximum(jnp.abs(gb), 0.25)
    h = _layernorm(x, axis=-1) * (1 + ca) + sa
    x = x + ga * _L2_attn_ref(h, L2_attn_W_in, L2_attn_conv_w, L2_attn_conv_b, L2_attn_A_log, L2_attn_D, L2_attn_W_out)
    h = _layernorm(x, axis=-1) * (1 + cb) + sb
    x = x + gb * _L2_ffn_ref(h, L2_ffn_w1_w, L2_ffn_w1_s, L2_ffn_w2_w, L2_ffn_w2_s, L2_ffn_h1_w, L2_ffn_h1_s, L2_ffn_h2_w, L2_ffn_h2_s, L2_ffn_w3_w, L2_ffn_w3_s)
    mod = (_silu(L3_c) @ L3_wmod).reshape(L3_c.shape[0], 6, 1, -1)
    sa, ca, ga, sb, cb, gb = (mod[:, 0], mod[:, 1], mod[:, 2], mod[:, 3], mod[:, 4], mod[:, 5])
    ga = (2 * (ga >= 0) - 1) * jnp.maximum(jnp.abs(ga), 0.25)
    gb = (2 * (gb >= 0) - 1) * jnp.maximum(jnp.abs(gb), 0.25)
    h = _layernorm(x, axis=-1) * (1 + ca) + sa
    x = x + ga * _L3_attn_ref(h, L3_attn_W_query, L3_attn_W_key, L3_attn_W_val, L3_attn_W_out)
    h = _layernorm(x, axis=-1) * (1 + cb) + sb
    x = x + gb * _L3_ffn_ref(h, L3_ffn_Wqkv, L3_ffn_q_scale, L3_ffn_k_scale, L3_ffn_Wo, L3_ffn_ln_g, L3_ffn_ln_b, L3_ffn_W1, L3_ffn_b1, L3_ffn_W2, L3_ffn_b2)
    return x

_drawn_inputs = setup_inputs


def setup_inputs(seed=0):
    import zlib

    import numpy as np

    out = dict(_drawn_inputs(seed))
    spreads = {'L0_attn_delta': (4.595119953155518, 0.2),
     'L0_attn_norm_w': (1.0, 0.2),
     'L1_attn_gk_b2': (0.0, 0.1),
     'L1_attn_g_norm_w': (1.0, 0.2),
     'L1_ffn_b1': (0.0, 0.1),
     'L1_ffn_b2': (0.0, 0.1),
     'L2_attn_conv_b': (0.0, 0.1),
     'L2_attn_D': (1.0, 0.2),
     'L3_ffn_q_scale': (1.0, 0.2),
     'L3_ffn_k_scale': (1.0, 0.2),
     'L3_ffn_ln_g': (1.0, 0.2),
     'L3_ffn_ln_b': (0.0, 0.1),
     'L3_ffn_b1': (0.0, 0.1),
     'L3_ffn_b2': (0.0, 0.1)}
    factors = {}
    for name, (base, spread) in spreads.items():
        noise = np.random.default_rng([zlib.crc32(name.encode()), seed]).standard_normal(out[name].shape)
        drawn = base * np.exp(spread * noise) if base else spread * noise
        out[name] = jnp.asarray(drawn.astype(out[name].dtype))
    for name, factor in factors.items():
        out[name] = (out[name] * factor).astype(out[name].dtype)
    return out
```

```python
from contextlib import ExitStack

import numpy as np
import concourse.bass as bass
from concourse import mybir

F32 = mybir.dt.float32
BF16 = mybir.dt.bfloat16
I32 = mybir.dt.int32
ALU = mybir.AluOpType
ACT = mybir.ActivationFunctionType
AX = mybir.AxisListType.X

P = 128
BATCH = 2
SEQ = 1024
TOK = BATCH * SEQ
TILES = TOK // P
BT = SEQ // P
BLK = 512
NBLK = TOK // BLK
HID = 512
HB = HID // P
LEVELS = 7
DEPTH = 6
EPS = 1e-5
ARENA = 32700
LAYERS = 4
DEEP_AT = 10852
ENGINES = 4

ATTN, FFN = 0, 1


PACKS = {
    "const": [("ident", P), ("band", 96), ("band0", 96), ("cT", 2 * LAYERS), ("sel", 9)],
    "mod": [("wmod", LAYERS * 6 * P)],
    "l0": [("wq", P), ("wk", P), ("wv", P), ("g1", 64), ("g2", P), ("wo", P), ("delta", 1), ("nw", 1)],
    "tern": [("w1", HID), ("w2", HID), ("h1", HB * HID), ("h2", HB * HID), ("w3", HB * P),
             ("s1", HB), ("s2", HB), ("sh1", HB), ("sh2", HB), ("s3", P)],
    "l1": [("wq", P), ("wk", P), ("wv", 256), ("wg", 256), ("gk1", 16), ("gk2", P), ("b2", 1), ("nw", 1),
           ("wo", 2 * P)],
    "mole": [("w1", HID), ("ar1", 27), ("b1", HID), ("w2", HB * P), ("ar2", HB * 27), ("b2", P)],
    "l2": [("win", 512), ("cw", 8), ("cb", 2), ("alog", 32), ("d", 2), ("wout", 2 * P)],
    "l3": [("wq", P), ("wk", P), ("wv", P), ("wo", P)],
    "deep": [("wqkv", 3072), ("wo", 8 * P), ("w1", 682), ("w2", 3 * P), ("b1", 6), ("b2", 1),
             ("qs", 64), ("ks", 64), ("lng", 1), ("lnb", 1)],
}


def columns(pack):
    return sum(n for _, n in PACKS[pack])


def view(tensor, pack, name, rows=P):
    at = 0
    for item, n in PACKS[pack]:
        if item == name:
            return tensor[0:rows, at:at + n]
        at += n
    raise KeyError(name)


class Memory:
    pass


class Carver:

    def __init__(self, arena, at=0):
        self.arena, self.at = arena, at

    def take(self, n):
        got = self.arena[:, self.at:self.at + n]
        self.at += n
        assert self.at <= ARENA, self.at
        return got

    def bf16(self, n):
        return self.take(n // 2).bitcast(BF16)


def spread(ap, n):
    return ap.rearrange("p (a o) -> p a o", o=1).broadcast_to([ap.shape[0], ap.shape[1], n])


def repeat(ap, n):
    return ap.rearrange("p (o a) -> p o a", o=1).broadcast_to([ap.shape[0], n, ap.shape[1]])


def finish_stage(eng, m, stage):
    eng.drain().then_inc(m.stage_done, 1)
    eng.wait_ge(m.stage_done, ENGINES * (stage + 1))


COLS = (0, 1, 3, 4)
GATES = (2, 5)


def mod_scalar(nc, act, m, s):
    act.wait_ge(m.loaded["const"], 16)
    nc.scalar.activation(m.sc[:, :], m.cT, ACT.Silu).then_inc(s["silu"], 1)


def mod_tensor(nc, pe, m, s):
    pe.wait_ge(s["silu"], 1)
    pe.wait_ge(m.loaded["mod"], 16)
    for l in range(LAYERS):
        for j, part in enumerate(COLS):
            at = (l * 4 + j) * 2
            last = nc.tensor.matmul(m.ps[:, 0, at:at + 2], m.wmod[:, l, part, :], m.sc[:, 2 * l:2 * l + 2],
                                    start=True, stop=True)
    last.then_inc(s["cols"], 1)
    pe.wait_ge(s["wide"], 1)
    for l in range(LAYERS):
        for g, part in enumerate(GATES):
            for b in range(BATCH):
                last = nc.tensor.matmul(m.ps[:, 1 + l, (g * 2 + b) * P:(g * 2 + b + 1) * P],
                                        m.scwide[:, 2 * l + b, :], m.wmod[:, l, part, :], start=True, stop=True)
        last.then_inc(s["rows"], 1)


def mod_vector(nc, dve, m, s):
    dve.wait_ge(s["silu"], 1)
    nc.vector.tensor_copy(m.scwide[:, :, :], spread(m.sc[:, :], P)).then_inc(s["wide"], 1)
    dve.wait_ge(s["cols"], 1)
    nc.vector.tensor_copy(m.modc[:, :], m.ps[:, 0, 0:LAYERS * 8])
    dve.drain()
    scales = m.modc[:, :].rearrange("p (a k b) -> p a k b", k=2, b=2)[:, :, 1, :]
    nc.vector.tensor_scalar(scales, scales, 1.0, None, ALU.add)
    for l in range(LAYERS):
        dve.wait_ge(s["rows"], l + 1)
        g = m.ps[:, 1 + l, :]
        nc.vector.tensor_scalar(m.gtmp[:, l, :], g, 0.0, 2.0, ALU.is_ge, ALU.mult)
        nc.vector.tensor_scalar(m.grow[:, l, :], g, -1.0, 0.25, ALU.mult, ALU.max)
        dve.drain()
        nc.vector.tensor_tensor(m.grow[:, l, :], g, m.grow[:, l, :], ALU.max)
        dve.drain()
        nc.vector.scalar_tensor_tensor(m.grow[:, l, :], m.gtmp[:, l, :], -1.0, m.grow[:, l, :], ALU.add, ALU.mult)


def mod_col(m, l, sub, which, b):
    at = (l * 4 + 2 * sub + which) * 2 + b
    return m.modc[:, at:at + 1]


def gate_row(m, l, sub, b):
    at = (sub * 2 + b) * P
    return m.grow[:, l, at:at + P]


def ln_vector(nc, dve, m, s, k):
    for t in range(TILES):
        nc.vector.bn_stats(m.stats[:, t, :], m.x[:, t, :])
    dve.drain()
    for t in range(TILES):
        last = nc.vector.bn_aggr(m.mv[:, t, :], m.stats[:, t, :])
    last.then_inc(s["stats"], 1)
    dve.wait_ge(s["rstd"], k + 1)
    for t in range(TILES):
        nc.vector.tensor_scalar(m.xn[:, t, :], m.x[:, t, :], m.mv[:, t, 0:1], m.rstd[:, t:t + 1],
                                ALU.subtract, ALU.mult).then_inc(s["xn"], 1)


def ln_gpsimd(nc, pool, m, s, k):
    pool.wait_ge(s["stats"], k + 1)
    nc.gpsimd.tensor_scalar(m.rstd[:, :], m.mv[:, :, 1], EPS, None, ALU.add)
    pool.drain()
    nc.gpsimd.tensor_tensor(m.rstd[:, :], m.rstd[:, :], m.nhalf[:, 0:TILES], ALU.pow).then_inc(s["rstd"], 1)


def ln_tensor(nc, pe, m, s, k):
    for g in range(NBLK):
        pe.wait_ge(s["xn"], TILES * k + 4 * (g + 1))
        for t in range(4):
            last = nc.tensor.transpose(m.ps[:, g, t * P:(t + 1) * P], m.xn[:, 4 * g + t, :], m.ident)
        last.then_inc(s["turned"], 1)


def ln_scalar(nc, act, m, s, k, l, sub):
    for g in range(NBLK):
        b = g // (NBLK // BATCH)
        act.wait_ge(s["turned"], NBLK * k + g + 1)
        nc.scalar.activation(m.hT[:, g * BLK:(g + 1) * BLK], m.ps[:, g, :], ACT.Identity,
                             bias=mod_col(m, l, sub, 0, b), scale=mod_col(m, l, sub, 1, b))


MOD_SEMS = ("silu", "cols", "wide", "rows")
LN_SEMS = ("stats", "rstd", "xn", "turned")


def add_gated(nc, dve, m, ps, t0, n, row, tmp):
    nc.vector.tensor_tensor(tmp, ps, row, ALU.mult)
    dve.drain()
    return nc.vector.tensor_tensor(m.x[:, t0:t0 + n, :], m.x[:, t0:t0 + n, :], tmp, ALU.add)


def gla_jobs(g):
    jobs = [("q", n) for n in range(NBLK)] + [("k", n) for n in range(NBLK)] + [("low", n) for n in range(NBLK)]
    if g.layer == 1:
        jobs += [("z", n) for n in range(NBLK)]
    per = BLK // g.vd
    jobs += [("v", n) for n in range(TILES // per)] + [("gate", n) for n in range(TILES // per)]
    return jobs


def gla_tensor(nc, pe, m, s, g):
    T = nc.tensor
    per = BLK // g.vd
    jobs = gla_jobs(g)
    pe.wait_ge(m.loaded[g.pack], 16)
    for n, (kind, i) in enumerate(jobs):
        if n >= 8:
            pe.wait_ge(s["proj_read"], n - 7)
        bank = m.ps[:, n % 8, :]
        cols = slice(i * BLK, (i + 1) * BLK)
        if kind in ("q", "k"):
            last = T.matmul(bank, g.w[kind], m.hT[:, cols], start=True, stop=True)
        elif kind == "low":
            last = T.matmul(m.ps[0:g.low, n % 8, :], g.w["low"], m.hT[:, cols], start=True, stop=True)
        elif kind == "z":
            pe.wait_ge(s["proj_read"], jobs.index(("low", i)) + 1)
            last = T.matmul(bank, g.w["z"], g.lowT[:, cols], start=True, stop=True)
        else:
            if kind == "gate" and g.layer == 0:
                pe.wait_ge(s["proj_read"], jobs.index(("low", NBLK - 1)) + 1)
            for j in range(per):
                t = i * per + j
                src = g.lowT if (kind == "gate" and g.layer == 0) else m.hT
                last = T.matmul(m.ps[:, n % 8, j * g.vd:(j + 1) * g.vd], src[:, t * P:(t + 1) * P], g.w[kind],
                                start=True, stop=True)
        last.then_inc(s["proj"], 1)

    pairs = g.heads // 2
    per_chunk = (LEVELS + 1) * pairs
    pe.wait_ge(s["proj_read"], len(jobs))
    for n in range(TILES):
        b, c = divmod(n, BT)
        cols = slice(c * P, (c + 1) * P)
        pe.wait_ge(s["scaled"], (b + 1))
        carry = c < BT - 1
        if carry:
            u = b * (BT - 1) + c
            pe.wait_ge(s["state"], u)
            T.transpose(m.ps[:, 7, 0:P], g.ks[:, cols], m.ident).then_inc(s["kturned"], 1)
        for j in range(per_chunk):
            lev, pair = divmod(j, pairs)
            job = n * per_chunk + j
            if job >= 3:
                pe.wait_ge(s["picked"], job - 2)
            if lev < LEVELS:
                pe.wait_ge(s["level"], b * LEVELS + lev + 1)
            for e in range(2):
                h = 2 * pair + e
                rows = slice(h * g.dk, (h + 1) * g.dk)
                if lev < LEVELS:
                    left = right = g.lev[rows, lev, cols]
                else:
                    left, right = g.kT[rows, n * P:(n + 1) * P], g.qT[rows, n * P:(n + 1) * P]
                last = T.matmul(m.ps[:, 2 * (job % 3) + e, 0:P], left, right, start=True, stop=True)
            last.then_inc(s["scored"], 1)
            if carry and j == per_chunk // 2:
                pe.wait_ge(s["kcopied"], u + 1)
                T.matmul(m.ps[:, 7, 256:256 + g.vd], g.ksT[:, :], g.v[:, n, :], start=True,
                         stop=True).then_inc(s["update"], 1)
        pe.wait_ge(s["picked"], (n + 1) * per_chunk)
        if n >= 1:
            pe.wait_ge(s["o_read"], n)
        if c > 0:
            pe.wait_ge(s["state"], b * (BT - 1) + c)
            T.matmul(m.ps[:, 6, 0:g.vd], g.qs[:, cols], g.state[:, n % 2, :], start=True, stop=False,
                     skip_group_check=True)
        for h in range(g.heads):
            out = m.ps[:, 6, h * g.dv:(h + 1) * g.dv]
            last = T.matmul(out, g.at[:, n % 2, h, :], g.v[:, n, h * g.dv:(h + 1) * g.dv], start=c == 0, stop=True,
                            skip_group_check=True)
        last.then_inc(s["o_made"], 1)

    blocks = g.vd // P
    n_turn = blocks * NBLK
    pe.wait_ge(s["o_read"], TILES)
    pe.wait_ge(s["o_norm"], 1)
    for n in range(n_turn):
        k, i = divmod(n, NBLK)
        if n >= 4:
            pe.wait_ge(s["oT"], n - 3)
        for t in range(4):
            last = T.transpose(m.ps[:, n % 4, t * P:(t + 1) * P], g.o[:, 4 * i + t, k * P:(k + 1) * P], m.ident)
        last.then_inc(s["o_turned"], 1)
    pe.wait_ge(s["oT"], n_turn)
    for i in range(NBLK):
        for t in range(4):
            for k in range(blocks):
                last = T.matmul(m.ps[:, 4 + i, t * P:(t + 1) * P], g.oT[:, k, (4 * i + t) * P:(4 * i + t + 1) * P],
                                g.wo[:, k, :], start=k == 0, stop=k == blocks - 1)
        last.then_inc(s["y"], 1)


def gla_scalar(nc, act, m, s, g):
    A = nc.scalar.activation
    per = BLK // g.vd
    for n, (kind, i) in enumerate(gla_jobs(g)):
        act.wait_ge(s["proj"], n + 1)
        bank = m.ps[:, n % 8, :]
        cols = slice(i * BLK, (i + 1) * BLK)
        if kind == "q":
            done = (A(g.qT[:, cols], bank, ACT.Silu) if g.layer == 0 else
                    A(g.qT[:, cols], bank, ACT.Copy, scale=g.qscale))
        elif kind == "k":
            done = (A(g.z[:, cols], bank, ACT.Identity, bias=g.zbias) if g.layer == 0 else
                    A(g.kT[:, cols], bank, ACT.Copy))
        elif kind == "low":
            done = A(g.lowT[:, cols], m.ps[0:g.low, n % 8, :], ACT.Copy)
        elif kind == "z":
            done = A(g.z[:, cols], bank, ACT.Identity, bias=g.zbias)
        elif kind == "v":
            done = A(g.v[:, i * per:(i + 1) * per, :], bank.rearrange("p (a b) -> p a b", a=per), ACT.Copy)
        else:
            done = A(g.gate[:, i * per:(i + 1) * per, :], bank.rearrange("p (a b) -> p a b", a=per),
                     ACT.Sigmoid if g.layer == 0 else ACT.Silu)
        done.then_inc(s["proj_read"], 1)
    act.drain()
    if g.layer == 0:
        A(g.kT[:, :], g.z[:, :], ACT.Sigmoid, scale=-1.0)
    A(g.soft[:, :], g.z[:, :], ACT.Abs)
    act.drain()
    A(g.soft[:, :], g.soft[:, :], ACT.Exp, scale=-1.0)
    act.drain()
    A(g.soft[:, :], g.soft[:, :], ACT.Ln, bias=1.0).then_inc(s["soft"], 1)
    for n in range(TILES):
        b, c = divmod(n, BT)
        if c == 0:
            act.wait_ge(s["diff"], b * (LEVELS + 2) + 2)
            A(g.es[:, :], g.es[:, :], ACT.Exp, scale=g.decay_scale).then_inc(s["exped"], 1)
            A(g.ks[:, :], g.ks[:, :], ACT.Exp, scale=g.decay_scale).then_inc(s["exped"], 1)
            for lev in range(LEVELS):
                act.wait_ge(s["diff"], b * (LEVELS + 2) + lev + 3)
                A(g.lev[:, lev, :], g.lev[:, lev, :], ACT.Exp, scale=g.decay_scale).then_inc(s["exped"], 1)
        if c < BT - 1:
            u = b * (BT - 1) + c
            act.wait_ge(s["kturned"], u + 1)
            A(g.ksT[:, :], m.ps[:, 7, 0:P], ACT.Copy).then_inc(s["kcopied"], 1)
        act.wait_ge(s["o_made"], n + 1)
        A(g.o[:, n, :], m.ps[:, 6, 0:g.vd], ACT.Copy).then_inc(s["o_read"], 1)
    for n in range(g.vd // P * NBLK):
        k, i = divmod(n, NBLK)
        act.wait_ge(s["o_turned"], n + 1)
        A(g.oT[:, k, i * BLK:(i + 1) * BLK], m.ps[:, n % 4, :], ACT.Identity,
          scale=g.nw).then_inc(s["oT"], 1)


def gla_vector(nc, dve, m, s, g):
    V = nc.vector
    V.memset(g.keep[:, :], 1.0)
    V.memset(g.at[:, :, :, :], 0.0)
    V.memset(g.state[:, :, :], 0.0)
    dve.drain()
    V.memset(g.keep[:, :].rearrange("p (a b) -> p a b", b=P)[:, :, 0:1], 0.0)
    dve.wait_ge(s["soft"], 1)
    V.scalar_tensor_tensor(g.soft[:, :], g.z[:, :], 0.0, g.soft[:, :], ALU.min, ALU.subtract)
    dve.drain()
    V.tensor_tensor_scan(g.c[:, :], g.keep[:, :], g.soft[:, :], 0.0, ALU.mult, ALU.add)
    dve.drain()
    pairs = g.heads // 2
    per_chunk = (LEVELS + 1) * pairs
    for n in range(TILES):
        b, c = divmod(n, BT)
        cols = slice(c * P, (c + 1) * P)
        if c == 0:
            half = slice(b * SEQ, (b + 1) * SEQ)
            if b > 0:
                dve.wait_ge(s["o_made"], n)
            cb = g.c[:, half]
            V.tensor_copy(g.es[:, :], cb).then_inc(s["diff"], 1)
            c3 = cb.rearrange("p (a b) -> p a b", b=P)
            V.tensor_tensor(g.ks[:, :].rearrange("p (a b) -> p a b", b=P),
                            c3[:, :, P - 1:P].broadcast_to([P, BT, P]), c3, ALU.subtract).then_inc(s["diff"], 1)
            for lev in range(LEVELS):
                w = 1 << lev
                nb = SEQ // (2 * w)
                c4 = cb.rearrange("p (a e b) -> p a e b", e=2, b=w)
                l4 = g.lev[:, lev, :].rearrange("p (a e b) -> p a e b", e=2, b=w)
                mid = c4[:, :, 0, w - 1:w].broadcast_to([P, nb, w])
                V.tensor_tensor(l4[:, :, 0, :], mid, c4[:, :, 0, :], ALU.subtract)
                V.tensor_tensor(l4[:, :, 1, :], c4[:, :, 1, :], mid, ALU.subtract).then_inc(s["diff"], 1)
            dve.wait_ge(s["exped"], b * (LEVELS + 2) + 2)
            V.tensor_tensor(g.qs[:, :], g.es[:, :], g.qT[:, half], ALU.mult)
            V.tensor_tensor(g.ks[:, :], g.ks[:, :], g.kT[:, half], ALU.mult).then_inc(s["scaled"], 1)
            for lev in range(LEVELS):
                w = 1 << lev
                dve.wait_ge(s["exped"], b * (LEVELS + 2) + lev + 3)
                l4 = g.lev[:, lev, :].rearrange("p (a e b) -> p a e b", e=2, b=w)
                k4 = g.kT[:, half].rearrange("p (a e b) -> p a e b", e=2, b=w)
                q4 = g.qT[:, half].rearrange("p (a e b) -> p a e b", e=2, b=w)
                V.tensor_tensor(l4[:, :, 0, :], l4[:, :, 0, :], k4[:, :, 0, :], ALU.mult)
                V.tensor_tensor(l4[:, :, 1, :], l4[:, :, 1, :], q4[:, :, 1, :], ALU.mult).then_inc(s["level"], 1)
        if n >= 2:
            dve.wait_ge(s["o_made"], n - 1)
        for j in range(per_chunk):
            lev, pair = divmod(j, pairs)
            job = n * per_chunk + j
            dve.wait_ge(s["scored"], job + 1)
            if pair == 0:
                dve.drain()
            slot = 2 * (job % 3)
            V.copy_predicated(g.at[:, n % 2, 2 * pair:2 * pair + 2, :], repeat(m.masks[:, lev, :], 2),
                              m.ps[:, slot:slot + 2, 0:P]).then_inc(s["picked"], 1)
        if c < BT - 1:
            u = b * (BT - 1) + c
            dve.wait_ge(s["update"], u + 1)
            for h in range(g.heads):
                rows = slice(h * g.dk, (h + 1) * g.dk)
                new = m.ps[rows, 7, 256 + h * g.dv:256 + (h + 1) * g.dv]
                to = g.state[rows, (n + 1) % 2, h * g.dv:(h + 1) * g.dv]
                if c == 0:
                    done = V.tensor_copy(to, new)
                else:
                    done = V.scalar_tensor_tensor(to, g.state[rows, n % 2, h * g.dv:(h + 1) * g.dv],
                                                  g.es[rows, c * P + P - 1:c * P + P], new, ALU.mult, ALU.add)
            done.then_inc(s["state"], 1)
            dve.drain()
    dve.wait_ge(s["o_read"], TILES)
    o2 = g.o[:, :, :].rearrange("p a b -> p (a b)")
    g2 = g.gate[:, :, :].rearrange("p a b -> p (a b)")
    if g.layer == 0:
        V.tensor_tensor(o2, o2, g2, ALU.mult)
        dve.drain()
    V.tensor_tensor(g.sq[:, :], o2, o2, ALU.mult)
    dve.drain()
    V.tensor_reduce(g.ms[:, :], g.sq[:, :].rearrange("p (a b) -> p a b", b=g.dv), AX, ALU.add).then_inc(s["ms"], 1)
    dve.wait_ge(s["rms"], 1)
    o3 = o2.rearrange("p (a b) -> p a b", b=g.dv)
    done = V.tensor_tensor(o3, o3, spread(g.ms[:, :], g.dv), ALU.mult)
    if g.layer == 1:
        dve.drain()
        done = V.tensor_tensor(o2, o2, g2, ALU.mult)
    done.then_inc(s["o_norm"], 1)
    for i in range(NBLK):
        dve.wait_ge(s["y"], i + 1)
        b = i // (NBLK // BATCH)
        add_gated(nc, dve, m, m.ps[:, 4 + i, :].rearrange("p (a b) -> p a b", a=4), 4 * i, 4,
                  repeat(gate_row(m, g.layer, ATTN, b), 4), g.tmp[:, i % 2, :].rearrange("p (a b) -> p a b", a=4))


def gla_gpsimd(nc, pool, m, s, g):
    pool.wait_ge(s["ms"], 1)
    n = TILES * g.heads
    nc.gpsimd.tensor_scalar(g.ms[:, :], g.ms[:, :], 1.0 / g.dv, EPS, ALU.mult, ALU.add)
    pool.drain()
    nc.gpsimd.tensor_tensor(g.ms[:, :], g.ms[:, :], m.nhalf[:, 0:n], ALU.pow).then_inc(s["rms"], 1)


GLA_SEMS = ("proj", "proj_read", "soft", "diff", "exped", "scaled", "level", "scored", "picked", "kturned",
            "kcopied", "update", "state", "o_made", "o_read", "ms", "rms", "o_norm", "o_turned", "oT", "y")


def gla_setup(m, layer):
    g = Memory()
    g.layer, g.pack = layer, "l0" if layer == 0 else "l1"
    w = m.packs[g.pack]
    g.heads, g.dk, g.dv = (2, 64, 64) if layer == 0 else (4, 32, 64)
    g.vd = g.heads * g.dv
    g.low = 64 if layer == 0 else 16
    g.qscale = float(g.dk) ** -0.5
    g.decay_scale = 1.0 if layer == 0 else 1.0 / 16.0
    v = lambda name, rows=P: view(w, g.pack, name, rows)
    if layer == 0:
        g.w = {"q": v("wq"), "k": v("wk"), "low": v("g1"), "v": v("wv"), "gate": v("g2", 64)}
        g.zbias = v("delta")
    else:
        g.w = {"q": v("wq"), "k": v("wk"), "low": v("gk1"), "z": v("gk2", 16), "v": v("wv"), "gate": v("wg")}
        g.zbias = v("b2")
    g.wo = v("wo").rearrange("p (a b) -> p a b", b=P)
    g.nw = v("nw")
    a = Carver(m.arena)
    g.qT, g.kT, g.c = a.take(TOK), a.take(TOK), a.take(TOK)
    g.v = a.take(TILES * g.vd).rearrange("p (a b) -> p a b", b=g.vd)
    g.gate = a.take(TILES * g.vd).rearrange("p (a b) -> p a b", b=g.vd)
    g.o = a.take(TILES * g.vd).rearrange("p (a b) -> p a b", b=g.vd)
    g.es, g.qs, g.ks = a.take(SEQ), a.take(SEQ), a.take(SEQ)
    g.at = a.take(2 * g.heads * P).rearrange("p (a h b) -> p a h b", a=2, h=g.heads)
    g.ksT = a.take(P)
    g.state = a.take(2 * g.vd).rearrange("p (a b) -> p a b", a=2)
    g.ms = a.take(TILES * g.heads)
    g.tmp = a.take(2 * BLK).rearrange("p (a b) -> p a b", a=2)
    levels = Carver(m.arena, a.at)
    g.lev = levels.take(LEVELS * SEQ).rearrange("p (a b) -> p a b", a=LEVELS)
    early = Carver(m.arena, a.at)
    g.z, g.soft, g.keep = early.take(TOK), early.take(TOK), early.take(TOK)
    g.lowT = g.o.rearrange("p a b -> p (a b)")[0:g.low, 0:TOK]
    late = Carver(m.arena, a.at)
    g.sq = g.lev.rearrange("p a b -> p (a b)")[:, 0:TILES * g.vd]
    g.oT = late.take(g.vd // P * TOK).rearrange("p (a b) -> p a b", b=TOK)
    return g


def tern_tensor(nc, pe, m, s, f):
    T = nc.tensor
    pe.wait_ge(m.loaded["tern"], f.loaded)
    n = 0
    for i in range(NBLK):
        cols = slice(i * BLK, (i + 1) * BLK)
        for j in range(HB):
            if n >= 4:
                pe.wait_ge(s["glu"], f.done["glu"] + n - 3)
            out = slice(j * P, (j + 1) * P)
            T.matmul(m.ps[:, 2 * (n % 4), :], f.w1[:, out], m.hT[:, cols], start=True, stop=True)
            T.matmul(m.ps[:, 2 * (n % 4) + 1, :], f.w2[:, out], m.hT[:, cols], start=True, stop=True).then_inc(s["up"], 1)
            n += 1
    pe.wait_ge(s["glu"], f.done["glu"] + n)
    n = 0
    for w, src in ((f.h1, f.a), (f.h2, f.b)):
        for i in range(NBLK):
            cols = slice(i * BLK, (i + 1) * BLK)
            if src is f.b:
                pe.wait_ge(s["hid_read"], f.done["hid_read"] + (i + 1) * HB)
            for j in range(HB):
                if n >= 8:
                    pe.wait_ge(s["hid_read"], f.done["hid_read"] + n - 7)
                for k in range(HB):
                    last = T.matmul(m.ps[:, n % 8, :], w[:, k, j * P:(j + 1) * P], src[:, k, cols],
                                    start=k == 0, stop=k == HB - 1)
                last.then_inc(s["hid"], 1)
                n += 1
    for i in range(NBLK):
        pe.wait_ge(s["hid_read"], f.done["hid_read"] + max(20 + 4 * i, 25 + i))
        for t in range(4):
            for k in range(HB):
                last = T.matmul(m.ps[:, i, t * P:(t + 1) * P], f.a[:, k, (4 * i + t) * P:(4 * i + t + 1) * P],
                                f.w3[:, k, :], start=k == 0, stop=k == HB - 1)
        last.then_inc(s["y"], 1)


def tern_scalar(nc, act, m, s, f):
    n = 0
    for i in range(NBLK):
        for j in range(HB):
            act.wait_ge(s["up"], f.done["up"] + n + 1)
            if n >= 2:
                act.wait_ge(s["glu"], f.done["glu"] + n - 1)
            nc.scalar.activation(f.u[:, n % 2, :], m.ps[:, 2 * (n % 4), :], ACT.Silu,
                                 scale=f.s1[:, j:j + 1]).then_inc(s["silu"], 1)
            n += 1
    n = 0
    for dst, sc in ((f.b, f.sh1), (f.a, f.sh2)):
        for i in range(NBLK):
            for j in range(HB):
                act.wait_ge(s["hid"], f.done["hid"] + n + 1)
                if dst is f.a and j == 0:
                    act.wait_ge(s["hid"], f.done["hid"] + 16)
                nc.scalar.activation(dst[:, j, i * BLK:(i + 1) * BLK], m.ps[:, n % 8, :], ACT.Gelu,
                                     scale=sc[:, j:j + 1]).then_inc(s["hid_read"], 1)
                n += 1


def tern_vector(nc, dve, m, s, f):
    n = 0
    for i in range(NBLK):
        for j in range(HB):
            dve.wait_ge(s["silu"], f.done["silu"] + n + 1)
            nc.vector.scalar_tensor_tensor(f.a[:, j, i * BLK:(i + 1) * BLK], m.ps[:, 2 * (n % 4) + 1, :],
                                           f.s2[:, j:j + 1], f.u[:, n % 2, :], ALU.mult, ALU.mult).then_inc(s["glu"], 1)
            n += 1
    for b in range(BATCH):
        nc.vector.tensor_tensor(f.row[:, b, :], f.s3, gate_row(m, f.layer, FFN, b), ALU.mult)
    dve.drain()
    for i in range(NBLK):
        dve.wait_ge(s["y"], f.done["y"] + i + 1)
        add_gated(nc, dve, m, m.ps[:, i, :].rearrange("p (a b) -> p a b", a=4), 4 * i, 4,
                  repeat(f.row[:, i // 2, :], 4), f.tmp[:, i % 2, :].rearrange("p (a b) -> p a b", a=4))


TERN_SEMS = {"up": 16, "silu": 16, "glu": 16, "hid": 32, "hid_read": 32, "y": 4}


def tern_setup(m, layer):
    f = Memory()
    f.layer, f.loaded = layer, 16 if layer == 0 else 32
    f.done = {k: 0 if layer == 0 else n for k, n in TERN_SEMS.items()}
    v = lambda name: view(m.packs["tern"], "tern", name)
    f.w1, f.w2 = v("w1"), v("w2")
    f.h1, f.h2 = (v(x).rearrange("p (a b) -> p a b", a=HB) for x in ("h1", "h2"))
    f.w3 = v("w3").rearrange("p (a b) -> p a b", a=HB)
    f.s1, f.s2, f.sh1, f.sh2, f.s3 = (v(x) for x in ("s1", "s2", "sh1", "sh2", "s3"))
    a = Carver(m.arena)
    f.a = a.take(HB * TOK).rearrange("p (a b) -> p a b", a=HB)
    f.b = a.take(HB * TOK).rearrange("p (a b) -> p a b", a=HB)
    f.u = a.take(2 * BLK).rearrange("p (a b) -> p a b", a=2)
    f.tmp = a.take(2 * BLK).rearrange("p (a b) -> p a b", a=2)
    f.row = a.take(2 * P).rearrange("p (a b) -> p a b", a=2)
    return f


EXPERTS, RANK = 3, 8
LOW = EXPERTS * RANK
LOW1 = LOW + 1


def mole_tensor(nc, pe, m, s, f):
    T = nc.tensor
    pe.wait_ge(m.loaded["mole"], 16)
    for layer in range(2):
        if layer == 1:
            pe.wait_ge(s["hidden"], NBLK * HB)
        for t in range(TILES):
            out = m.ps[:, 0, t * 32:t * 32 + 27]
            if layer == 0:
                last = T.matmul(out, m.hT[:, t * P:(t + 1) * P], f.ar1, start=True, stop=True)
            else:
                for k in range(HB):
                    last = T.matmul(out, f.a[:, k, t * P:(t + 1) * P], f.ar2[:, k, :], start=k == 0, stop=k == HB - 1)
        last.then_inc(s["low"], 1)
        pe.wait_ge(s["gated"], layer + 1)
        for i in range(NBLK):
            for t in range(4):
                last = T.transpose(m.ps[0:LOW1, 1 + i, t * P:(t + 1) * P], f.zg[:, 4 * i + t, :], m.ident)
            last.then_inc(s["turned"], 1)
        pe.wait_ge(s["zT"], NBLK * (layer + 1))
        if layer == 0:
            n = 0
            for i in range(NBLK):
                cols = slice(i * BLK, (i + 1) * BLK)
                for j in range(HB):
                    out = slice(j * P, (j + 1) * P)
                    if n >= 8:
                        pe.wait_ge(s["hidden"], n - 7)
                    T.matmul(m.ps[:, n % 8, :], f.w1[:, out], m.hT[:, cols], start=True, stop=False)
                    T.matmul(m.ps[:, n % 8, :], f.b1[:, out], f.zT[0:LOW1, cols], start=False,
                             stop=True).then_inc(s["hid"], 1)
                    n += 1
    for i in range(NBLK):
        for t in range(4):
            tok = slice((4 * i + t) * P, (4 * i + t + 1) * P)
            out = m.ps[:, 4 + i, t * P:(t + 1) * P]
            if i == 0 and t == 0:
                pe.wait_ge(s["zT"], 2 * NBLK)
            for k in range(HB):
                T.matmul(out, f.a[:, k, tok], f.w2[:, k, :], start=k == 0, stop=False)
            last = T.matmul(out, f.zT[0:LOW1, tok], f.b2, start=False, stop=True)
        last.then_inc(s["y"], 1)


def mole_scalar(nc, act, m, s, f):
    for layer in range(2):
        act.wait_ge(s["logits"], layer + 1)
        nc.scalar.activation(f.lg[:, :, :], f.lg[:, :, :], ACT.Exp).then_inc(s["exped"], 1)
        for i in range(NBLK):
            act.wait_ge(s["turned"], NBLK * layer + i + 1)
            if layer == 1 and i == 0:
                act.wait_ge(s["hid"], NBLK * HB)
            nc.scalar.activation(f.zT[0:LOW1, i * BLK:(i + 1) * BLK], m.ps[0:LOW1, 1 + i, :], ACT.Copy)\
                .then_inc(s["zT"], 1)
        if layer == 0:
            for n in range(NBLK * HB):
                i, j = divmod(n, HB)
                act.wait_ge(s["hid"], n + 1)
                nc.scalar.activation(f.a[:, j, i * BLK:(i + 1) * BLK], m.ps[:, n % 8, :], ACT.Relu)\
                    .then_inc(s["hidden"], 1)


def mole_vector(nc, dve, m, s, f):
    V = nc.vector
    V.memset(f.zg[:, :, LOW:LOW1], 1.0)
    for layer in range(2):
        dve.wait_ge(s["low"], layer + 1)
        zr = m.ps[:, 0, :].rearrange("p (a b) -> p a b", b=32)
        if layer == 1:
            dve.wait_ge(s["turned"], NBLK)
        V.tensor_copy(f.z[:, :, :], zr[:, :, 0:27])
        dve.drain()
        V.tensor_reduce(f.red[:, :], f.z[:, :, LOW:27], AX, ALU.max)
        dve.drain()
        V.tensor_tensor(f.lg[:, :, :], f.z[:, :, LOW:27], spread(f.red[:, :], EXPERTS), ALU.subtract)\
            .then_inc(s["logits"], 1)
        dve.wait_ge(s["exped"], layer + 1)
        V.tensor_reduce(f.red[:, :], f.lg[:, :, :], AX, ALU.add)
        dve.drain()
        V.reciprocal(f.red[:, :], f.red[:, :])
        dve.drain()
        V.tensor_scalar(f.red[:, :], f.red[:, :], 1.0 / RANK, None, ALU.mult)
        dve.drain()
        V.tensor_tensor(f.lg[:, :, :], f.lg[:, :, :], spread(f.red[:, :], EXPERTS), ALU.mult)
        dve.drain()
        for e in range(EXPERTS):
            part = slice(e * RANK, (e + 1) * RANK)
            last = V.tensor_tensor(f.zg[:, :, part], f.z[:, :, part], f.lg[:, :, e:e + 1].broadcast_to([P, TILES, RANK]),
                                   ALU.mult)
        last.then_inc(s["gated"], 1)
    for i in range(NBLK):
        dve.wait_ge(s["y"], i + 1)
        add_gated(nc, dve, m, m.ps[:, 4 + i, :].rearrange("p (a b) -> p a b", a=4), 4 * i, 4,
                  repeat(gate_row(m, 1, FFN, i // 2), 4), f.tmp[:, i % 2, :].rearrange("p (a b) -> p a b", a=4))


MOLE_SEMS = ("low", "gated", "turned", "zT", "hid", "hidden", "logits", "exped", "y")


def mole_setup(m):
    f = Memory()
    v = lambda name, rows=P: view(m.packs["mole"], "mole", name, rows)
    f.w1, f.ar1, f.b1, f.b2 = v("w1"), v("ar1"), v("b1", LOW1), v("b2", LOW1)
    f.w2 = v("w2").rearrange("p (a b) -> p a b", a=HB)
    f.ar2 = v("ar2").rearrange("p (a b) -> p a b", a=HB)
    a = Carver(m.arena)
    f.a = a.take(HB * TOK).rearrange("p (a b) -> p a b", a=HB)
    f.z = a.take(TILES * 27).rearrange("p (a b) -> p a b", b=27)
    f.zg = a.take(TILES * LOW1).rearrange("p (a b) -> p a b", b=LOW1)
    f.lg = a.take(TILES * EXPERTS).rearrange("p (a b) -> p a b", b=EXPERTS)
    f.red = a.take(TILES)
    f.zT = a.take(TOK)
    f.tmp = a.take(2 * BLK).rearrange("p (a b) -> p a b", a=2)
    return f


STATES, TAPS, INB = 16, 4, 2


def ssm_tensor(nc, pe, m, s, f):
    T = nc.tensor
    pe.wait_ge(m.loaded["l2"], 16)
    n = 0
    for j in range(2 * INB):
        for i in range(NBLK):
            if n >= 8:
                pe.wait_ge(s["proj_read"], n - 7)
            T.matmul(m.ps[:, n % 8, :], f.win[:, j * P:(j + 1) * P], m.hT[:, i * BLK:(i + 1) * BLK], start=True,
                     stop=True).then_inc(s["proj"], 1)
            n += 1
    pe.wait_ge(s["proj_read"], n)
    for j in range(INB):
        for st in range(STATES):
            k = j * STATES + st
            for i in range(NBLK):
                pe.wait_ge(s["scanned"], 2 * k + i // 2 + 1)
                last = T.matmul(m.ps[:, 4 * j + i, :], m.ident, f.h[:, k % 2, i * BLK:(i + 1) * BLK], start=st == 0,
                                stop=st == STATES - 1)
            last.then_inc(s["summed"], 1)
    pe.wait_ge(s["mixed"], INB)
    for i in range(NBLK):
        for t in range(4):
            for k in range(INB):
                last = T.matmul(m.ps[:, i, t * P:(t + 1) * P], f.y[:, k, (4 * i + t) * P:(4 * i + t + 1) * P],
                                f.wout[:, k, :], start=k == 0, stop=k == INB - 1)
        last.then_inc(s["out"], 1)


def ssm_scalar(nc, act, m, s, f):
    A = nc.scalar.activation
    n = 0
    for j in range(2 * INB):
        for i in range(NBLK):
            act.wait_ge(s["proj"], n + 1)
            if j < INB:
                b, half = divmod(i, 2)
                at = TAPS - 1 + half * BLK
                done = A(f.xs[:, j, b, at:at + BLK], m.ps[:, n % 8, :], ACT.Copy)
            else:
                done = A(f.res[:, j - INB, i * BLK:(i + 1) * BLK], m.ps[:, n % 8, :], ACT.Silu)
            done.then_inc(s["proj_read"], 1)
            n += 1
    for j in range(INB):
        act.wait_ge(s["conv"], j + 1)
        A(f.xc[:, j, :], f.acc[:, j, :], ACT.Silu, bias=f.cb[:, j:j + 1]).then_inc(s["silu"], 1)
    act.drain()
    A(f.bx[:, :, :], f.xc[:, :, :], ACT.Square)
    A(f.dt[:, :, :], f.xc[:, :, :], ACT.Abs)
    A(f.arate[:, :], f.alog, ACT.Exp)
    act.drain()
    A(f.dt[:, :, :], f.dt[:, :, :], ACT.Exp, scale=-1.0)
    act.drain()
    A(f.dt[:, :, :], f.dt[:, :, :], ACT.Ln, bias=1.0).then_inc(s["soft"], 1)
    act.wait_ge(s["delta"], 1)
    for k in range(INB * STATES):
        if k >= 2:
            act.wait_ge(s["scanned"], 2 * (k - 1))
        A(f.decay[:, k % 2, :], f.dt[:, k // STATES, :], ACT.Exp, scale=f.arate[:, k:k + 1]).then_inc(s["decayed"], 1)


def ssm_vector(nc, dve, m, s, f):
    V = nc.vector
    V.memset(f.xs[:, :, :, 0:TAPS - 1], 0.0)
    dve.drain()
    for j in range(INB):
        dve.wait_ge(s["proj_read"], (j + 1) * NBLK)
        acc = f.acc[:, j, :].rearrange("p (b t) -> p b t", b=BATCH)
        V.tensor_scalar(acc, f.xs[:, j, :, 0:SEQ], f.cw[:, j, 0:1], None, ALU.mult)
        for tap in range(1, TAPS):
            dve.drain()
            last = V.scalar_tensor_tensor(acc, f.xs[:, j, :, tap:tap + SEQ], f.cw[:, j, tap:tap + 1], acc, ALU.mult,
                                          ALU.add)
        last.then_inc(s["conv"], 1)
    dve.wait_ge(s["soft"], 1)
    V.scalar_tensor_tensor(f.dt[:, :, :], f.xc[:, :, :], 0.0, f.dt[:, :, :], ALU.max, ALU.add)
    V.tensor_scalar(f.arate[:, :], f.arate[:, :], -1.0, None, ALU.mult).then_inc(s["delta"], 1)
    dve.drain()
    for k in range(INB * STATES):
        j = k // STATES
        dve.wait_ge(s["decayed"], k + 1)
        if k >= 2:
            dve.wait_ge(s["summed"], k - 1)
        for b in range(BATCH):
            half = slice(b * SEQ, (b + 1) * SEQ)
            V.tensor_tensor_scan(f.h[:, k % 2, half], f.decay[:, k % 2, half], f.bx[:, j, half], 0.0, ALU.mult,
                                 ALU.add).then_inc(s["scanned"], 1)
    for j in range(INB):
        dve.wait_ge(s["summed"], (j + 1) * STATES)
        for i in range(NBLK):
            cols = slice(i * BLK, (i + 1) * BLK)
            V.tensor_tensor(f.y[:, j, cols], m.ps[:, 4 * j + i, :], f.xc[:, j, cols], ALU.mult)
        dve.drain()
        V.tensor_tensor(f.y[:, j, :], f.y[:, j, :], f.res[:, j, :], ALU.mult)
        dve.drain()
        V.scalar_tensor_tensor(f.y[:, j, :], f.xc[:, j, :], f.d[:, j:j + 1], f.y[:, j, :], ALU.mult, ALU.add)\
            .then_inc(s["mixed"], 1)
    for i in range(NBLK):
        dve.wait_ge(s["out"], i + 1)
        add_gated(nc, dve, m, m.ps[:, i, :].rearrange("p (a b) -> p a b", a=4), 4 * i, 4,
                  repeat(gate_row(m, 2, ATTN, i // 2), 4), f.tmp[:, i % 2, :].rearrange("p (a b) -> p a b", a=4))


SSM_SEMS = ("proj", "proj_read", "conv", "silu", "soft", "delta", "decayed", "scanned", "summed", "mixed", "out")


def ssm_setup(m):
    f = Memory()
    v = lambda name: view(m.packs["l2"], "l2", name)
    f.win, f.cb, f.d, f.alog = v("win"), v("cb"), v("d"), v("alog")
    f.cw = v("cw").rearrange("p (a b) -> p a b", a=INB)
    f.wout = v("wout").rearrange("p (a b) -> p a b", a=INB)
    a = Carver(m.arena)
    two = lambda n: a.take(2 * n).rearrange("p (a b) -> p a b", a=2)
    f.xs = a.take(INB * BATCH * (SEQ + TAPS - 1)).rearrange("p (a b t) -> p a b t", a=INB, b=BATCH)
    f.res, f.xc, f.dt, f.bx, f.decay, f.h = (two(TOK) for _ in range(6))
    f.acc, f.y = f.h, f.dt
    f.arate = a.take(INB * STATES)
    f.tmp = f.decay[:, 0, 0:2 * BLK].rearrange("p (a b) -> p a b", a=2)
    return f


HEADS, KD = 16, 8
PAIRS = BATCH * HEADS
STACK = 9 * KD
RING = 4
ROUNDS = PAIRS // RING
S_JOBS = 2 * BT + 1
LEAD = 2


def pair_at(r, par, ahead=0):
    return r + (par + ahead) // RING, (par + ahead) % RING


def pair_steps(eng, step):
    for par in range(RING):
        step(0, par, par == 0, False)
    with eng.Fori(1, ROUNDS - 1) as r:
        for par in range(RING):
            step(r, par, False, False)
    for par in range(RING):
        step(ROUNDS - 1, par, False, par >= RING - LEAD)


def mha_tensor(nc, pe, m, s, f):
    T = nc.tensor
    pe.wait_ge(m.loaded["l3"], 16)
    for n in range(12):
        if n >= 8:
            pe.wait_ge(s["proj_read"], n - 7)
        kind, i = divmod(n, NBLK)
        if kind < 2:
            T.matmul(m.ps[:, n % 8, :], (f.wq, f.wk)[kind], m.hT[:, i * BLK:(i + 1) * BLK], start=True,
                     stop=True).then_inc(s["proj"], 1)
        else:
            for t in range(4):
                last = T.matmul(m.ps[:, n % 8, t * P:(t + 1) * P], m.hT[:, (4 * i + t) * P:(4 * i + t + 1) * P], f.wv,
                                start=True, stop=True)
            last.then_inc(s["proj"], 1)
    pe.wait_ge(s["proj_read"], 12)

    def scores_job(r, par, j):
        n = RING * r + par
        job = n * S_JOBS + j
        bank = (par + j) % 2
        if j == 0:
            pe.wait_ge(s["stack"][par], 16 * 6 * (r + 1))
        if not isinstance(job, int) or job >= 2:
            pe.wait_ge(s["s_read"], job - 1)
        if j < 2 * BT:
            T.matmul(m.ps[:, bank, :], f.qst[par][0:STACK, (j // 2) * P:(j // 2 + 1) * P],
                     f.kst[par][0:STACK, (j % 2) * BLK:(j % 2 + 1) * BLK], start=True, stop=True).then_inc(s["s_made"], 1)
        else:
            pe.wait_ge(s["maxima"], n + 1)
            T.transpose(m.ps[0:BT, bank, 0:P], f.mcol[:, :], m.ident).then_inc(s["s_made"], 1)

    def exponents(r, par, kt):
        n = RING * r + par
        if kt == 0:
            pe.wait_ge(s["mrow"][par % 2], 16 * (2 * r + par // 2 + 1))
        job = n * BT + kt
        if not isinstance(job, int) or job >= 2:
            pe.wait_ge(s["exped"], job - 1)
        for half in range(2):
            last = T.matmul(m.ps[:, 2 + 2 * (kt % 2) + half, :], f.kst[par][0:STACK + 3, kt * P:(kt + 1) * P],
                            f.qst[par][0:STACK + 3, half * BLK:(half + 1) * BLK], start=True, stop=True)
        last.then_inc(s["st_made"], 1)

    def values(r, par, quad):
        n = RING * r + par
        pe.wait_ge(s["exped"], n * BT + 4 * quad + 4)
        if quad == 0:
            pe.wait_ge(s["vcopied"], n + 1)
            if not isinstance(n, int) or n >= 1:
                pe.wait_ge(s["o9"], n)
        for half in range(2):
            for g in range(4):
                kt = 4 * quad + g
                last = T.matmul(m.ps[32 * g:32 * g + 32, 6 + half, :], f.vst[par][:, kt, :],
                                f.prob[:, kt, half * BLK:(half + 1) * BLK], start=quad == 0, stop=quad == 1)
        last.then_inc(s["pv"], 1)

    def groups_sum(n):
        pe.wait_ge(s["osum"], n + 1)
        for half in range(2):
            last = T.matmul(m.ps[0:KD + 1, 6 + half, :], f.sel, f.osum[:, half * BLK:(half + 1) * BLK], start=True,
                            stop=True)
        last.then_inc(s["o9_made"], 1)

    def step(r, par, first, last):
        ahead = pair_at(r, par, LEAD)
        for kt in range(BT):
            exponents(r, par, kt)
            if not last:
                scores_job(*ahead, 2 * kt)
                scores_job(*ahead, 2 * kt + 1)
            if kt == 3 and not first:
                groups_sum(RING * r + par - 1)
            if kt == 5:
                values(r, par, 0)
        values(r, par, 1)
        if not last:
            scores_job(*ahead, 2 * BT)

    for n in range(LEAD):
        for j in range(S_JOBS):
            scores_job(0, n, j)
    pair_steps(pe, step)
    groups_sum(PAIRS - 1)

    pe.wait_ge(s["normed"], 1)
    for i in range(NBLK):
        for t in range(4):
            last = T.matmul(m.ps[:, i, t * P:(t + 1) * P], f.oT[:, (4 * i + t) * P:(4 * i + t + 1) * P], f.wo,
                            start=True, stop=True)
        last.then_inc(s["y"], 1)


def mha_scalar(nc, act, m, s, f):
    A = nc.scalar.activation
    for n in range(12):
        kind, i = divmod(n, NBLK)
        act.wait_ge(s["proj"], n + 1)
        if kind < 2:
            A((f.q, f.k)[kind][:, i * BLK:(i + 1) * BLK], m.ps[:, n % 8, :], ACT.Copy).then_inc(s["proj_read"], 1)
        else:
            for t in range(4):
                b, kt = divmod(4 * i + t, BT)
                last = A(f.v[:, b, :, kt, :], m.ps[:, n % 8, t * P:(t + 1) * P].rearrange("p (h v) -> p h v", h=HEADS),
                         ACT.Copy)
            last.then_inc(s["proj_read"], 1)

    def collect(n):
        act.wait_ge(s["pv"], 2 * n + 2)
        if not isinstance(n, int) or n >= 1:
            act.wait_ge(s["o9_made"], n)
        A(f.osum[:, :].rearrange("p (a b) -> p a b", a=2), m.ps[:, 6:8, :], ACT.Copy).then_inc(s["osum"], 1)

    def collect_sum(n, r, par):
        act.wait_ge(s["o9_made"], n + 1)
        if not isinstance(n, int) or n >= 2:
            act.wait_ge(s["ostored"][par % 2], 16 * (2 * r + par // 2))
        A(f.out9[par % 2][:, :].rearrange("p (a b) -> p a b", a=2), m.ps[0:KD + 1, 6:8, :], ACT.Copy)\
            .then_inc(s["o9"], 1)

    def step(r, par, first, last):
        n = RING * r + par
        before_r, before_par = pair_at(r, par, -1)
        for kt in range(BT):
            act.wait_ge(s["st_made"], n * BT + kt + 1)
            if kt % 4 == 0 and not first:
                act.wait_ge(s["pv"], 2 * n - 1 + kt // 4)
            slot = 2 + 2 * (kt % 2)
            A(f.prob[:, kt, :].rearrange("p (a b) -> p a b", a=2), m.ps[:, slot:slot + 2, :], ACT.Exp,
              scale=float(KD) ** -0.5).then_inc(s["exped"], 1)
            if kt == 1 and not first:
                collect(n - 1)
            if kt == 3 and not first:
                collect_sum(n - 1, before_r, before_par)

    act.wait_ge(s["sent"], 6 * 16)
    pair_steps(act, step)
    collect(PAIRS - 1)
    collect_sum(PAIRS - 1, ROUNDS - 1, RING - 1)


def mha_vector(nc, dve, m, s, f):
    V = nc.vector
    for par in range(RING):
        V.memset(f.kst[par][0:96, :], 1.0)
        V.memset(f.vst[par][:, :, :], 0.0)
    dve.drain()
    for par in range(RING):
        V.memset(f.vst[par][:, :, KD:KD + 1], 1.0)
    dve.drain().then_inc(s["ones"], 1)
    for a, (src, dst) in enumerate(((f.q, f.qp), (f.k, f.kp))):
        dve.wait_ge(s["proj_read"], 4 * (a + 1))
        for part in range(3):
            V.tensor_copy(dst[:, part, :], src[:, :]).then_inc(s["parts"], 1)
            if part < 2:
                dve.drain()
                V.tensor_tensor(src[:, :], src[:, :], dst[:, part, :], ALU.subtract)
                dve.drain()

    def row_max(r, par, j):
        n = RING * r + par
        dve.wait_ge(s["s_made"], n * S_JOBS + j + 1)
        V.tensor_reduce(f.mp[:, j:j + 1], m.ps[:, (par + j) % 2, :], AX, ALU.max).then_inc(s["s_read"], 1)

    def maxima(r, par):
        n = RING * r + par
        dve.drain()
        mp = f.mp[:, :].rearrange("p (a b) -> p a b", b=2)
        V.tensor_tensor(f.mcol[:, :], mp[:, :, 0], mp[:, :, 1], ALU.max).then_inc(s["maxima"], 1)
        dve.wait_ge(s["s_made"], n * S_JOBS + S_JOBS)
        V.tensor_scalar(f.mneg[:, :], m.ps[0:BT, par % 2, 0:P], -1.0, None, ALU.mult).then_inc(s["s_read"], 1)
        dve.drain()
        if not isinstance(n, int) or n >= 1:
            dve.wait_ge(s["mstored"], 16 * n)
        V.tensor_copy(f.mparts[:, 0, :], f.mneg[:, :])
        dve.drain()
        V.tensor_tensor(f.mneg[:, :], f.mneg[:, :], f.mparts[:, 0, :], ALU.subtract)
        dve.drain()
        V.tensor_copy(f.mparts[:, 1, :], f.mneg[:, :])
        dve.drain()
        V.tensor_tensor(f.mparts[:, 2, :], f.mneg[:, :], f.mparts[:, 1, :], ALU.subtract).then_inc(s["mparts"], 1)

    def step(r, par, first, last):
        if not last:
            ahead = pair_at(r, par, LEAD)
            for j in range(2 * BT):
                row_max(*ahead, j)
            maxima(*ahead)

    for n in range(LEAD):
        for j in range(2 * BT):
            row_max(0, n, j)
        maxima(0, n)
    pair_steps(dve, step)

    dve.wait_ge(s["finals"], 2 * HEADS * 16)
    V.reciprocal(f.denom[:, :], f.denom[:, :])
    dve.drain()
    V.tensor_tensor(f.oT[:, :], f.oT[:, :], f.denom[:, :], ALU.mult).then_inc(s["normed"], 1)
    for i in range(NBLK):
        dve.wait_ge(s["y"], i + 1)
        add_gated(nc, dve, m, m.ps[:, i, :].rearrange("p (a b) -> p a b", a=4), 4 * i, 4,
                  repeat(gate_row(m, 3, ATTN, i // 2), 4), f.tmp[:, i % 2, :].rearrange("p (a b) -> p a b", a=4))


def mha_gpsimd(nc, pool, m, s, f):
    pool.wait_ge(s["proj_read"], 12)
    pool.wait_ge(s["ones"], 1)

    def pair(r, par):
        n = RING * r + par
        if not isinstance(r, int) or r >= 1:
            pool.wait_ge(s["pv"], 2 * (n - RING) + 2)
        nc.gpsimd.tensor_copy(f.vst[par][:, :, 0:KD],
                              f.vflat[:, bass.ds(n * (BT * KD), BT * KD)].rearrange("p (a b) -> p a b", b=KD))\
            .then_inc(s["vcopied"], 1)

    for par in range(RING):
        pair(0, par)
    with pool.Fori(1, ROUNDS) as r:
        for par in range(RING):
            pair(r, par)


def mha_sync(nc, sp, m, s, f):
    for a, (src, dst) in enumerate(((f.qp, f.scr_q), (f.kp, f.scr_k))):
        for part in range(3):
            sp.wait_ge(s["parts"], 3 * a + part + 1)
            sp.dma_start(f.scr_parts[a, part].rearrange("(b r) t -> r b t", b=BATCH),
                         src[:, part, :].rearrange("p (b t) -> p b t", b=BATCH)).then_inc(s["sent"], 16)
    sp.wait_ge(s["sent"], 6 * 16)
    for a, dst in enumerate((f.scr_q, f.scr_k)):
        for at in range(5 if a == 0 else 3):
            part = at % 3
            sp.dma_start(dst[:, at, :, :], f.scr_parts[a, part].rearrange("(n k) t -> n k t", k=KD))\
                .then_inc(s["grouped"], 16)
    sp.wait_ge(s["grouped"], 8 * 16)
    sp.wait_ge(s["ones"], 1)

    def stacks(r, par):
        n = RING * r + par
        if not isinstance(r, int) or r >= 1:
            sp.wait_ge(s["pv"], 2 * (n - RING) + 2)
        q_rows = f.scr_q.rearrange("n p k t -> (n p k) t")
        k_rows = f.scr_k.rearrange("n p k t -> (n p k) t")
        for a in range(3):
            at = slice(a * 3 * KD, (a + 1) * 3 * KD)
            sp.dma_start(f.qst[par][at, :], q_rows[bass.ds(n * (5 * KD) + a * KD, 3 * KD), :])\
                .then_inc(s["stack"][par], 16)
            sp.dma_start(f.kst[par][at, :], k_rows[bass.ds(n * (3 * KD), 3 * KD), :]).then_inc(s["stack"][par], 16)

    def maxima(r, par):
        n = RING * r + par
        sp.wait_ge(s["mparts"], n + 1)
        sp.dma_start(f.scr_m[par].rearrange("s (q t) -> q s t", q=BT), f.mparts[:, :, :]).then_inc(s["mstored"], 16)
        sp.wait_ge(s["mstored"], 16 * n + 16)
        sp.dma_start(f.qst[par][STACK:STACK + 3, :], f.scr_m[par]).then_inc(s["mrow"][par % 2], 16)

    def store(r, par):
        n = RING * r + par
        sp.wait_ge(s["o9"], n + 1)
        sp.dma_start(f.scr_o[bass.ds(n, 1), :, :].rearrange("a r t -> (a r) t"), f.out9[par % 2][:, :])\
            .then_inc(s["ostored"][par % 2], 16)

    def step(r, par, first, last):
        if not first:
            store(*pair_at(r, par, -1))
        ahead = pair_at(r, par, LEAD + 1)
        if not isinstance(r, int) or RING * r + par + LEAD + 1 < PAIRS:
            stacks(*ahead)
        if not last:
            maxima(*pair_at(r, par, LEAD))

    for n in range(LEAD + 1):
        stacks(0, n)
    for n in range(LEAD):
        maxima(0, n)
    pair_steps(sp, step)
    store(ROUNDS - 1, RING - 1)
    for k in range(2):
        sp.wait_ge(s["ostored"][k], 16 * PAIRS // 2)
    for h in range(HEADS):
        rows = slice(h * KD, (h + 1) * KD)
        here = f.scr_o.rearrange("(b h) r t -> h r b t", b=BATCH)[h]
        sp.dma_start(f.oT[rows, :].rearrange("p (b t) -> p b t", b=BATCH), here[0:KD]).then_inc(s["finals"], 16)
        sp.dma_start(f.denom[rows, :].rearrange("p (b t) -> p b t", b=BATCH),
                     here[KD:KD + 1].broadcast_to([KD, BATCH, SEQ])).then_inc(s["finals"], 16)


MHA_SEMS = ("proj", "proj_read", "parts", "sent", "grouped", "ones", "stack0", "stack1", "stack2", "stack3",
            "s_made", "s_read", "maxima", "mparts", "mstored", "mrow0", "mrow1", "st_made", "exped",
            "vcopied", "pv", "osum", "o9_made", "o9", "ostored0", "ostored1", "finals",
            "normed", "y")


def mha_setup(m):
    f = Memory()
    nc = m.d["nc"]
    v = lambda name: view(m.packs["l3"], "l3", name)
    f.wq, f.wk, f.wv, f.wo = v("wq"), v("wk"), v("wv"), v("wo")
    f.sel = view(m.packs["const"], "const", "sel")
    f.scr_parts = nc.dram_tensor("scr_parts", (2, 3, PAIRS * KD, SEQ), BF16).ap()
    f.scr_q = nc.dram_tensor("scr_q", (PAIRS, 5, KD, SEQ), BF16).ap()
    f.scr_k = nc.dram_tensor("scr_k", (PAIRS, 3, KD, SEQ), BF16).ap()
    f.scr_m = nc.dram_tensor("scr_m", (RING, 3, SEQ), BF16).ap()
    f.scr_o = nc.dram_tensor("scr_o", (PAIRS, KD + 1, SEQ), F32).ap()
    a = Carver(m.arena, DEEP_AT // 2)
    f.qst = [a.bf16(SEQ) for _ in range(RING)]
    f.kst = [a.bf16(SEQ) for _ in range(RING)]
    f.vst = [a.take(BT * 32).rearrange("p (a b) -> p a b", b=32) for _ in range(RING)]
    f.vflat = a.take(TOK)
    f.v = f.vflat.rearrange("p (b h t v) -> p b h t v", b=BATCH, h=HEADS, t=BT)
    f.osum = a.take(SEQ)
    f.out9 = [a.take(SEQ)[0:KD + 1, :] for _ in range(2)]
    f.mp, f.mcol = a.take(2 * BT), a.take(BT)
    f.mneg = a.take(P)[0:BT, :]
    f.mparts = a.bf16(3 * P + 128)[0:BT, 0:3 * P].rearrange("p (s t) -> p s t", s=3)
    early = Carver(m.arena, a.at)
    f.q, f.k = early.take(TOK), early.take(TOK)
    f.qp, f.kp = (early.bf16(3 * TOK).rearrange("p (s t) -> p s t", s=3) for _ in range(2))
    main = Carver(m.arena, a.at)
    f.prob = main.take(BT * SEQ).rearrange("p (a b) -> p a b", a=BT)
    late = Carver(m.arena, a.at)
    f.oT, f.denom = late.take(TOK), late.take(TOK)
    f.tmp = late.take(2 * BLK).rearrange("p (a b) -> p a b", a=2)
    return f


DH = 64
LH = 16
INNER = LH * DH
QB = INNER // P
WIN = 32
HALF = P // 2
SPAN = WIN + HALF
KEYS = WIN + P
FRONT = WIN + 1
ORDER = [h for h in range(0, LH, 2)] + [h for h in range(1, LH, 2)]
GROUP = 4
NORM_SHIFT = 2.0 ** 20
GUARD = 1e-24
FF = 341
FF_ROWS = [P, P, FF - 2 * P]
LOOPED = BT - 1


class Ring:

    def __init__(self, made, freed, start, tile, last):
        self.made, self.freed = made, freed
        self.jobs = {"start": start, "tile": tile, "last0": last[0], "last1": last[1]}
        n = len(tile)
        self.at = {"start": 0, "tile": len(start), "last0": len(start) + 2 * LOOPED * n}
        self.at["last1"] = self.at["last0"] + len(last[0])
        self.total = self.at["last1"] + len(last[1])
        assert self.total % 2 == 0

    def position(self, where, name):
        rnd, kind, c, b = where
        if kind == "last":
            kind = f"last{b}"
        i = self.at[kind] + self.jobs[kind].index(name)
        before = rnd * (self.total // 2)
        if kind == "tile":
            n = len(self.jobs["tile"])
            i += n * b
            before = before + n * c
        return i % 2, before + i // 2

    def place(self, where, name):
        return self.position(where, name)[0]

    def before_fill(self, eng, where, name):
        place, before = self.position(where, name)
        eng.wait_ge(self.freed[place], before)

    def before_read(self, eng, where, name):
        place, before = self.position(where, name)
        eng.wait_ge(self.made[place], before + 1)

    def after_read(self, eng, where, name):
        place, before = self.position(where, name)
        eng.wait_ge(self.freed[place], before + 1)


def deep_rings(s):
    wide = Ring(s["wide_made"], s["wide_freed"], start=["q0", "k0", "q1", "k1", "v0", "v1"],
                tile=["q", "p0", "k", "p1", "v0", "heads", "v1"],
                last=(["p0", "p1", "v0", "heads", "v1"], ["p0", "p1", "heads"]))
    tile = ["t0", "t1", "o0", "o1", "t2", "t3", "y"]
    turn = Ring(s["turn_made"], s["turn_freed"], start=["t0", "t1", "t2", "t3"], tile=tile, last=(tile, ["o0", "o1", "y"]))
    groups = [f"s{j}" for j in range(LH // GROUP)]
    score = Ring(s["score_made"], s["score_freed"], start=[], tile=groups, last=(groups, groups))
    return wide, score, turn


def deep_rounds(eng, start, tile, ffn):
    with eng.Fori(0, DEPTH // 2) as dd:
        for par in range(2):
            rnd = 2 * dd + par
            start(rnd, dd, par)
            with eng.Fori(0, LOOPED) as c:
                for b in range(BATCH):
                    tile((rnd, "tile", c, b), 16 * rnd + 2 * c + b, c, b, par, True, True)
            for b in range(BATCH):
                tile((rnd, "last", LOOPED, b), 16 * rnd + 2 * LOOPED + b, LOOPED, b, par, False, b == 0)
            if ffn is not None:
                ffn(rnd, par)


def deep_tensor(nc, pe, m, s, f):
    T = nc.tensor
    wide, score, turn = deep_rings(s)
    pe.wait_ge(s["ready"], 1)

    def project(w, where, name, j, b, rows):
        wide.before_fill(pe, where, name)
        at = 2 * wide.place(where, name)
        for half in range(2):
            last = T.matmul(m.ps[0:rows.stop - rows.start, at + half, :], f.xs[b][:, rows],
                            w.wqkv[:, j * INNER + half * BLK:j * INNER + (half + 1) * BLK], start=True, stop=True)
        last.then_inc(wide.made[wide.place(where, name)], 1)

    def values(w, where, b, half):
        project(w, where, f"v{half}", 2, b, slice(HALF * half, HALF * half + SPAN))

    def turned(where, name, src, k0):
        turn.before_fill(pe, where, name)
        place = turn.place(where, name)
        for i in range(4):
            last = T.transpose(m.ps[:, 6 + place, i * P:(i + 1) * P], src[:, (k0 + i) * P:(k0 + i + 1) * P], m.ident)
        last.then_inc(turn.made[place], 1)

    def start(rnd, dd, par):
        where, w = (rnd, "start", 0, 0), f.w[par]
        for b in range(BATCH):
            pe.wait_ge(s["staged"], 16 * rnd + b + 1)
            pe.wait_ge(s["weights"][par], 16 * dd + 16)
            project(w, where, f"q{b}", 0, b, slice(WIN, KEYS))
            project(w, where, f"k{b}", 1, b, slice(WIN, KEYS))
        values(w, where, 0, 0)
        values(w, where, 0, 1)
        pe.wait_ge(s["rotated"], 16 * rnd + 1)
        for j in range(4):
            turned(where, f"t{j}", f.rot[0], 4 * j)

    def tile(where, t, c, b, par, ahead2, ahead1):
        w = f.w[par]

        def scores(j):
            name = f"s{j}"
            score.before_fill(pe, where, name)
            bank = 4 + score.place(where, name)
            T.matmul(m.ps[:, bank, 0:GROUP * SPAN], f.identb,
                     f.bands[:, bass.ds(c, 1), :].broadcast_to([P, GROUP, SPAN]), start=True, stop=False,
                     skip_group_check=True)
            for i, h in enumerate(ORDER[GROUP * j:GROUP * (j + 1)]):
                rows = slice(DH * (h % 2), DH * (h % 2) + DH)
                for half in range(2):
                    last = T.matmul(m.ps[HALF * half:HALF * (half + 1), bank, i * SPAN:(i + 1) * SPAN],
                                    f.qT[rows, h // 2, HALF * half:HALF * (half + 1)],
                                    f.kT[b][rows, h // 2, HALF * half:HALF * half + SPAN], start=False, stop=True,
                                    skip_group_check=True)
            last.then_inc(score.made[score.place(where, name)], 1)

        def probs(j):
            name = f"p{j}"
            score.after_read(pe, where, f"s{2 * j}")
            score.after_read(pe, where, f"s{2 * j + 1}")
            wide.before_fill(pe, where, name)
            place = wide.place(where, name)
            for i in range(8):
                last = T.transpose(m.ps[0:SPAN, 2 * place + i // 4, (i % 4) * P:(i % 4 + 1) * P],
                                   f.prob[:, 8 * j + i, :], m.ident)
            last.then_inc(wide.made[place], 1)

        pe.wait_ge(s["turned"], t + 1)
        scores(0)
        scores(1)
        if ahead2:
            pe.wait_ge(s["staged"], t + 3)
            project(w, where, "q", 0, b, slice(WIN, KEYS))
        scores(2)
        scores(3)
        probs(0)
        if ahead2:
            project(w, where, "k", 1, b, slice(WIN, KEYS))
        probs(1)
        if ahead1:
            values(w, where, 1 - b, 0)
        wide.before_fill(pe, where, "heads")
        wide.after_read(pe, where, "p0")
        wide.after_read(pe, where, "p1")
        pe.wait_ge(s["v0_copied"], t + 1)
        pe.wait_ge(s["v1_copied"], t + 1)
        at = 2 * wide.place(where, "heads")
        for p, h in enumerate(ORDER):
            col = (h % 8) * DH
            for half in range(2):
                last = T.matmul(m.ps[HALF * half:HALF * (half + 1), at + h // 8, col:col + DH],
                                f.pT[0:SPAN, p, HALF * half:HALF * (half + 1)], f.v[0:SPAN, half, h * DH:(h + 1) * DH],
                                start=True, stop=True)
        last.then_inc(wide.made[wide.place(where, "heads")], 1)
        if ahead1:
            pe.wait_ge(s["rotated"], t + 2)
            turned(where, "t0", f.rot[1 - b], 0)
            turned(where, "t1", f.rot[1 - b], 4)
            values(w, where, 1 - b, 1)
        pe.wait_ge(s["normed"], t + 1)
        turned(where, "o0", f.o, 0)
        turned(where, "o1", f.o, 4)
        if ahead1:
            turned(where, "t2", f.rot[1 - b], 8)
            turned(where, "t3", f.rot[1 - b], 12)
        turn.before_fill(pe, where, "y")
        turn.after_read(pe, where, "o0")
        turn.after_read(pe, where, "o1")
        place = turn.place(where, "y")
        for k in range(QB):
            last = T.matmul(m.ps[:, 6 + place, 0:P], w.wo[:, k, :], f.oT[:, k, :], start=k == 0, stop=k == QB - 1)
        last.then_inc(turn.made[place], 1)

    def ffn(rnd, par):
        w = f.w[par]
        for i in range(NBLK):
            pe.wait_ge(s["shifted"], NBLK * rnd + i + 1)
            T.matmul(m.ps[:, i, :], f.mean, f.g.xc[:, i, :], start=True, stop=True).then_inc(s["mean"], 1)
        for i in range(NBLK):
            pe.wait_ge(s["squared"], NBLK * rnd + i + 1)
            T.matmul(m.ps[:, 4 + i, :], f.mean, f.g.sq[:, i, :], start=True, stop=True).then_inc(s["var"], 1)
        pe.wait_ge(s["hn"], NBLK * rnd + NBLK)

        def second(i):
            pe.wait_ge(s["glu"], 12 * rnd + 3 * i + 3)
            if i >= 2:
                pe.wait_ge(s["added"], NBLK * rnd + i - 1)
            for k, rows in enumerate(FF_ROWS):
                last = T.matmul(m.ps[:, 6 + i % 2, :], w.w2[0:rows, k, :], f.g.u[i % 2][0:rows, k, :], start=k == 0,
                                stop=k == 2)
            last.then_inc(s["second"], 1)

        for i in range(NBLK):
            for k, rows in enumerate(FF_ROWS):
                p = 3 * i + k
                if p >= 3:
                    pe.wait_ge(s["glu"], 12 * rnd + p - 2)
                for e in range(2):
                    at = e * FF + k * P
                    last = T.matmul(m.ps[0:rows, 2 * (p % 3) + e, :], w.w1[:, at:at + rows], m.hT[:, i * BLK:(i + 1) * BLK],
                                    start=True, stop=True)
                last.then_inc(s["first"], 1)
            if i > 0:
                second(i - 1)
        second(NBLK - 1)

    deep_rounds(pe, start, tile, ffn)

    pe.wait_ge(s["added"], NBLK * DEPTH)
    for t in range(TILES):
        b, c = divmod(t, BT)
        last = T.transpose(m.ps[:, t // 4, (t % 4) * P:(t % 4 + 1) * P],
                           f.xa[:, b, FRONT + c * P:FRONT + (c + 1) * P], m.ident)
        if t % 4 == 3:
            last.then_inc(s["final"], 1)


def deep_scalar(nc, act, m, s, f):
    A = nc.scalar.activation
    wide, score, turn = deep_rings(s)
    act.wait_ge(s["ready"], 1)

    def raw(where, name, j, t, b):
        wide.before_read(act, where, name)
        place = wide.place(where, name)
        A(f.raw[b][:, j * INNER:(j + 1) * INNER].rearrange("p (a b) -> p a b", a=2),
          m.ps[:, 2 * place:2 * place + 2, :], ACT.Copy).then_inc(wide.freed[place], 1)
        if j == 1:
            act.drain().then_inc(s["raw"], 1)

    def values(where):
        wide.before_read(act, where, "v0")
        place = wide.place(where, "v0")
        A(f.v[0:SPAN, 0, :].rearrange("p (a b) -> p a b", a=2), m.ps[0:SPAN, 2 * place:2 * place + 2, :], ACT.Copy)\
            .then_inc(wide.freed[place], 1)
        act.drain().then_inc(s["v0_copied"], 1)

    def stage(t, c, b):
        A(f.xs[b][0:64, :], f.xa[0:64, b, bass.ds(1 + c * P, KEYS)], ACT.Copy)
        A(f.xs[b][64:P, :], f.xa[64:P, b, bass.ds(c * P, KEYS)], ACT.Copy)
        act.drain().then_inc(s["staged"], 1)

    def norms(t, b):
        act.wait_ge(s["sumsq"], t + 1)
        A(f.ss[b], f.ss[b], ACT.Ln, scale=NORM_SHIFT)
        act.drain()
        A(f.ss[b], f.ss[b], ACT.Exp, scale=-0.5).then_inc(s["rnorm"], 1)

    def turned(where, name, dst):
        turn.before_read(act, where, name)
        place = turn.place(where, name)
        A(dst, m.ps[:, 6 + place, :].rearrange("p (a b) -> p a b", a=4), ACT.Copy).then_inc(turn.freed[place], 1)

    def queries(where):
        turned(where, "t0", f.qT[:, 0:4, :])
        turned(where, "t1", f.qT[:, 4:8, :])

    def keys(where, b):
        turned(where, "t2", f.kT[b][:, 0:4, WIN:KEYS])
        turned(where, "t3", f.kT[b][:, 4:8, WIN:KEYS])
        act.drain().then_inc(s["turned"], 1)

    def carry(where, b):
        turn.before_read(act, where, "t0")
        A(f.kT[b][:, :, 0:WIN], f.kT[b][:, :, P:KEYS], ACT.Copy)
        act.drain()

    def start(rnd, dd, par):
        where = (rnd, "start", 0, 0)
        act.wait_ge(s["weights"][par], 16 * dd + 16)
        A(f.spare, f.eps, ACT.Copy)
        act.preload_act_table_set(EXP_LN)
        act.wait_ge(s["ready"], rnd + 2)
        for b in range(BATCH):
            stage(16 * rnd + b, 0, b)
        for b in range(BATCH):
            raw(where, f"q{b}", 0, None, b)
            raw(where, f"k{b}", 1, None, b)
        values(where)
        norms(16 * rnd, 0)
        carry(where, 0)
        queries(where)
        keys(where, 0)

    def tile(where, t, c, b, par, ahead2, ahead1):
        def exponentials(j):
            act.wait_ge(s["maxima"], 4 * t + j + 1)
            place = score.place(where, f"s{j}")
            for i in range(GROUP):
                p = GROUP * j + i
                last = A(f.prob[:, p, :], m.ps[:, 4 + place, i * SPAN:(i + 1) * SPAN], ACT.Exp,
                         bias=f.nmax[b][:, p:p + 1], accum_out=f.rsum[b][:, ORDER[p]:ORDER[p] + 1])
            last.then_inc(score.freed[place], 1)

        if ahead2:
            act.wait_ge(s["v1_copied"], t + 1)
            stage(t + 2, c + 1, b)
        if ahead1:
            norms(t + 1, 1 - b)
        exponentials(0)
        exponentials(1)
        if ahead2:
            act.wait_ge(s["rotated"], t + 1)
            raw(where, "q", 0, t + 2, b)
        exponentials(2)
        exponentials(3)
        if ahead2:
            raw(where, "k", 1, t + 2, b)
        wide.before_read(act, where, "p1")
        place = wide.place(where, "p1")
        A(f.pT[0:SPAN, 8:16, :], m.ps[0:SPAN, 2 * place:2 * place + 2, :].rearrange("p a (i b) -> p (a i) b", b=P),
          ACT.Copy).then_inc(wide.freed[place], 1)
        if ahead1:
            wide.before_read(act, where, "heads")
            values(where)
            carry(where, 1 - b)
            queries(where)
        turned(where, "o0", f.oT[:, 0:4, :])
        if ahead1:
            keys(where, 1 - b)

    def ffn(rnd, par):
        w = f.w[par]
        for i in range(NBLK):
            act.wait_ge(s["centred"], NBLK * rnd + i + 1)
            A(f.g.sq[:, i, :], f.g.xc[:, i, :], ACT.Square).then_inc(s["squared"], 1)
        for i in range(NBLK):
            act.wait_ge(s["var"], NBLK * rnd + i + 1)
            A(f.g.sq[:, i, :], m.ps[:, 4 + i, :], ACT.Ln, bias=f.eps)
            act.drain()
            A(f.g.sq[:, i, :], f.g.sq[:, i, :], ACT.Exp, scale=-0.5).then_inc(s["rstd"], 1)
        for p in range(3 * NBLK):
            k = p % 3
            rows = FF_ROWS[k]
            act.wait_ge(s["first"], 12 * rnd + p + 1)
            if p >= 2:
                act.wait_ge(s["glu"], 12 * rnd + p - 1)
            A(f.g.gl[0:rows, p % 2, :], m.ps[0:rows, 2 * (p % 3) + 1, :], ACT.Gelu,
              bias=w.b1[0:rows, 3 + k:4 + k]).then_inc(s["gelu"], 1)

    deep_rounds(act, start, tile, ffn)


def deep_vector(nc, dve, m, s, f):
    V = nc.vector
    wide, score, turn = deep_rings(s)
    for x in (f.xa, f.xb):
        V.memset(x[:, :, 0:FRONT], 0.0)
    V.tensor_copy(f.xa[:, :, FRONT:FRONT + SEQ], m.hT[:, :].rearrange("p (b t) -> p b t", b=BATCH))
    V.memset(f.mean, 1.0 / P)
    V.memset(f.eps, EPS)
    V.tensor_copy(f.identb, m.ident)
    V.tensor_copy(f.bands[:, 0, :], f.band0)
    V.tensor_copy(f.bands[:, 1:BT, :], repeat(f.band, BT - 1))
    dve.drain().then_inc(s["ready"], 1)

    def values(where):
        wide.before_read(dve, where, "v1")
        place = wide.place(where, "v1")
        V.tensor_copy(f.v[0:SPAN, 1, :].rearrange("p (a b) -> p a b", a=2), m.ps[0:SPAN, 2 * place:2 * place + 2, :])\
            .then_inc(wide.freed[place], 1)
        dve.drain().then_inc(s["v1_copied"], 1)

    def norms(t, b):
        dve.wait_ge(s["cosines"], t + 1)
        V.tensor_reduce(f.ss[b], f.sq[b].rearrange("p (h d) -> p h d", d=DH), AX, ALU.add)
        dve.drain()
        V.tensor_scalar(f.ss[b], f.ss[b], GUARD, None, ALU.max).then_inc(s["sumsq"], 1)

    def sines(c, b, js=(0, 1)):
        for j in js:
            raw = f.raw[b][:, j * INNER:(j + 1) * INNER].rearrange("p (h d) -> p h d", d=DH)
            to = f.sq[b][:, j * INNER:(j + 1) * INNER].rearrange("p (h d) -> p h d", d=DH)
            for e in range(2):
                here, there = slice(32 * e, 32 * e + 32), slice(32 - 32 * e, 64 - 32 * e)
                V.tensor_tensor(to[:, :, here], raw[:, :, there],
                                f.tab[:, bass.ds(c, 1), 2 * j + 1, here].broadcast_to([P, LH, 32]), ALU.mult)

    def rotate(t, b):
        dve.drain()
        V.tensor_tensor(f.rot[b], f.rot[b], f.sq[b], ALU.add)
        dve.drain()
        dve.wait_ge(s["rnorm"], t + 1)
        r = f.rot[b].rearrange("p (h d) -> p h d", d=DH)
        V.tensor_tensor(r, r, spread(f.ss[b], DH), ALU.mult).then_inc(s["rotated"], 1)

    def start(rnd, dd, par):
        where = (rnd, "start", 0, 0)
        for b in range(BATCH):
            V.memset(f.kT[b][:, :, P:KEYS], 0.0)
        dve.drain().then_inc(s["ready"], 1)
        norms(16 * rnd, 0)
        sines(0, 0)
        rotate(16 * rnd, 0)
        values(where)
        norms(16 * rnd + 1, 1)

    def tile(where, t, c, b, par, ahead2, ahead1):
        def maxima(j):
            name = f"s{j}"
            score.before_read(dve, where, name)
            bank = 4 + score.place(where, name)
            V.tensor_reduce(f.nmax[b][:, GROUP * j:GROUP * (j + 1)],
                            m.ps[:, bank, 0:GROUP * SPAN].rearrange("p (h k) -> p h k", h=GROUP), AX, ALU.max,
                            negate=True).then_inc(s["maxima"], 1)

        maxima(0)
        maxima(1)
        if ahead1:
            sines(c + b, 1 - b, (0,))
        maxima(2)
        maxima(3)
        wide.before_read(dve, where, "p0")
        place = wide.place(where, "p0")
        V.tensor_copy(f.pT[0:SPAN, 0:8, :],
                      m.ps[0:SPAN, 2 * place:2 * place + 2, :].rearrange("p a (i b) -> p (a i) b", b=P))\
            .then_inc(wide.freed[place], 1)
        if ahead1:
            sines(c + b, 1 - b, (1,))
            rotate(t + 1, 1 - b)
        score.after_read(dve, where, "s2")
        score.after_read(dve, where, "s3")
        V.reciprocal(f.rsum[b], f.rsum[b])
        dve.drain()
        wide.before_read(dve, where, "heads")
        place = wide.place(where, "heads")
        V.tensor_tensor(f.o.rearrange("p (h d) -> p h d", d=DH),
                        m.ps[:, 2 * place:2 * place + 2, :].rearrange("p a (h d) -> p (a h) d", d=DH),
                        spread(f.rsum[b], DH), ALU.mult).then_inc(wide.freed[place], 1)
        dve.drain().then_inc(s["normed"], 1)
        turn.before_read(dve, where, "o1")
        place = turn.place(where, "o1")
        V.tensor_copy(f.oT[:, 4:8, :], m.ps[:, 6 + place, :].rearrange("p (a b) -> p a b", a=4))\
            .then_inc(turn.freed[place], 1)
        if ahead1:
            values(where)
        if ahead2:
            norms(t + 2, b)
        turn.before_read(dve, where, "y")
        place = turn.place(where, "y")
        here = bass.ds(FRONT + c * P, P)
        V.tensor_tensor(f.xb[:, b, here], m.ps[:, 6 + place, 0:P], f.xa[:, b, here], ALU.add)\
            .then_inc(turn.freed[place], 1)

    def ffn(rnd, par):
        w = f.w[par]
        dve.drain()
        for i in range(NBLK):
            b, half = divmod(i, 2)
            at = half * BLK
            V.tensor_copy(f.g.xc[0:64, i, :], f.xb[0:64, b, FRONT + at:FRONT + at + BLK])
            V.tensor_copy(f.g.xc[64:P, i, :], f.xb[64:P, b, FRONT + at - 1:FRONT + at - 1 + BLK]).then_inc(s["shifted"], 1)
        for i in range(NBLK):
            dve.wait_ge(s["mean"], NBLK * rnd + i + 1)
            V.tensor_tensor(f.g.xc[:, i, :], f.g.xc[:, i, :], m.ps[:, i, :], ALU.subtract).then_inc(s["centred"], 1)
        for i in range(NBLK):
            dve.wait_ge(s["rstd"], NBLK * rnd + i + 1)
            V.tensor_tensor(f.g.xc[:, i, :], f.g.xc[:, i, :], f.g.sq[:, i, :], ALU.mult)
            dve.drain()
            V.tensor_scalar(m.hT[:, i * BLK:(i + 1) * BLK], f.g.xc[:, i, :], w.lng, w.lnb, ALU.mult, ALU.add)\
                .then_inc(s["hn"], 1)

        def add(i):
            b, half = divmod(i, 2)
            here = slice(FRONT + half * BLK, FRONT + (half + 1) * BLK)
            dve.wait_ge(s["second"], NBLK * rnd + i + 1)
            V.scalar_tensor_tensor(f.xa[:, b, here], m.ps[:, 6 + i % 2, :], w.b2, f.xb[:, b, here], ALU.add,
                                   ALU.add).then_inc(s["added"], 1)

        for i in range(NBLK):
            for k, rows in enumerate(FF_ROWS):
                p = 3 * i + k
                dve.wait_ge(s["gelu"], 12 * rnd + p + 1)
                if i >= 2 and k == 0:
                    dve.wait_ge(s["second"], NBLK * rnd + i - 1)
                V.scalar_tensor_tensor(f.g.u[i % 2][0:rows, k, :], m.ps[0:rows, 2 * (p % 3), :],
                                       w.b1[0:rows, k:k + 1], f.g.gl[0:rows, p % 2, :], ALU.add, ALU.mult)\
                    .then_inc(s["glu"], 1)
            if i > 0:
                add(i - 1)
        add(NBLK - 1)

    deep_rounds(dve, start, tile, ffn)
    for i in range(NBLK):
        dve.wait_ge(s["final"], i + 1)
        add_gated(nc, dve, m, m.ps[:, i, :].rearrange("p (a b) -> p a b", a=4), 4 * i, 4,
                  repeat(gate_row(m, 3, FFN, i // 2), 4), f.g.gl[:, i % 2, :].rearrange("p (a b) -> p a b", a=4))


def deep_gpsimd(nc, pool, m, s, f):
    G = nc.gpsimd
    pool.wait_ge(s["ready"], 1)

    def squares(t, c, b):
        pool.wait_ge(s["raw"], t + 1)
        G.tensor_tensor(f.sq[b], f.raw[b], f.raw[b], ALU.mult)
        for j in range(2):
            last = G.tensor_tensor(f.rot[b][:, j * INNER:(j + 1) * INNER].rearrange("p (h d) -> p h d", d=DH),
                                   f.raw[b][:, j * INNER:(j + 1) * INNER].rearrange("p (h d) -> p h d", d=DH),
                                   f.tab[:, bass.ds(c, 1), 2 * j, :].broadcast_to([P, LH, DH]), ALU.mult)
        last.then_inc(s["cosines"], 1)

    def start(rnd, dd, par):
        pool.wait_ge(s["weights"][par], 16 * dd + 16)
        pool.wait_ge(s["rotary"], 16 * rnd + 16)
        w = f.w[par]
        for j, scale in ((0, w.qs), (1, w.qs), (2, w.ks), (3, w.ks)):
            if j % 2 == 0:
                G.tensor_tensor(f.tab[:, :, j, :], f.tab[:, :, j, :], repeat(scale, BT), ALU.mult)
            else:
                for e in range(2):
                    here, there = slice(32 * e, 32 * e + 32), slice(32 - 32 * e, 64 - 32 * e)
                    G.tensor_tensor(f.tab[:, :, j, here], f.tab[:, :, j, here], repeat(scale[:, there], BT), ALU.mult)
        pool.drain()
        squares(16 * rnd, 0, 0)
        squares(16 * rnd + 1, 0, 1)

    def tile(where, t, c, b, par, ahead2, ahead1):
        if ahead2:
            pool.wait_ge(s["turned"], t + 1)
            squares(t + 2, c + 1, b)

    deep_rounds(pool, start, tile, None)


def deep_sync(nc, sp, m, s, f):
    def rotary():
        sp.dma_start(f.tab_flat, m.d["rotary"]).then_inc(s["rotary"], 16)

    def attended(rnd):
        sp.wait_ge(s["rotated"], 16 * (rnd + 1))
        sp.wait_ge(s["cosines"], 16 * (rnd + 1))
        rotary()

    rotary()
    for par in range(2):
        sp.dma_start(f.wbuf[par], m.d["deep"][par]).then_inc(s["weights"][par], 16)
    with sp.Fori(0, DEPTH // 2 - 1) as dd:
        for par in range(2):
            attended(2 * dd + par)
            sp.wait_ge(s["added"], NBLK * (2 * dd + par + 1))
            sp.dma_start(f.wbuf[par], m.d["deep"][bass.ds(2 * dd + par + 2, 1)].rearrange("a p n -> (a p) n"))\
                .then_inc(s["weights"][par], 16)
    attended(DEPTH - 2)
    sp.wait_ge(s["rotary"], 16 * DEPTH)


EXP_LN = "natural_log_exp_and_others"
DEEP_SEMS = ("rotary", "weights0", "weights1", "ready", "staged", "wide_made0", "wide_made1", "wide_freed0",
             "wide_freed1", "score_made0", "score_made1", "score_freed0", "score_freed1", "turn_made0", "turn_made1",
             "turn_freed0", "turn_freed1", "raw", "cosines", "sumsq", "rnorm", "rotated", "turned", "maxima",
             "v0_copied", "v1_copied", "normed", "shifted", "mean", "centred", "squared", "var", "rstd", "hn", "first",
             "gelu", "glu", "second", "added", "final")


def deep_setup(m):
    f = Memory()
    f.band, f.band0 = view(m.packs["const"], "const", "band"), view(m.packs["const"], "const", "band0")
    n = columns("deep")
    assert 2 * n <= DEEP_AT
    f.wbuf = [m.arena[:, par * n:(par + 1) * n] for par in range(2)]
    f.w = []
    for buf in f.wbuf:
        w = Memory()
        w.wqkv, w.w1, w.b1, w.b2, w.qs, w.ks, w.lng, w.lnb = (
            view(buf, "deep", name) for name in ("wqkv", "w1", "b1", "b2", "qs", "ks", "lng", "lnb"))
        w.wo = view(buf, "deep", "wo").rearrange("p (a b) -> p a b", a=QB)
        w.w2 = view(buf, "deep", "w2").rearrange("p (a b) -> p a b", a=3)
        f.w.append(w)
    old = Carver(m.packs["tern"])
    f.xa, f.xb = (old.take(BATCH * (FRONT + SEQ)).rearrange("p (b t) -> p b t", b=BATCH) for _ in range(2))
    f.oT = old.take(INNER).rearrange("p (a b) -> p a b", b=P)
    f.o = m.packs["l1"][:, 0:INNER]
    f.qT = m.packs["mole"][:, 0:INNER].rearrange("p (a b) -> p a b", b=P)
    a = Carver(m.arena, DEEP_AT)
    f.raw = [m.hT[:, :], a.take(2 * INNER)]
    f.rot = [a.take(2 * INNER) for _ in range(2)]
    f.sq = [a.take(2 * INNER) for _ in range(2)]
    f.pT = a.take(LH * P).rearrange("p (a b) -> p a b", b=P)
    f.v = a.take(2 * INNER).rearrange("p (a b) -> p a b", a=2)
    f.prob = a.take(LH * SPAN).rearrange("p (a b) -> p a b", b=SPAN)
    f.kT = [a.take(QB * KEYS).rearrange("p (a b) -> p a b", b=KEYS) for _ in range(2)]
    f.xs = [a.take(KEYS) for _ in range(2)]
    f.tab_flat = a.take(BT * 4 * DH)
    f.tab = f.tab_flat.rearrange("p (c j d) -> p c j d", c=BT, j=4)
    f.bands = a.bf16(BT * SPAN).rearrange("p (c k) -> p c k", k=SPAN)
    f.identb = a.bf16(P)
    f.mean = a.take(P)
    f.eps, f.spare = a.take(1), a.take(1)
    f.ss = [a.take(2 * LH) for _ in range(2)]
    f.nmax = [a.take(LH) for _ in range(2)]
    f.rsum = [a.take(LH) for _ in range(2)]
    g = Memory()
    b = Carver(m.arena, DEEP_AT)
    four = lambda: b.take(TOK).rearrange("p (a b) -> p a b", b=BLK)
    g.xc, g.sq = four(), four()
    g.gl = b.take(2 * BLK).rearrange("p (a b) -> p a b", b=BLK)
    g.u = [b.take(3 * BLK).rearrange("p (a b) -> p a b", b=BLK) for _ in range(2)]
    f.g = g
    return f


def build(nc, d, out):
    with ExitStack() as ctx:
        def sb(name, shape, dt=F32):
            return ctx.enter_context(nc.sbuf_tensor(name, shape, dt))

        def sem(name):
            return ctx.enter_context(nc.semaphore(name))

        m = Memory()
        m.d = d
        m.ps = ctx.enter_context(nc.psum_tensor("ps", [P, 8, BLK], F32))
        m.x = sb("x", [P, TILES, P])
        m.hT = sb("hT", [P, TOK])
        m.masks = sb("masks", [P, LEVELS + 1, P], I32)
        m.packs = {k: sb("pack_" + k, [P, columns(k)]) for k in ("const", "l0", "tern", "l1", "mole", "l2", "l3")}
        m.arena = sb("arena", [P, ARENA])
        m.sc = sb("sc", [P, 2 * LAYERS])
        m.modc = sb("modc", [P, 8 * LAYERS])
        m.grow = sb("grow", [P, LAYERS, 4 * P])
        m.stats = sb("stats", [P, TILES, 6])
        m.mv = sb("mv", [P, TILES, 2])
        m.rstd = sb("rstd", [P, TILES])
        m.nhalf = sb("nhalf", [P, 64])
        m.ident = view(m.packs["const"], "const", "ident")
        m.cT = view(m.packs["const"], "const", "cT")
        first = Carver(m.arena)
        wmod = first.take(columns("mod"))
        m.wmod = wmod.rearrange("p (l a b) -> p l a b", l=LAYERS, a=6)
        m.scwide = first.take(2 * LAYERS * P).rearrange("p (a b) -> p a b", b=P)
        m.gtmp = first.take(LAYERS * BLK).rearrange("p (a b) -> p a b", b=BLK)
        m.xn = m.arena[:, ARENA - TOK:ARENA].rearrange("p (a b) -> p a b", b=P)

        m.loaded = {k: sem("loaded_" + k) for k in list(m.packs) + ["mod", "x", "masks"]}
        m.stage_done = sem("stage_done")
        m.out_written = sem("out_written")


        def sems(stage, names):
            s = {n: sem(f"{stage}_{n}") for n in names}
            for n in [n[:-1] for n in names if n.endswith("0")]:
                s[n] = [s[f"{n}{i}"] for i in range(4) if f"{n}{i}" in names]
            return s

        mod, ln, tern = sems("mod", MOD_SEMS), sems("ln", LN_SEMS), sems("tern", TERN_SEMS)
        attn_s = [sems("gla0", GLA_SEMS), sems("gla1", GLA_SEMS), sems("ssm", SSM_SEMS), sems("mha", MHA_SEMS)]
        attn_m = [gla_setup(m, 0), gla_setup(m, 1), ssm_setup(m), mha_setup(m)]
        ffn_s = [tern, sems("mole", MOLE_SEMS), tern, sems("deep", DEEP_SEMS)]
        ffn_m = [tern_setup(m, 0), mole_setup(m), tern_setup(m, 2), deep_setup(m)]

        block = ctx.enter_context(nc.Block())

        @block.sync
        def _(sp):
            sp.dma_start(m.packs["const"][:, :], d["const"]).then_inc(m.loaded["const"], 16)
            sp.dma_start(wmod, d["mod"]).then_inc(m.loaded["mod"], 16)
            sp.dma_start(m.x[:, :, :], d["x"].rearrange("b (t p) f -> p (b t) f", p=P)).then_inc(m.loaded["x"], 16)
            sp.dma_start(m.masks[:, :, :], d["masks"].rearrange("p (a b) -> p a b", b=P)).then_inc(m.loaded["masks"], 16)
            for k in ("l0", "tern", "l1", "mole", "l2", "l3"):
                sp.dma_start(m.packs[k][:, :], d[k]).then_inc(m.loaded[k], 16)
            sp.wait_ge(m.stage_done, ENGINES * 5)
            sp.dma_start(m.packs["tern"][:, :], d["tern2"]).then_inc(m.loaded["tern"], 16)
            sp.wait_ge(m.stage_done, ENGINES * 14)
            mha_sync(nc, sp, m, attn_s[3], attn_m[3])
            sp.wait_ge(m.stage_done, ENGINES * 16)
            deep_sync(nc, sp, m, ffn_s[3], ffn_m[3])
            sp.wait_ge(m.stage_done, ENGINES * 17)
            sp.dma_start(out.rearrange("b (t p) f -> p (b t) f", p=P), m.x[:, :, :]).then_inc(m.out_written, 16)
            sp.wait_ge(m.out_written, 16)
            for name, loaded in m.loaded.items():
                sp.wait_ge(loaded, 32 if name == "tern" else 16)

        @block.tensor
        def _(pe):
            mod_tensor(nc, pe, m, mod)
            finish_stage(pe, m, 0)
            for l in range(LAYERS):
                ln_tensor(nc, pe, m, ln, 2 * l)
                finish_stage(pe, m, 1 + 4 * l)
                (gla_tensor, gla_tensor, ssm_tensor, mha_tensor)[l](nc, pe, m, attn_s[l], attn_m[l])
                finish_stage(pe, m, 2 + 4 * l)
                ln_tensor(nc, pe, m, ln, 2 * l + 1)
                finish_stage(pe, m, 3 + 4 * l)
                (tern_tensor, mole_tensor, tern_tensor, deep_tensor)[l](nc, pe, m, ffn_s[l], ffn_m[l])
                finish_stage(pe, m, 4 + 4 * l)

        @block.scalar
        def _(act):
            mod_scalar(nc, act, m, mod)
            finish_stage(act, m, 0)
            for l in range(LAYERS):
                ln_scalar(nc, act, m, ln, 2 * l, l, ATTN)
                finish_stage(act, m, 1 + 4 * l)
                (gla_scalar, gla_scalar, ssm_scalar, mha_scalar)[l](nc, act, m, attn_s[l], attn_m[l])
                finish_stage(act, m, 2 + 4 * l)
                ln_scalar(nc, act, m, ln, 2 * l + 1, l, FFN)
                finish_stage(act, m, 3 + 4 * l)
                (tern_scalar, mole_scalar, tern_scalar, deep_scalar)[l](nc, act, m, ffn_s[l], ffn_m[l])
                finish_stage(act, m, 4 + 4 * l)

        @block.vector
        def _(dve):
            dve.wait_ge(m.loaded["x"], 16)
            dve.wait_ge(m.loaded["masks"], 16)
            mod_vector(nc, dve, m, mod)
            finish_stage(dve, m, 0)
            for l in range(LAYERS):
                ln_vector(nc, dve, m, ln, 2 * l)
                finish_stage(dve, m, 1 + 4 * l)
                (gla_vector, gla_vector, ssm_vector, mha_vector)[l](nc, dve, m, attn_s[l], attn_m[l])
                finish_stage(dve, m, 2 + 4 * l)
                ln_vector(nc, dve, m, ln, 2 * l + 1)
                finish_stage(dve, m, 3 + 4 * l)
                (tern_vector, mole_vector, tern_vector, deep_vector)[l](nc, dve, m, ffn_s[l], ffn_m[l])
                finish_stage(dve, m, 4 + 4 * l)

        @block.gpsimd
        def _(pool):
            nc.gpsimd.memset(m.nhalf[:, :], -0.5)
            pool.drain()
            finish_stage(pool, m, 0)
            for l in range(LAYERS):
                ln_gpsimd(nc, pool, m, ln, 2 * l)
                finish_stage(pool, m, 1 + 4 * l)
                if l in (0, 1):
                    gla_gpsimd(nc, pool, m, attn_s[l], attn_m[l])
                if l == 3:
                    mha_gpsimd(nc, pool, m, attn_s[l], attn_m[l])
                finish_stage(pool, m, 2 + 4 * l)
                ln_gpsimd(nc, pool, m, ln, 2 * l + 1)
                finish_stage(pool, m, 3 + 4 * l)
                if l == 3:
                    deep_gpsimd(nc, pool, m, ffn_s[l], ffn_m[l])
                finish_stage(pool, m, 4 + 4 * l)


def pad(a, rows=P):
    a = a.reshape(a.shape[0], -1)
    out = np.zeros((rows, a.shape[1]), a.dtype)
    out[:a.shape[0]] = a
    return out


def by_rows(a):
    k = -(-a.shape[0] // P)
    a = pad(a, k * P)
    return a.reshape(k, P, -1).transpose(1, 0, 2).reshape(P, -1)


def col(v):
    return by_rows(v.reshape(-1, 1))


def rows_of(v):
    return np.broadcast_to(v.reshape(1, -1), (P, v.size))


def pack(name, parts):
    assert set(parts) == {n for n, _ in PACKS[name]}, name
    out = [pad(np.asarray(parts[n])) for n, _ in PACKS[name]]
    assert [a.shape[1] for a in out] == [c for _, c in PACKS[name]], [(n, a.shape) for (n, _), a in zip(PACKS[name], out)]
    return np.ascontiguousarray(np.concatenate(out, axis=1))


def level_masks():
    j, i = np.meshgrid(np.arange(P), np.arange(P), indexing="ij")
    out = [((i >> lev) == (j >> lev) + 1) & ((j >> lev) % 2 == 0) for lev in range(LEVELS)] + [i == j]
    return np.ascontiguousarray(np.stack(out, axis=1).astype(np.int32).reshape(P, -1))


def rotary_tables():
    half = np.arange(0, 64, 2, dtype=np.float32)
    inv_freq = (np.float32(1.0) / np.float32(10000.0) ** (half / np.float32(64))).astype(np.float32)
    t = np.arange(SEQ, dtype=np.float32)
    freqs = np.concatenate([t[:, None] * inv_freq[None, :]] * 2, -1).astype(np.float32)
    base = ((half + np.float32(0.4 * 64)) / np.float32(1.4 * 64)).astype(np.float32)
    power = ((t - SEQ // 2) / np.float32(16)).astype(np.float32)
    scale = np.power(base[None, :], power[:, None]).astype(np.float32)
    scale = np.concatenate([scale, scale], -1)
    sign = np.concatenate([-np.ones(32), np.ones(32)]).astype(np.float32)
    cos, sin = np.cos(freqs).astype(np.float32), np.sin(freqs).astype(np.float32) * sign
    inv = np.float32(1.0) / scale
    tables = np.stack([8192 * cos * scale, 8192 * sin * scale, 1024 * cos * inv, 1024 * sin * inv], axis=1)
    return np.ascontiguousarray(tables.reshape(BT, P, 4, 64).transpose(1, 0, 2, 3).reshape(P, -1).astype(np.float32))


def band_masks():
    i, j = np.arange(P)[:, None], np.arange(96)[None, :] - 32
    seen = (j <= i % 64) & (j >= i % 64 - 32)
    first = seen & ((j >= 0) | (i >= 64))
    big = np.float32(-1e30)
    return np.where(seen, np.float32(0), big), np.where(first, np.float32(0), big)


def kernel(**inputs):
    import concourse.bacc as _bacc
    from concourse.bass_utils import run_bass_kernel_spmd as _run

    i = {k: np.asarray(v) for k, v in inputs.items()}
    band, band0 = band_masks()
    arrays = {
        "const": pack("const", {"ident": np.eye(P, dtype=np.float32), "band": band, "band0": band0,
                                "cT": np.concatenate([i[f"L{l}_c"].T for l in range(LAYERS)], axis=1),
                                "sel": np.tile(np.eye(32, 9, dtype=np.float32), (4, 1))}),
        "masks": level_masks(),
        "rotary": rotary_tables(),
        "mod": pack("mod", {"wmod": np.concatenate([i[f"L{l}_wmod"] for l in range(LAYERS)], axis=1)}),
        "x": i["L0_attn_x"],
        "l0": pack("l0", {"wq": i["L0_attn_Wq"], "wk": i["L0_attn_Wk"], "wv": i["L0_attn_Wv"],
                          "g1": i["L0_attn_G1"], "g2": i["L0_attn_G2"], "wo": i["L0_attn_Wo"],
                          "delta": col(i["L0_attn_delta"]), "nw": col(i["L0_attn_norm_w"])}),
        "l1": pack("l1", {"wq": i["L1_attn_Wq"], "wk": i["L1_attn_Wk"], "wv": i["L1_attn_Wv"],
                          "wg": i["L1_attn_Wg"], "gk1": i["L1_attn_gk_w1"], "gk2": i["L1_attn_gk_w2"],
                          "b2": col(i["L1_attn_gk_b2"]),
                          "nw": col(np.concatenate([i["L1_attn_g_norm_w"]] * 2)), "wo": by_rows(i["L1_attn_Wo"])}),
        "mole": pack("mole", {
            "w1": i["L1_ffn_W1"], "w2": by_rows(i["L1_ffn_W2"]),
            "ar1": np.concatenate([i["L1_ffn_A1"].transpose(1, 0, 2).reshape(P, 24), i["L1_ffn_R1"]], axis=1),
            "b1": np.concatenate([i["L1_ffn_B1"].reshape(24, HID), i["L1_ffn_b1"].reshape(1, -1)]),
            "ar2": by_rows(np.concatenate([i["L1_ffn_A2"].transpose(1, 0, 2).reshape(HID, 24), i["L1_ffn_R2"]], axis=1)),
            "b2": np.concatenate([i["L1_ffn_B2"].reshape(24, P), i["L1_ffn_b2"].reshape(1, -1)])}),
        "l2": pack("l2", {"win": i["L2_attn_W_in"].T,
                          "cw": by_rows(i["L2_attn_conv_w"][:, 0, :]), "cb": col(i["L2_attn_conv_b"]),
                          "alog": by_rows(i["L2_attn_A_log"]), "d": col(i["L2_attn_D"]),
                          "wout": by_rows(i["L2_attn_W_out"].T)}),
        "l3": pack("l3", {"wq": i["L3_attn_W_query"].transpose(1, 0, 2).reshape(P, P),
                          "wk": i["L3_attn_W_key"].transpose(1, 0, 2).reshape(P, P),
                          "wv": i["L3_attn_W_val"].transpose(1, 0, 2).reshape(P, P),
                          "wo": i["L3_attn_W_out"].reshape(P, P)}),
    }
    for l, name in ((0, "tern"), (2, "tern2")):
        f = lambda k: i[f"L{l}_ffn_{k}"]
        arrays[name] = pack("tern", {
            "w1": f("w1_w").T, "w2": f("w2_w").T, "h1": by_rows(f("h1_w").T), "h2": by_rows(f("h2_w").T),
            "w3": by_rows(f("w3_w").T), "s1": col(f("w1_s")), "s2": col(f("w2_s")), "sh1": col(f("h1_s")),
            "sh2": col(f("h2_s")), "s3": rows_of(f("w3_s"))})
    g = lambda k: i[f"L3_ffn_{k}"]

    def halves(b):
        return np.concatenate([col(b[:341]), col(b[341:])], axis=1)

    arrays["deep"] = np.stack([pack("deep", {
        "wqkv": g("Wqkv")[r], "wo": by_rows(g("Wo")[r]), "w1": g("W1")[r], "w2": by_rows(g("W2")[r]),
        "b1": halves(g("b1")[r]), "b2": col(g("b2")[r]), "qs": rows_of(g("q_scale")[r]),
        "ks": rows_of(g("k_scale")[r]), "lng": col(g("ln_g")[r]), "lnb": col(g("ln_b")[r])}) for r in range(DEPTH)])

    nc = _bacc.Bacc("TRN2", target_bir_lowering=False, num_devices=1)
    feeds, drams = {}, {}
    for name, a in arrays.items():
        feeds["in_" + name] = np.ascontiguousarray(a)
        drams[name] = nc.dram_tensor("in_" + name, a.shape, mybir.dt.from_np(a.dtype), kind="ExternalInput").ap()
    out = nc.dram_tensor("out", (BATCH, SEQ, P), F32, kind="ExternalOutput").ap()
    drams["nc"] = nc
    build(nc, drams, out)
    return _run(nc, [feeds], core_ids=[0]).results[0]["out"]
```

```python
from contextlib import ExitStack

import numpy as np
import concourse.bass as bass
from concourse import mybir

F32 = mybir.dt.float32
BF16 = mybir.dt.bfloat16
ALU = mybir.AluOpType
ACT = mybir.ActivationFunctionType
AX = mybir.AxisListType.X

P = 128
BATCH = 2
SEQ = 1024
TOK = BATCH * SEQ
TILES = TOK // P
BT = SEQ // P
BLK = 512
NBLK = TOK // BLK
HID = 512
HB = HID // P
LEVELS = 7
DEPTH = 6
EPS = 1e-5
ARENA = 32700
LAYERS = 4
DEEP_AT = 10852
ENGINES = 4

ATTN, FFN = 0, 1


PACKS = {
    "const": [("ident", P), ("band", 96), ("band0", 96), ("cT", 2 * LAYERS)],
    "mod": [("wmod", LAYERS * 6 * P)],
    "l0": [("wq", P), ("wk", P), ("wv", P), ("g1", 64), ("g2", P), ("wo", P), ("delta", 1), ("nw", 1)],
    "tern": [("w1", HID), ("w2", HID), ("h1", HB * HID), ("h2", HB * HID), ("w3", HB * P),
             ("s1", HB), ("s2", HB), ("sh1", HB), ("sh2", HB), ("s3", P)],
    "l1": [("wq", P), ("wk", P), ("wv", 256), ("wg", 256), ("gk1", 16), ("gk2", P), ("b2", 1), ("nw", 1),
           ("wo", 2 * P)],
    "mole": [("w1", HID), ("ar1", 27), ("b1", HID), ("w2", HB * P), ("ar2", HB * 27), ("b2", P)],
    "l2": [("win", 512), ("cw", 8), ("cb", 2), ("alog", 32), ("d", 2), ("wout", 2 * P)],
    "l3": [("wq", P), ("wk", P), ("wv", P), ("wo", P)],
    "deep": [("wqkv", 3072), ("wo", 8 * P), ("w1", 682), ("w2", 3 * P), ("b1", 6), ("b2", 1),
             ("qs", 64), ("ks", 64), ("lng", 1), ("lnb", 1)],
}


def columns(pack):
    return sum(n for _, n in PACKS[pack])


def view(tensor, pack, name, rows=P):
    at = 0
    for item, n in PACKS[pack]:
        if item == name:
            return tensor[0:rows, at:at + n]
        at += n
    raise KeyError(name)


class Memory:
    pass


class Carver:

    def __init__(self, arena, at=0):
        self.arena, self.at = arena, at

    def take(self, n):
        got = self.arena[:, self.at:self.at + n]
        self.at += n
        assert self.at <= ARENA, self.at
        return got

    def bf16(self, n):
        return self.take(n // 2).bitcast(BF16)


def spread(ap, n):
    return ap.rearrange("p (a o) -> p a o", o=1).broadcast_to([ap.shape[0], ap.shape[1], n])


def repeat(ap, n):
    return ap.rearrange("p (o a) -> p o a", o=1).broadcast_to([ap.shape[0], n, ap.shape[1]])


def finish_stage(eng, m, stage):
    eng.drain().then_inc(m.stage_done, 1)
    eng.wait_ge(m.stage_done, ENGINES * (stage + 1))


COLS = (0, 1, 3, 4)
GATES = (2, 5)


def mod_scalar(nc, act, m, s):
    act.wait_ge(m.loaded["const"], 16)
    nc.scalar.activation(m.sc[:, :], m.cT, ACT.Silu).then_inc(s["silu"], 1)


def mod_tensor(nc, pe, m, s):
    pe.wait_ge(s["silu"], 1)
    pe.wait_ge(m.loaded["mod"], 16)
    for l in range(LAYERS):
        for j, part in enumerate(COLS):
            at = (l * 4 + j) * 2
            last = nc.tensor.matmul(m.ps[:, 0, at:at + 2], m.wmod[:, l, part, :], m.sc[:, 2 * l:2 * l + 2],
                                    start=True, stop=True)
    last.then_inc(s["cols"], 1)
    pe.wait_ge(s["wide"], 1)
    for l in range(LAYERS):
        for g, part in enumerate(GATES):
            for b in range(BATCH):
                last = nc.tensor.matmul(m.ps[:, 1 + l, (g * 2 + b) * P:(g * 2 + b + 1) * P],
                                        m.scwide[:, 2 * l + b, :], m.wmod[:, l, part, :], start=True, stop=True)
        last.then_inc(s["rows"], 1)


def mod_vector(nc, dve, m, s):
    dve.wait_ge(s["silu"], 1)
    nc.vector.tensor_copy(m.scwide[:, :, :], spread(m.sc[:, :], P)).then_inc(s["wide"], 1)
    dve.wait_ge(s["cols"], 1)
    nc.vector.tensor_copy(m.modc[:, :], m.ps[:, 0, 0:LAYERS * 8])
    dve.drain()
    scales = m.modc[:, :].rearrange("p (a k b) -> p a k b", k=2, b=2)[:, :, 1, :]
    nc.vector.tensor_scalar(scales, scales, 1.0, None, ALU.add)
    for l in range(LAYERS):
        dve.wait_ge(s["rows"], l + 1)
        g = m.ps[:, 1 + l, :]
        nc.vector.tensor_scalar(m.gtmp[:, l, :], g, 0.0, 2.0, ALU.is_ge, ALU.mult)
        nc.vector.tensor_scalar(m.grow[:, l, :], g, -1.0, 0.25, ALU.mult, ALU.max)
        dve.drain()
        nc.vector.tensor_tensor(m.grow[:, l, :], g, m.grow[:, l, :], ALU.max)
        dve.drain()
        nc.vector.scalar_tensor_tensor(m.grow[:, l, :], m.gtmp[:, l, :], -1.0, m.grow[:, l, :], ALU.add, ALU.mult)


def mod_col(m, l, sub, which, b):
    at = (l * 4 + 2 * sub + which) * 2 + b
    return m.modc[:, at:at + 1]


def gate_row(m, l, sub, b):
    at = (sub * 2 + b) * P
    return m.grow[:, l, at:at + P]


def ln_vector(nc, dve, m, s, k):
    for g in range(NBLK):
        tiles = range(4 * g, 4 * g + 4)
        for t in tiles:
            nc.vector.bn_stats(m.stats[:, t, :], m.x[:, t, :])
        dve.drain()
        for t in tiles:
            last = nc.vector.bn_aggr(m.mv[:, t, :], m.stats[:, t, :])
        last.then_inc(s["stats"], 1)
    for t in range(TILES):
        if t % 4 == 0:
            dve.wait_ge(s["rstd"], NBLK * k + t // 4 + 1)
        nc.vector.tensor_scalar(m.xn[:, t, :], m.x[:, t, :], m.mv[:, t, 0:1], m.rstd[:, t:t + 1],
                                ALU.subtract, ALU.mult).then_inc(s["xn"], 1)


def ln_gpsimd(nc, pool, m, s, k):
    for g in range(NBLK):
        here = slice(4 * g, 4 * g + 4)
        pool.wait_ge(s["stats"], NBLK * k + g + 1)
        nc.gpsimd.tensor_scalar(m.rstd[:, here], m.mv[:, here, 1], EPS, None, ALU.add)
        pool.drain()
        nc.gpsimd.tensor_tensor(m.rstd[:, here], m.rstd[:, here], m.nhalf[:, 0:4], ALU.pow).then_inc(s["rstd"], 1)


def ln_tensor(nc, pe, m, s, k):
    for g in range(NBLK):
        pe.wait_ge(s["xn"], TILES * k + 4 * (g + 1))
        for t in range(4):
            last = nc.tensor.transpose(m.ps[:, g, t * P:(t + 1) * P], m.xn[:, 4 * g + t, :], m.ident)
        last.then_inc(s["turned"], 1)


def ln_scalar(nc, act, m, s, k, l, sub):
    for g in range(NBLK):
        b = g // (NBLK // BATCH)
        act.wait_ge(s["turned"], NBLK * k + g + 1)
        nc.scalar.activation(m.hT[:, g * BLK:(g + 1) * BLK], m.ps[:, g, :], ACT.Identity,
                             bias=mod_col(m, l, sub, 0, b), scale=mod_col(m, l, sub, 1, b))


MOD_SEMS = ("silu", "cols", "wide", "rows")
LN_SEMS = ("stats", "rstd", "xn", "turned")


def add_gated(nc, dve, m, ps, t0, n, row, tmp):
    nc.vector.tensor_tensor(tmp, ps, row, ALU.mult)
    dve.drain()
    return nc.vector.tensor_tensor(m.x[:, t0:t0 + n, :], m.x[:, t0:t0 + n, :], tmp, ALU.add)


def gla_jobs(g):
    jobs = [("q", n) for n in range(NBLK)] + [("k", n) for n in range(NBLK)] + [("low", n) for n in range(NBLK)]
    if g.layer == 1:
        jobs += [("z", n) for n in range(NBLK)]
    per = BLK // g.vd
    jobs += [("v", n) for n in range(TILES // per)] + [("gate", n) for n in range(TILES // per)]
    return jobs


SPAN4 = BLK
CHUNKS = SPAN4 // P
FINE = 5
BLOCK = 32


def level_blocks(lev):
    if lev < FINE or lev == LEVELS:
        slot = min(lev, FINE)
        return [(k, k, BLOCK, slot * BLOCK) for k in range(0, P, BLOCK)]
    at = (FINE + 1) * BLOCK
    if lev == FINE:
        return [(0, BLOCK, BLOCK, at), (2 * BLOCK, 3 * BLOCK, BLOCK, at)]
    return [(0, 2 * BLOCK, 2 * BLOCK, at + BLOCK)]


def gla_tensor(nc, pe, m, s, g):
    T = nc.tensor
    per = BLK // g.vd
    jobs = gla_jobs(g)
    pe.wait_ge(m.loaded[g.pack], 16)
    for n, (kind, i) in enumerate(jobs):
        if n >= 8:
            pe.wait_ge(s["proj_read"], n - 7)
        bank = m.ps[:, n % 8, :]
        cols = slice(i * BLK, (i + 1) * BLK)
        if kind in ("q", "k"):
            last = T.matmul(bank, g.w[kind], m.hT[:, cols], start=True, stop=True)
        elif kind == "low":
            last = T.matmul(m.ps[0:g.low, n % 8, :], g.w["low"], m.hT[:, cols], start=True, stop=True)
        elif kind == "z":
            pe.wait_ge(s["proj_read"], jobs.index(("low", i)) + 1)
            last = T.matmul(bank, g.w["z"], g.lowT[:, cols], start=True, stop=True)
        else:
            if kind == "gate" and g.layer == 0:
                pe.wait_ge(s["proj_read"], jobs.index(("low", NBLK - 1)) + 1)
            for j in range(per):
                t = i * per + j
                src = g.lowT if (kind == "gate" and g.layer == 0) else m.hT
                last = T.matmul(m.ps[:, n % 8, j * g.vd:(j + 1) * g.vd], src[:, t * P:(t + 1) * P], g.w[kind],
                                start=True, stop=True)
        last.then_inc(s["proj"], 1)

    pairs = g.heads // 2
    pe.wait_ge(s["proj_read"], len(jobs))

    def scores(n, pair):
        quarter, c = divmod(n, CHUNKS)
        cols = slice(c * P, (c + 1) * P)
        job = n * pairs + pair
        if job >= 3:
            pe.wait_ge(s["picked"], job - 2)
        for lev in range(LEVELS + 1):
            if c == 0 and pair == 0 and lev < LEVELS:
                pe.wait_ge(s["level"], quarter * LEVELS + lev + 1)
            for e in range(2):
                h = 2 * pair + e
                rows = slice(h * g.dk, (h + 1) * g.dk)
                if lev < LEVELS:
                    left = right = g.lev[rows, quarter % 2, lev, cols]
                else:
                    left, right = g.kT[rows, n * P:(n + 1) * P], g.qT[rows, n * P:(n + 1) * P]
                bank = 2 * (job % 3) + e
                for key, query, size, at in level_blocks(lev):
                    last = T.matmul(m.ps[key:key + size, bank, at:at + size], left[:, key:key + size],
                                    right[:, query:query + size], start=True, stop=True)
        last.then_inc(s["scored"], 1)

    for n in range(TILES):
        b, c = divmod(n, BT)
        quarter, c4 = divmod(n, CHUNKS)
        cols = slice(c4 * P, (c4 + 1) * P)
        if c4 == 0:
            pe.wait_ge(s["scaled"], quarter + 1)
        if n == 0:
            for pair in range(pairs):
                scores(n, pair)
        if c < BT - 1:
            u = b * (BT - 1) + c
            pe.wait_ge(s["state"], u)
            T.transpose(m.ps[:, 7, 0:P], g.ks[:, quarter % 2, cols], m.ident).then_inc(s["kturned"], 1)
        if n + 1 < TILES:
            scores(n + 1, 0)
        if c < BT - 1:
            pe.wait_ge(s["kcopied"], u + 1)
            T.matmul(m.ps[:, 7, 256:256 + g.vd], g.ksT[:, :], g.v[:, n, :], start=True, stop=True)\
                .then_inc(s["update"], 1)
        if n + 1 < TILES:
            for pair in range(1, pairs):
                scores(n + 1, pair)
        pe.wait_ge(s["picked"], (n + 1) * pairs)
        if n >= 1:
            pe.wait_ge(s["o_read"], n)
        if c > 0:
            pe.wait_ge(s["state"], b * (BT - 1) + c)
            T.matmul(m.ps[:, 6, 0:g.vd], g.qs[:, quarter % 2, cols], g.state[:, n % 2, :], start=True, stop=False,
                     skip_group_check=True)
        for h in range(g.heads):
            out = m.ps[:, 6, h * g.dv:(h + 1) * g.dv]
            last = T.matmul(out, g.at[:, n % 2, h, :], g.v[:, n, h * g.dv:(h + 1) * g.dv], start=c == 0, stop=True,
                            skip_group_check=True)
        last.then_inc(s["o_made"], 1)

    blocks = g.vd // P
    n_turn = blocks * NBLK
    pe.wait_ge(s["o_read"], TILES)
    pe.wait_ge(s["o_norm"], 1)
    for n in range(n_turn):
        k, i = divmod(n, NBLK)
        if n >= 4:
            pe.wait_ge(s["oT"], n - 3)
        for t in range(4):
            last = T.transpose(m.ps[:, n % 4, t * P:(t + 1) * P], g.o[:, 4 * i + t, k * P:(k + 1) * P], m.ident)
        last.then_inc(s["o_turned"], 1)
    pe.wait_ge(s["oT"], n_turn)
    for i in range(NBLK):
        for t in range(4):
            for k in range(blocks):
                last = T.matmul(m.ps[:, 4 + i, t * P:(t + 1) * P], g.oT[:, k, (4 * i + t) * P:(4 * i + t + 1) * P],
                                g.wo[:, k, :], start=k == 0, stop=k == blocks - 1)
        last.then_inc(s["y"], 1)


def gla_operand(g, quarter, j):
    return (g.es, g.ks)[j][:, quarter % 2, :] if j < 2 else g.lev[:, quarter % 2, j - 2, :]


def gla_scalar(nc, act, m, s, g):
    A = nc.scalar.activation
    per = BLK // g.vd
    for n, (kind, i) in enumerate(gla_jobs(g)):
        act.wait_ge(s["proj"], n + 1)
        bank = m.ps[:, n % 8, :]
        cols = slice(i * BLK, (i + 1) * BLK)
        if kind == "q":
            done = (A(g.qT[:, cols], bank, ACT.Silu) if g.layer == 0 else
                    A(g.qT[:, cols], bank, ACT.Copy, scale=g.qscale))
        elif kind == "k":
            done = (A(g.z[:, cols], bank, ACT.Identity, bias=g.zbias) if g.layer == 0 else
                    A(g.kT[:, cols], bank, ACT.Copy))
        elif kind == "low":
            done = A(g.lowT[:, cols], m.ps[0:g.low, n % 8, :], ACT.Copy)
        elif kind == "z":
            done = A(g.z[:, cols], bank, ACT.Identity, bias=g.zbias)
        elif kind == "v":
            done = A(g.v[:, i * per:(i + 1) * per, :], bank.rearrange("p (a b) -> p a b", a=per), ACT.Copy)
        else:
            done = A(g.gate[:, i * per:(i + 1) * per, :], bank.rearrange("p (a b) -> p a b", a=per),
                     ACT.Sigmoid if g.layer == 0 else ACT.Silu)
        done.then_inc(s["proj_read"], 1)
    act.drain()
    if g.layer == 0:
        A(g.kT[:, :], g.z[:, :], ACT.Sigmoid, scale=-1.0)
    A(g.soft[:, :], g.z[:, :], ACT.Abs)
    act.drain()
    A(g.soft[:, :], g.soft[:, :], ACT.Exp, scale=-1.0)
    act.drain()
    A(g.soft[:, :], g.soft[:, :], ACT.Ln, bias=1.0).then_inc(s["soft"], 1)

    def decays(quarter, which):
        for j in which:
            act.wait_ge(s["diff"], quarter * (LEVELS + 2) + j + 1)
            x = gla_operand(g, quarter, j)
            A(x, x, ACT.Exp, scale=g.decay_scale).then_inc(s["exped"], 1)

    decays(0, range(LEVELS + 2))
    for n in range(TILES):
        b, c = divmod(n, BT)
        if c < BT - 1:
            u = b * (BT - 1) + c
            act.wait_ge(s["kturned"], u + 1)
            A(g.ksT[:, :], m.ps[:, 7, 0:P], ACT.Copy).then_inc(s["kcopied"], 1)
        act.wait_ge(s["o_made"], n + 1)
        A(g.o[:, n, :], m.ps[:, 6, 0:g.vd], ACT.Copy).then_inc(s["o_read"], 1)
        quarter, c4 = divmod(n, CHUNKS)
        if quarter + 1 < TILES // CHUNKS and c4 < 2:
            decays(quarter + 1, (range(0, 5), range(5, LEVELS + 2))[c4])
    for n in range(g.vd // P * NBLK):
        k, i = divmod(n, NBLK)
        act.wait_ge(s["o_turned"], n + 1)
        A(g.oT[:, k, i * BLK:(i + 1) * BLK], m.ps[:, n % 4, :], ACT.Identity,
          scale=g.nw).then_inc(s["oT"], 1)


def gla_vector(nc, dve, m, s, g):
    V = nc.vector
    V.memset(g.keep[:, :], 1.0)
    V.memset(g.at[:, :, :, :], 0.0)
    V.memset(g.state[:, :, :], 0.0)
    dve.drain()
    V.memset(g.keep[:, :].rearrange("p (a b) -> p a b", b=P)[:, :, 0:1], 0.0)
    dve.wait_ge(s["soft"], 1)
    V.scalar_tensor_tensor(g.soft[:, :], g.z[:, :], 0.0, g.soft[:, :], ALU.min, ALU.subtract)
    dve.drain()
    V.tensor_tensor_scan(g.c[:, :], g.keep[:, :], g.soft[:, :], 0.0, ALU.mult, ALU.add)
    dve.drain()
    pairs = g.heads // 2

    def halves(x, lev):
        return x.rearrange("p (a e b) -> p a e b", e=2, b=1 << lev)

    def differences(quarter, which):
        here = slice(quarter * SPAN4, (quarter + 1) * SPAN4)
        if 0 in which and quarter >= 2:
            dve.wait_ge(s["o_made"], CHUNKS * (quarter - 1))
        for j in which:
            to = gla_operand(g, quarter, j)
            if j == 0:
                last = V.tensor_copy(to, g.c[:, here])
            elif j == 1:
                c3 = g.c[:, here].rearrange("p (a b) -> p a b", b=P)
                last = V.tensor_tensor(to.rearrange("p (a b) -> p a b", b=P),
                                       c3[:, :, P - 1:P].broadcast_to([P, CHUNKS, P]), c3, ALU.subtract)
            else:
                c4, l4 = halves(g.c[:, here], j - 2), halves(to, j - 2)
                w = 1 << (j - 2)
                mid = c4[:, :, 0, w - 1:w].broadcast_to([P, SPAN4 // (2 * w), w])
                V.tensor_tensor(l4[:, :, 0, :], mid, c4[:, :, 0, :], ALU.subtract)
                last = V.tensor_tensor(l4[:, :, 1, :], c4[:, :, 1, :], mid, ALU.subtract)
            last.then_inc(s["diff"], 1)

    def scaled(quarter, which):
        here = slice(quarter * SPAN4, (quarter + 1) * SPAN4)
        for j in which:
            dve.wait_ge(s["exped"], quarter * (LEVELS + 2) + j + 1)
            x = gla_operand(g, quarter, j)
            if j == 0:
                V.tensor_tensor(g.qs[:, quarter % 2, :], x, g.qT[:, here], ALU.mult)
            elif j == 1:
                V.tensor_tensor(x, x, g.kT[:, here], ALU.mult).then_inc(s["scaled"], 1)
            else:
                l4, k4, q4 = (halves(y, j - 2) for y in (x, g.kT[:, here], g.qT[:, here]))
                V.tensor_tensor(l4[:, :, 0, :], l4[:, :, 0, :], k4[:, :, 0, :], ALU.mult)
                V.tensor_tensor(l4[:, :, 1, :], l4[:, :, 1, :], q4[:, :, 1, :], ALU.mult).then_inc(s["level"], 1)

    differences(0, range(LEVELS + 2))
    scaled(0, range(LEVELS + 2))
    for n in range(TILES):
        b, c = divmod(n, BT)
        quarter, c4 = divmod(n, CHUNKS)
        if n >= 2:
            dve.wait_ge(s["o_made"], n - 1)
        for pair in range(pairs):
            job = n * pairs + pair
            dve.wait_ge(s["scored"], job + 1)
            bank = 2 * (job % 3)
            heads = slice(2 * pair, 2 * pair + 2)
            fine = (FINE + 1) * BLOCK
            V.tensor_tensor(g.fine[:, :, :], m.ps[:, bank:bank + 2, 0:fine], repeat(m.masks[:, :], 2), ALU.mult)
            dve.drain()
            V.tensor_reduce(g.block[:, :, :], g.fine[:, :, :].rearrange("p h (l q) -> p h q l", q=BLOCK), AX, ALU.add)
            for lev in (FINE, FINE + 1):
                for key, query, size, at in level_blocks(lev):
                    last = V.tensor_copy(g.at[key:key + size, n % 2, heads, query:query + size],
                                         m.ps[key:key + size, bank:bank + 2, at:at + size])
            dve.drain()
            for k in range(0, P, BLOCK):
                last = V.tensor_copy(g.at[k:k + BLOCK, n % 2, heads, k:k + BLOCK], g.block[k:k + BLOCK, :, :])
            last.then_inc(s["picked"], 1)
        if c < BT - 1:
            u = b * (BT - 1) + c
            dve.wait_ge(s["update"], u + 1)
            for h in range(g.heads):
                rows = slice(h * g.dk, (h + 1) * g.dk)
                new = m.ps[rows, 7, 256 + h * g.dv:256 + (h + 1) * g.dv]
                to = g.state[rows, (n + 1) % 2, h * g.dv:(h + 1) * g.dv]
                if c == 0:
                    done = V.tensor_copy(to, new)
                else:
                    done = V.scalar_tensor_tensor(to, g.state[rows, n % 2, h * g.dv:(h + 1) * g.dv],
                                                  g.es[rows, quarter % 2, c4 * P + P - 1:c4 * P + P], new, ALU.mult, ALU.add)
            done.then_inc(s["state"], 1)
            dve.drain()
        if quarter + 1 < TILES // CHUNKS:
            if c4 == 0:
                differences(quarter + 1, range(0, 5))
            elif c4 == 1:
                differences(quarter + 1, range(5, LEVELS + 2))
                scaled(quarter + 1, range(0, 3))
            elif c4 == 2:
                scaled(quarter + 1, range(3, LEVELS + 2))
    dve.wait_ge(s["o_read"], TILES)
    o2 = g.o[:, :, :].rearrange("p a b -> p (a b)")
    g2 = g.gate[:, :, :].rearrange("p a b -> p (a b)")
    if g.layer == 0:
        V.tensor_tensor(o2, o2, g2, ALU.mult)
        dve.drain()
    V.tensor_tensor(g.sq[:, :], o2, o2, ALU.mult)
    dve.drain()
    V.tensor_reduce(g.ms[:, :], g.sq[:, :].rearrange("p (a b) -> p a b", b=g.dv), AX, ALU.add).then_inc(s["ms"], 1)
    dve.wait_ge(s["rms"], 1)
    o3 = o2.rearrange("p (a b) -> p a b", b=g.dv)
    done = V.tensor_tensor(o3, o3, spread(g.ms[:, :], g.dv), ALU.mult)
    if g.layer == 1:
        dve.drain()
        done = V.tensor_tensor(o2, o2, g2, ALU.mult)
    done.then_inc(s["o_norm"], 1)
    for i in range(NBLK):
        dve.wait_ge(s["y"], i + 1)
        b = i // (NBLK // BATCH)
        add_gated(nc, dve, m, m.ps[:, 4 + i, :].rearrange("p (a b) -> p a b", a=4), 4 * i, 4,
                  repeat(gate_row(m, g.layer, ATTN, b), 4), g.tmp[:, i % 2, :].rearrange("p (a b) -> p a b", a=4))


def gla_gpsimd(nc, pool, m, s, g):
    pool.wait_ge(s["ms"], 1)
    n = TILES * g.heads
    nc.gpsimd.tensor_scalar(g.ms[:, :], g.ms[:, :], 1.0 / g.dv, EPS, ALU.mult, ALU.add)
    pool.drain()
    nc.gpsimd.tensor_tensor(g.ms[:, :], g.ms[:, :], m.nhalf[:, 0:n], ALU.pow).then_inc(s["rms"], 1)


GLA_SEMS = ("proj", "proj_read", "soft", "diff", "exped", "scaled", "level", "scored", "picked", "kturned",
            "kcopied", "update", "state", "o_made", "o_read", "ms", "rms", "o_norm", "o_turned", "oT", "y")


def gla_setup(m, layer):
    g = Memory()
    g.layer, g.pack = layer, "l0" if layer == 0 else "l1"
    w = m.packs[g.pack]
    g.heads, g.dk, g.dv = (2, 64, 64) if layer == 0 else (4, 32, 64)
    g.vd = g.heads * g.dv
    g.low = 64 if layer == 0 else 16
    g.qscale = float(g.dk) ** -0.5
    g.decay_scale = 1.0 if layer == 0 else 1.0 / 16.0
    v = lambda name, rows=P: view(w, g.pack, name, rows)
    if layer == 0:
        g.w = {"q": v("wq"), "k": v("wk"), "low": v("g1"), "v": v("wv"), "gate": v("g2", 64)}
        g.zbias = v("delta")
    else:
        g.w = {"q": v("wq"), "k": v("wk"), "low": v("gk1"), "z": v("gk2", 16), "v": v("wv"), "gate": v("wg")}
        g.zbias = v("b2")
    g.wo = v("wo").rearrange("p (a b) -> p a b", b=P)
    g.nw = v("nw")
    a = Carver(m.arena)
    g.qT, g.kT, g.c = a.take(TOK), a.take(TOK), a.take(TOK)
    g.v = a.take(TILES * g.vd).rearrange("p (a b) -> p a b", b=g.vd)
    g.gate = a.take(TILES * g.vd).rearrange("p (a b) -> p a b", b=g.vd)
    g.o = a.take(TILES * g.vd).rearrange("p (a b) -> p a b", b=g.vd)
    two = lambda: a.take(2 * SPAN4).rearrange("p (a b) -> p a b", a=2)
    g.es, g.qs, g.ks = two(), two(), two()
    g.at = a.take(2 * g.heads * P).rearrange("p (a h b) -> p a h b", a=2, h=g.heads)
    g.ksT = a.take(P)
    g.fine = a.take(2 * (FINE + 1) * BLOCK).rearrange("p (h b) -> p h b", h=2)
    g.block = a.take(2 * BLOCK).rearrange("p (h b) -> p h b", h=2)
    g.state = a.take(2 * g.vd).rearrange("p (a b) -> p a b", a=2)
    g.ms = a.take(TILES * g.heads)
    g.tmp = a.take(2 * BLK).rearrange("p (a b) -> p a b", a=2)
    levels = Carver(m.arena, a.at)
    lev = levels.take(2 * LEVELS * SPAN4)
    g.lev = lev.rearrange("p (q a b) -> p q a b", q=2, a=LEVELS)
    early = Carver(m.arena, a.at)
    g.z, g.soft, g.keep = early.take(TOK), early.take(TOK), early.take(TOK)
    g.lowT = g.o.rearrange("p a b -> p (a b)")[0:g.low, 0:TOK]
    late = Carver(m.arena, a.at)
    g.sq = lev[:, 0:TILES * g.vd]
    g.oT = late.take(g.vd // P * TOK).rearrange("p (a b) -> p a b", b=TOK)
    return g


def tern_tensor(nc, pe, m, s, f):
    T = nc.tensor
    pe.wait_ge(m.loaded["tern"], f.loaded)
    n = 0
    for i in range(NBLK):
        cols = slice(i * BLK, (i + 1) * BLK)
        for j in range(HB):
            if n >= 4:
                pe.wait_ge(s["glu"], f.done["glu"] + n - 3)
            out = slice(j * P, (j + 1) * P)
            T.matmul(m.ps[:, 2 * (n % 4), :], f.w1[:, out], m.hT[:, cols], start=True, stop=True)
            T.matmul(m.ps[:, 2 * (n % 4) + 1, :], f.w2[:, out], m.hT[:, cols], start=True, stop=True).then_inc(s["up"], 1)
            n += 1
    pe.wait_ge(s["glu"], f.done["glu"] + n)
    n = 0
    for w, src in ((f.h1, f.a), (f.h2, f.b)):
        for i in range(NBLK):
            cols = slice(i * BLK, (i + 1) * BLK)
            if src is f.b:
                pe.wait_ge(s["hid_read"], f.done["hid_read"] + (i + 1) * HB)
            for j in range(HB):
                if n >= 8:
                    pe.wait_ge(s["hid_read"], f.done["hid_read"] + n - 7)
                for k in range(HB):
                    last = T.matmul(m.ps[:, n % 8, :], w[:, k, j * P:(j + 1) * P], src[:, k, cols],
                                    start=k == 0, stop=k == HB - 1)
                last.then_inc(s["hid"], 1)
                n += 1
    for i in range(NBLK):
        pe.wait_ge(s["hid_read"], f.done["hid_read"] + max(20 + 4 * i, 25 + i))
        for t in range(4):
            for k in range(HB):
                last = T.matmul(m.ps[:, i, t * P:(t + 1) * P], f.a[:, k, (4 * i + t) * P:(4 * i + t + 1) * P],
                                f.w3[:, k, :], start=k == 0, stop=k == HB - 1)
        last.then_inc(s["y"], 1)


def tern_scalar(nc, act, m, s, f):
    n = 0
    for i in range(NBLK):
        for j in range(HB):
            act.wait_ge(s["up"], f.done["up"] + n + 1)
            if n >= 2:
                act.wait_ge(s["glu"], f.done["glu"] + n - 1)
            nc.scalar.activation(f.u[:, n % 2, :], m.ps[:, 2 * (n % 4), :], ACT.Silu,
                                 scale=f.s1[:, j:j + 1]).then_inc(s["silu"], 1)
            n += 1
    n = 0
    for dst, sc in ((f.b, f.sh1), (f.a, f.sh2)):
        for i in range(NBLK):
            for j in range(HB):
                act.wait_ge(s["hid"], f.done["hid"] + n + 1)
                if dst is f.a and j == 0:
                    act.wait_ge(s["hid"], f.done["hid"] + 16)
                nc.scalar.activation(dst[:, j, i * BLK:(i + 1) * BLK], m.ps[:, n % 8, :], ACT.Gelu,
                                     scale=sc[:, j:j + 1]).then_inc(s["hid_read"], 1)
                n += 1


def tern_vector(nc, dve, m, s, f):
    n = 0
    for i in range(NBLK):
        for j in range(HB):
            dve.wait_ge(s["silu"], f.done["silu"] + n + 1)
            nc.vector.scalar_tensor_tensor(f.a[:, j, i * BLK:(i + 1) * BLK], m.ps[:, 2 * (n % 4) + 1, :],
                                           f.s2[:, j:j + 1], f.u[:, n % 2, :], ALU.mult, ALU.mult).then_inc(s["glu"], 1)
            n += 1
    for b in range(BATCH):
        nc.vector.tensor_tensor(f.row[:, b, :], f.s3, gate_row(m, f.layer, FFN, b), ALU.mult)
    dve.drain()
    for i in range(NBLK):
        dve.wait_ge(s["y"], f.done["y"] + i + 1)
        add_gated(nc, dve, m, m.ps[:, i, :].rearrange("p (a b) -> p a b", a=4), 4 * i, 4,
                  repeat(f.row[:, i // 2, :], 4), f.tmp[:, i % 2, :].rearrange("p (a b) -> p a b", a=4))


TERN_SEMS = {"up": 16, "silu": 16, "glu": 16, "hid": 32, "hid_read": 32, "y": 4}


def tern_setup(m, layer):
    f = Memory()
    f.layer, f.loaded = layer, 16 if layer == 0 else 32
    f.done = {k: 0 if layer == 0 else n for k, n in TERN_SEMS.items()}
    v = lambda name: view(m.packs["tern"], "tern", name)
    f.w1, f.w2 = v("w1"), v("w2")
    f.h1, f.h2 = (v(x).rearrange("p (a b) -> p a b", a=HB) for x in ("h1", "h2"))
    f.w3 = v("w3").rearrange("p (a b) -> p a b", a=HB)
    f.s1, f.s2, f.sh1, f.sh2, f.s3 = (v(x) for x in ("s1", "s2", "sh1", "sh2", "s3"))
    a = Carver(m.arena)
    f.a = a.take(HB * TOK).rearrange("p (a b) -> p a b", a=HB)
    f.b = a.take(HB * TOK).rearrange("p (a b) -> p a b", a=HB)
    f.u = a.take(2 * BLK).rearrange("p (a b) -> p a b", a=2)
    f.tmp = a.take(2 * BLK).rearrange("p (a b) -> p a b", a=2)
    f.row = a.take(2 * P).rearrange("p (a b) -> p a b", a=2)
    return f


EXPERTS, RANK = 3, 8
LOW = EXPERTS * RANK
LOW1 = LOW + 1


def mole_tensor(nc, pe, m, s, f):
    T = nc.tensor
    pe.wait_ge(m.loaded["mole"], 16)
    for layer in range(2):
        if layer == 1:
            pe.wait_ge(s["hidden"], NBLK * HB)
        for t in range(TILES):
            out = m.ps[:, 0, t * 32:t * 32 + 27]
            if layer == 0:
                last = T.matmul(out, m.hT[:, t * P:(t + 1) * P], f.ar1, start=True, stop=True)
            else:
                for k in range(HB):
                    last = T.matmul(out, f.a[:, k, t * P:(t + 1) * P], f.ar2[:, k, :], start=k == 0, stop=k == HB - 1)
        last.then_inc(s["low"], 1)
        pe.wait_ge(s["gated"], layer + 1)
        for i in range(NBLK):
            for t in range(4):
                last = T.transpose(m.ps[0:LOW1, 1 + i, t * P:(t + 1) * P], f.zg[:, 4 * i + t, :], m.ident)
            last.then_inc(s["turned"], 1)
        pe.wait_ge(s["zT"], NBLK * (layer + 1))
        if layer == 0:
            n = 0
            for i in range(NBLK):
                cols = slice(i * BLK, (i + 1) * BLK)
                for j in range(HB):
                    out = slice(j * P, (j + 1) * P)
                    if n >= 8:
                        pe.wait_ge(s["hidden"], n - 7)
                    T.matmul(m.ps[:, n % 8, :], f.w1[:, out], m.hT[:, cols], start=True, stop=False)
                    T.matmul(m.ps[:, n % 8, :], f.b1[:, out], f.zT[0:LOW1, cols], start=False,
                             stop=True).then_inc(s["hid"], 1)
                    n += 1
    for i in range(NBLK):
        for t in range(4):
            tok = slice((4 * i + t) * P, (4 * i + t + 1) * P)
            out = m.ps[:, 4 + i, t * P:(t + 1) * P]
            if i == 0 and t == 0:
                pe.wait_ge(s["zT"], 2 * NBLK)
            for k in range(HB):
                T.matmul(out, f.a[:, k, tok], f.w2[:, k, :], start=k == 0, stop=False)
            last = T.matmul(out, f.zT[0:LOW1, tok], f.b2, start=False, stop=True)
        last.then_inc(s["y"], 1)


def mole_scalar(nc, act, m, s, f):
    for layer in range(2):
        act.wait_ge(s["logits"], layer + 1)
        nc.scalar.activation(f.lg[:, :, :], f.lg[:, :, :], ACT.Exp).then_inc(s["exped"], 1)
        for i in range(NBLK):
            act.wait_ge(s["turned"], NBLK * layer + i + 1)
            if layer == 1 and i == 0:
                act.wait_ge(s["hid"], NBLK * HB)
            nc.scalar.activation(f.zT[0:LOW1, i * BLK:(i + 1) * BLK], m.ps[0:LOW1, 1 + i, :], ACT.Copy)\
                .then_inc(s["zT"], 1)
        if layer == 0:
            for n in range(NBLK * HB):
                i, j = divmod(n, HB)
                act.wait_ge(s["hid"], n + 1)
                nc.scalar.activation(f.a[:, j, i * BLK:(i + 1) * BLK], m.ps[:, n % 8, :], ACT.Relu)\
                    .then_inc(s["hidden"], 1)


def mole_vector(nc, dve, m, s, f):
    V = nc.vector
    V.memset(f.zg[:, :, LOW:LOW1], 1.0)
    for layer in range(2):
        dve.wait_ge(s["low"], layer + 1)
        zr = m.ps[:, 0, :].rearrange("p (a b) -> p a b", b=32)
        if layer == 1:
            dve.wait_ge(s["turned"], NBLK)
        V.tensor_copy(f.z[:, :, :], zr[:, :, 0:27])
        dve.drain()
        V.tensor_reduce(f.red[:, :], f.z[:, :, LOW:27], AX, ALU.max)
        dve.drain()
        V.tensor_tensor(f.lg[:, :, :], f.z[:, :, LOW:27], spread(f.red[:, :], EXPERTS), ALU.subtract)\
            .then_inc(s["logits"], 1)
        dve.wait_ge(s["exped"], layer + 1)
        V.tensor_reduce(f.red[:, :], f.lg[:, :, :], AX, ALU.add)
        dve.drain()
        V.reciprocal(f.red[:, :], f.red[:, :])
        dve.drain()
        V.tensor_scalar(f.red[:, :], f.red[:, :], 1.0 / RANK, None, ALU.mult)
        dve.drain()
        V.tensor_tensor(f.lg[:, :, :], f.lg[:, :, :], spread(f.red[:, :], EXPERTS), ALU.mult)
        dve.drain()
        for e in range(EXPERTS):
            part = slice(e * RANK, (e + 1) * RANK)
            last = V.tensor_tensor(f.zg[:, :, part], f.z[:, :, part], f.lg[:, :, e:e + 1].broadcast_to([P, TILES, RANK]),
                                   ALU.mult)
        last.then_inc(s["gated"], 1)
    for i in range(NBLK):
        dve.wait_ge(s["y"], i + 1)
        add_gated(nc, dve, m, m.ps[:, 4 + i, :].rearrange("p (a b) -> p a b", a=4), 4 * i, 4,
                  repeat(gate_row(m, 1, FFN, i // 2), 4), f.tmp[:, i % 2, :].rearrange("p (a b) -> p a b", a=4))


MOLE_SEMS = ("low", "gated", "turned", "zT", "hid", "hidden", "logits", "exped", "y")


def mole_setup(m):
    f = Memory()
    v = lambda name, rows=P: view(m.packs["mole"], "mole", name, rows)
    f.w1, f.ar1, f.b1, f.b2 = v("w1"), v("ar1"), v("b1", LOW1), v("b2", LOW1)
    f.w2 = v("w2").rearrange("p (a b) -> p a b", a=HB)
    f.ar2 = v("ar2").rearrange("p (a b) -> p a b", a=HB)
    a = Carver(m.arena)
    f.a = a.take(HB * TOK).rearrange("p (a b) -> p a b", a=HB)
    f.z = a.take(TILES * 27).rearrange("p (a b) -> p a b", b=27)
    f.zg = a.take(TILES * LOW1).rearrange("p (a b) -> p a b", b=LOW1)
    f.lg = a.take(TILES * EXPERTS).rearrange("p (a b) -> p a b", b=EXPERTS)
    f.red = a.take(TILES)
    f.zT = a.take(TOK)
    f.tmp = a.take(2 * BLK).rearrange("p (a b) -> p a b", a=2)
    return f


STATES, TAPS, INB = 16, 4, 2


def ssm_tensor(nc, pe, m, s, f):
    T = nc.tensor
    pe.wait_ge(m.loaded["l2"], 16)
    n = 0
    for j in range(2 * INB):
        for i in range(NBLK):
            if n >= 8:
                pe.wait_ge(s["proj_read"], n - 7)
            T.matmul(m.ps[:, n % 8, :], f.win[:, j * P:(j + 1) * P], m.hT[:, i * BLK:(i + 1) * BLK], start=True,
                     stop=True).then_inc(s["proj"], 1)
            n += 1
    pe.wait_ge(s["proj_read"], n)
    for j in range(INB):
        for st in range(STATES):
            k = j * STATES + st
            for i in range(NBLK):
                pe.wait_ge(s["scanned"], 2 * k + i // 2 + 1)
                last = T.matmul(m.ps[:, 4 * j + i, :], m.ident, f.h[:, k % 2, i * BLK:(i + 1) * BLK], start=st == 0,
                                stop=st == STATES - 1)
            last.then_inc(s["summed"], 1)
    pe.wait_ge(s["mixed"], INB)
    for i in range(NBLK):
        for t in range(4):
            for k in range(INB):
                last = T.matmul(m.ps[:, i, t * P:(t + 1) * P], f.y[:, k, (4 * i + t) * P:(4 * i + t + 1) * P],
                                f.wout[:, k, :], start=k == 0, stop=k == INB - 1)
        last.then_inc(s["out"], 1)


def ssm_scalar(nc, act, m, s, f):
    A = nc.scalar.activation
    n = 0
    for j in range(2 * INB):
        for i in range(NBLK):
            act.wait_ge(s["proj"], n + 1)
            if j < INB:
                b, half = divmod(i, 2)
                at = TAPS - 1 + half * BLK
                done = A(f.xs[:, j, b, at:at + BLK], m.ps[:, n % 8, :], ACT.Copy)
            else:
                done = A(f.res[:, j - INB, i * BLK:(i + 1) * BLK], m.ps[:, n % 8, :], ACT.Silu)
            done.then_inc(s["proj_read"], 1)
            n += 1
    for j in range(INB):
        act.wait_ge(s["conv"], j + 1)
        A(f.xc[:, j, :], f.acc[:, j, :], ACT.Silu, bias=f.cb[:, j:j + 1]).then_inc(s["silu"], 1)
    act.drain()
    A(f.bx[:, :, :], f.xc[:, :, :], ACT.Square)
    A(f.dt[:, :, :], f.xc[:, :, :], ACT.Abs)
    A(f.arate[:, :], f.alog, ACT.Exp)
    act.drain()
    A(f.dt[:, :, :], f.dt[:, :, :], ACT.Exp, scale=-1.0)
    act.drain()
    A(f.dt[:, :, :], f.dt[:, :, :], ACT.Ln, bias=1.0).then_inc(s["soft"], 1)
    act.wait_ge(s["delta"], 1)
    for k in range(INB * STATES):
        if k >= 2:
            act.wait_ge(s["scanned"], 2 * (k - 1))
        A(f.decay[:, k % 2, :], f.dt[:, k // STATES, :], ACT.Exp, scale=f.arate[:, k:k + 1]).then_inc(s["decayed"], 1)


def ssm_vector(nc, dve, m, s, f):
    V = nc.vector
    V.memset(f.xs[:, :, :, 0:TAPS - 1], 0.0)
    dve.drain()
    for j in range(INB):
        dve.wait_ge(s["proj_read"], (j + 1) * NBLK)
        acc = f.acc[:, j, :].rearrange("p (b t) -> p b t", b=BATCH)
        V.tensor_scalar(acc, f.xs[:, j, :, 0:SEQ], f.cw[:, j, 0:1], None, ALU.mult)
        for tap in range(1, TAPS):
            dve.drain()
            last = V.scalar_tensor_tensor(acc, f.xs[:, j, :, tap:tap + SEQ], f.cw[:, j, tap:tap + 1], acc, ALU.mult,
                                          ALU.add)
        last.then_inc(s["conv"], 1)
    dve.wait_ge(s["soft"], 1)
    V.scalar_tensor_tensor(f.dt[:, :, :], f.xc[:, :, :], 0.0, f.dt[:, :, :], ALU.max, ALU.add)
    V.tensor_scalar(f.arate[:, :], f.arate[:, :], -1.0, None, ALU.mult).then_inc(s["delta"], 1)
    dve.drain()
    for k in range(INB * STATES):
        j = k // STATES
        dve.wait_ge(s["decayed"], k + 1)
        if k >= 2:
            dve.wait_ge(s["summed"], k - 1)
        for b in range(BATCH):
            half = slice(b * SEQ, (b + 1) * SEQ)
            V.tensor_tensor_scan(f.h[:, k % 2, half], f.decay[:, k % 2, half], f.bx[:, j, half], 0.0, ALU.mult,
                                 ALU.add).then_inc(s["scanned"], 1)
    for j in range(INB):
        dve.wait_ge(s["summed"], (j + 1) * STATES)
        for i in range(NBLK):
            cols = slice(i * BLK, (i + 1) * BLK)
            V.tensor_tensor(f.y[:, j, cols], m.ps[:, 4 * j + i, :], f.xc[:, j, cols], ALU.mult)
        dve.drain()
        V.tensor_tensor(f.y[:, j, :], f.y[:, j, :], f.res[:, j, :], ALU.mult)
        dve.drain()
        V.scalar_tensor_tensor(f.y[:, j, :], f.xc[:, j, :], f.d[:, j:j + 1], f.y[:, j, :], ALU.mult, ALU.add)\
            .then_inc(s["mixed"], 1)
    for i in range(NBLK):
        dve.wait_ge(s["out"], i + 1)
        add_gated(nc, dve, m, m.ps[:, i, :].rearrange("p (a b) -> p a b", a=4), 4 * i, 4,
                  repeat(gate_row(m, 2, ATTN, i // 2), 4), f.tmp[:, i % 2, :].rearrange("p (a b) -> p a b", a=4))


SSM_SEMS = ("proj", "proj_read", "conv", "silu", "soft", "delta", "decayed", "scanned", "summed", "mixed", "out")


def ssm_setup(m):
    f = Memory()
    v = lambda name: view(m.packs["l2"], "l2", name)
    f.win, f.cb, f.d, f.alog = v("win"), v("cb"), v("d"), v("alog")
    f.cw = v("cw").rearrange("p (a b) -> p a b", a=INB)
    f.wout = v("wout").rearrange("p (a b) -> p a b", a=INB)
    a = Carver(m.arena)
    two = lambda n: a.take(2 * n).rearrange("p (a b) -> p a b", a=2)
    f.xs = a.take(INB * BATCH * (SEQ + TAPS - 1)).rearrange("p (a b t) -> p a b t", a=INB, b=BATCH)
    f.res, f.xc, f.dt, f.bx, f.decay, f.h = (two(TOK) for _ in range(6))
    f.acc, f.y = f.h, f.dt
    f.arate = a.take(INB * STATES)
    f.tmp = f.decay[:, 0, 0:2 * BLK].rearrange("p (a b) -> p a b", a=2)
    return f


HEADS, KD = 16, 8
PAIRS = BATCH * HEADS
STACK = 9 * KD
RING = 4
ROUNDS = PAIRS // RING
S_JOBS = 2 * BT + 1
LEAD = 2


def pair_at(r, par, ahead=0):
    return r + (par + ahead) // RING, (par + ahead) % RING


def pair_steps(eng, step):
    for par in range(RING):
        step(0, par, par == 0, False)
    with eng.Fori(1, ROUNDS - 1) as r:
        for par in range(RING):
            step(r, par, False, False)
    for par in range(RING):
        step(ROUNDS - 1, par, False, par >= RING - LEAD)


def mha_tensor(nc, pe, m, s, f):
    T = nc.tensor
    pe.wait_ge(m.loaded["l3"], 16)
    for n in range(12):
        if n >= 8:
            pe.wait_ge(s["proj_read"], n - 7)
        kind, i = divmod(n, NBLK)
        if kind < 2:
            T.matmul(m.ps[:, n % 8, :], (f.wq, f.wk)[kind], m.hT[:, i * BLK:(i + 1) * BLK], start=True,
                     stop=True).then_inc(s["proj"], 1)
        else:
            for t in range(4):
                last = T.matmul(m.ps[:, n % 8, t * P:(t + 1) * P], m.hT[:, (4 * i + t) * P:(4 * i + t + 1) * P], f.wv,
                                start=True, stop=True)
            last.then_inc(s["proj"], 1)
    pe.wait_ge(s["proj_read"], 12)

    def scores_job(r, par, j):
        n = RING * r + par
        job = n * S_JOBS + j
        bank = (par + j) % 2
        if j == 0:
            pe.wait_ge(s["stack"][par], 16 * 6 * (r + 1))
        if not isinstance(job, int) or job >= 2:
            pe.wait_ge(s["s_read"], job - 1)
        if j < 2 * BT:
            T.matmul(m.ps[:, bank, :], f.qst[par][0:STACK, (j // 2) * P:(j // 2 + 1) * P],
                     f.kst[par][0:STACK, (j % 2) * BLK:(j % 2 + 1) * BLK], start=True, stop=True).then_inc(s["s_made"], 1)
        else:
            pe.wait_ge(s["maxima"], n + 1)
            T.transpose(m.ps[0:BT, bank, 0:P], f.mcol[:, :], m.ident).then_inc(s["s_made"], 1)

    def exponents(r, par, kt):
        n = RING * r + par
        if kt == 0:
            pe.wait_ge(s["mrow"][par % 2], 16 * (2 * r + par // 2 + 1))
        job = n * BT + kt
        if not isinstance(job, int) or job >= 2:
            pe.wait_ge(s["exped"], job - 1)
        for half in range(2):
            last = T.matmul(m.ps[:, 2 + 2 * (kt % 2) + half, :], f.kst[par][0:STACK + 3, kt * P:(kt + 1) * P],
                            f.qst[par][0:STACK + 3, half * BLK:(half + 1) * BLK], start=True, stop=True)
        last.then_inc(s["st_made"], 1)

    def values(r, par, quad, half):
        n = RING * r + par
        if half == 0:
            pe.wait_ge(s["exped"], n * BT + 4 * quad + 4)
            if quad == 0:
                pe.wait_ge(s["vcopied"], n + 1)
        if quad == 0 and (not isinstance(n, int) or n >= 1):
            pe.wait_ge(s["osum"], n)
        for g in range(4):
            kt = 4 * quad + g
            last = T.matmul(m.ps[32 * g:32 * g + 32, 6 + half, :], f.vst[par][:, kt, :],
                            f.prob[:, kt, half * BLK:(half + 1) * BLK], start=quad == 0, stop=quad == 1)
        if half == 1:
            last.then_inc(s["pv"], 1)

    def step(r, par, first, last):
        ahead = pair_at(r, par, LEAD)
        for kt in range(BT):
            exponents(r, par, kt)
            if kt < 2 and not first:
                values(*pair_at(r, par, -1), 1, kt)
            if kt == 0 and not first and not (last and par == RING - 1):
                scores_job(*pair_at(r, par, LEAD - 1), 2 * BT)
            if not last:
                scores_job(*ahead, 2 * kt)
                scores_job(*ahead, 2 * kt + 1)
            if kt in (5, 6):
                values(r, par, 0, kt - 5)

    for n in range(LEAD):
        for j in range(S_JOBS):
            scores_job(0, n, j)
    pair_steps(pe, step)
    for half in range(2):
        values(ROUNDS - 1, RING - 1, 1, half)

    pe.wait_ge(s["normed"], 1)
    for i in range(NBLK):
        for t in range(4):
            last = T.matmul(m.ps[:, i, t * P:(t + 1) * P], f.oT[:, (4 * i + t) * P:(4 * i + t + 1) * P], f.wo,
                            start=True, stop=True)
        last.then_inc(s["y"], 1)


def mha_scalar(nc, act, m, s, f):
    A = nc.scalar.activation
    for n in range(12):
        kind, i = divmod(n, NBLK)
        act.wait_ge(s["proj"], n + 1)
        if kind < 2:
            A((f.q, f.k)[kind][:, i * BLK:(i + 1) * BLK], m.ps[:, n % 8, :], ACT.Copy).then_inc(s["proj_read"], 1)
        else:
            for t in range(4):
                b, kt = divmod(4 * i + t, BT)
                last = A(f.v[:, b, :, kt, :], m.ps[:, n % 8, t * P:(t + 1) * P].rearrange("p (h v) -> p h v", h=HEADS),
                         ACT.Copy)
            last.then_inc(s["proj_read"], 1)

    def collect(n, r, par):
        act.wait_ge(s["pv"], 2 * n + 2)
        if not isinstance(n, int) or n >= 2:
            act.wait_ge(s["ostored"][par % 2], 16 * (2 * r + par // 2))
        A(f.osum[par % 2].rearrange("p (a b) -> p a b", a=2), m.ps[:, 6:8, :], ACT.Copy).then_inc(s["osum"], 1)

    def step(r, par, first, last):
        n = RING * r + par
        for kt in range(BT):
            act.wait_ge(s["st_made"], n * BT + kt + 1)
            if kt % 4 == 0 and not first:
                act.wait_ge(s["pv"], 2 * n - 1 + kt // 4)
            slot = 2 + 2 * (kt % 2)
            A(f.prob[:, kt, :].rearrange("p (a b) -> p a b", a=2), m.ps[:, slot:slot + 2, :], ACT.Exp,
              scale=float(KD) ** -0.5).then_inc(s["exped"], 1)
            if kt == 3 and not first:
                collect(n - 1, *pair_at(r, par, -1))

    act.wait_ge(s["sent"], 6 * 16)
    pair_steps(act, step)
    collect(PAIRS - 1, ROUNDS - 1, RING - 1)


def mha_vector(nc, dve, m, s, f):
    V = nc.vector
    for par in range(RING):
        V.memset(f.kst[par][0:96, :], 1.0)
        V.memset(f.vst[par][:, :, :], 0.0)
    dve.drain()
    for par in range(RING):
        V.memset(f.vst[par][:, :, KD:KD + 1], 1.0)
    dve.drain().then_inc(s["ones"], 1)
    for a, (src, dst) in enumerate(((f.q, f.qp), (f.k, f.kp))):
        dve.wait_ge(s["proj_read"], 4 * (a + 1))
        for part in range(3):
            V.tensor_copy(dst[:, part, :], src[:, :]).then_inc(s["parts"], 1)
            if part < 2:
                dve.drain()
                V.tensor_tensor(src[:, :], src[:, :], dst[:, part, :], ALU.subtract)
                dve.drain()

    def row_max(r, par, j):
        n = RING * r + par
        dve.wait_ge(s["s_made"], n * S_JOBS + j + 1)
        V.tensor_reduce(f.mp[:, j:j + 1], m.ps[:, (par + j) % 2, :], AX, ALU.max).then_inc(s["s_read"], 1)

    def maxima(r, par):
        n = RING * r + par
        dve.drain()
        mp = f.mp[:, :].rearrange("p (a b) -> p a b", b=2)
        V.tensor_tensor(f.mcol[:, :], mp[:, :, 0], mp[:, :, 1], ALU.max).then_inc(s["maxima"], 1)
        dve.wait_ge(s["s_made"], n * S_JOBS + S_JOBS)
        if not isinstance(n, int) or n >= 1:
            dve.wait_ge(s["mparts"], n)
        V.tensor_scalar(f.mneg[:, :], m.ps[0:BT, par % 2, 0:P], -1.0, None, ALU.mult).then_inc(s["s_read"], 1)
        dve.drain().then_inc(s["mneg"], 1)

    def step(r, par, first, last):
        if not last:
            ahead = pair_at(r, par, LEAD)
            for j in range(2 * BT):
                row_max(*ahead, j)
            maxima(*ahead)

    for n in range(LEAD):
        for j in range(2 * BT):
            row_max(0, n, j)
        maxima(0, n)
    pair_steps(dve, step)

    def four_groups(whole, total, at):
        V.tensor_tensor(whole[:, 0:2, at], whole[:, 0:2, at], whole[:, 2:4, at], ALU.add)
        dve.drain()
        V.tensor_tensor(total[:, at], whole[:, 0, at], whole[:, 1, at], ALU.add)
        dve.drain()

    for b in range(BATCH):
        dve.wait_ge(s["final"][0], 16 * HEADS * (b + 1))
        at = slice(b * SEQ, (b + 1) * SEQ)
        four_groups(f.denom4, f.denom, at)
        V.reciprocal(f.denom[:, at], f.denom[:, at])
    dve.wait_ge(s["final"][1], 16 * HEADS * BATCH)
    four_groups(f.o4, f.oT, slice(0, TOK))
    V.tensor_tensor(f.oT[:, :], f.oT[:, :], f.denom[:, :], ALU.mult).then_inc(s["normed"], 1)
    for i in range(NBLK):
        dve.wait_ge(s["y"], i + 1)
        add_gated(nc, dve, m, m.ps[:, i, :].rearrange("p (a b) -> p a b", a=4), 4 * i, 4,
                  repeat(gate_row(m, 3, ATTN, i // 2), 4), f.tmp[:, i % 2, :].rearrange("p (a b) -> p a b", a=4))


def mha_gpsimd(nc, pool, m, s, f):
    nc.gpsimd.memset(f.zeros, 0.0)
    pool.drain()
    pool.wait_ge(s["proj_read"], 12)
    pool.wait_ge(s["ones"], 1)

    def pair(r, par):
        n = RING * r + par
        if not isinstance(r, int) or r >= 1:
            pool.wait_ge(s["pv"], 2 * (n - RING) + 2)
        nc.gpsimd.tensor_copy(f.vst[par][:, :, 0:KD],
                              f.vflat[:, bass.ds(n * (BT * KD), BT * KD)].rearrange("p (a b) -> p a b", b=KD))\
            .then_inc(s["vcopied"], 1)

    def split(r, par):
        G = nc.gpsimd
        n = RING * r + par
        pool.wait_ge(s["mneg"], n + 1)
        if not isinstance(n, int) or n >= 1:
            pool.wait_ge(s["mstored"], 16 * n)
        G.tensor_tensor(f.mparts[:, 0, :], f.mneg[:, :], f.zeros, ALU.add)
        pool.drain()
        G.tensor_tensor(f.mneg[:, :], f.mneg[:, :], f.mparts[:, 0, :], ALU.subtract)
        pool.drain()
        G.tensor_copy(f.mparts[:, 1, :], f.mneg[:, :])
        pool.drain()
        G.tensor_tensor(f.mparts[:, 2, :], f.mneg[:, :], f.mparts[:, 1, :], ALU.subtract).then_inc(s["mparts"], 1)

    def step(r, par, first, last):
        if not isinstance(r, int) or 1 <= RING * r + par <= PAIRS - RING:
            pair(*pair_at(r, par, RING - 1))
        if not last:
            split(*pair_at(r, par, LEAD))

    for par in range(RING):
        pair(0, par)
    for n in range(LEAD):
        split(0, n)
    pair_steps(pool, step)


def mha_sync(nc, sp, m, s, f):
    for a, (src, dst) in enumerate(((f.qp, f.scr_q), (f.kp, f.scr_k))):
        for part in range(3):
            sp.wait_ge(s["parts"], 3 * a + part + 1)
            sp.dma_start(f.scr_parts[a, part].rearrange("(b r) t -> r b t", b=BATCH),
                         src[:, part, :].rearrange("p (b t) -> p b t", b=BATCH)).then_inc(s["sent"], 16)
    sp.wait_ge(s["sent"], 6 * 16)
    for a, dst in enumerate((f.scr_q, f.scr_k)):
        for at in range(5 if a == 0 else 3):
            part = at % 3
            sp.dma_start(dst[:, at, :, :], f.scr_parts[a, part].rearrange("(n k) t -> n k t", k=KD))\
                .then_inc(s["grouped"], 16)
    sp.wait_ge(s["grouped"], 8 * 16)
    sp.wait_ge(s["ones"], 1)

    def stacks(r, par):
        n = RING * r + par
        if not isinstance(r, int) or r >= 1:
            sp.wait_ge(s["pv"], 2 * (n - RING) + 2)
        q_rows = f.scr_q.rearrange("n p k t -> (n p k) t")
        k_rows = f.scr_k.rearrange("n p k t -> (n p k) t")
        for a in range(3):
            at = slice(a * 3 * KD, (a + 1) * 3 * KD)
            sp.dma_start(f.qst[par][at, :], q_rows[bass.ds(n * (5 * KD) + a * KD, 3 * KD), :])\
                .then_inc(s["stack"][par], 16)
            sp.dma_start(f.kst[par][at, :], k_rows[bass.ds(n * (3 * KD), 3 * KD), :]).then_inc(s["stack"][par], 16)

    def maxima(r, par):
        n = RING * r + par
        sp.wait_ge(s["mparts"], n + 1)
        sp.dma_start(f.scr_m[par].rearrange("s (q t) -> q s t", q=BT), f.mparts[:, :, :]).then_inc(s["mstored"], 16)
        sp.wait_ge(s["mstored"], 16 * n + 16)
        sp.dma_start(f.qst[par][STACK:STACK + 3, :], f.scr_m[par]).then_inc(s["mrow"][par % 2], 16)

    def store(r, par):
        n = RING * r + par
        sp.wait_ge(s["osum"], n + 1)
        sp.dma_start(f.scr_o[bass.ds(n, 1), :, :].rearrange("a r t -> (a r) t"), f.osum[par % 2])\
            .then_inc(s["ostored"][par % 2], 16)

    def step(r, par, first, last):
        if not first:
            store(*pair_at(r, par, -1))
        ahead = pair_at(r, par, LEAD + 1)
        if not isinstance(r, int) or RING * r + par + LEAD + 1 < PAIRS:
            stacks(*ahead)
        if not last:
            maxima(*pair_at(r, par, LEAD))

    for n in range(LEAD + 1):
        stacks(0, n)
    for n in range(LEAD):
        maxima(0, n)
    pair_steps(sp, step)
    scr_o = f.scr_o.rearrange("(b h) (g r) t -> b h r g t", b=BATCH, g=4)

    def denominators(b):
        for h in range(HEADS):
            sp.dma_start(f.denom4[h * KD:(h + 1) * KD, :, b * SEQ:(b + 1) * SEQ],
                         scr_o[b, h, KD:KD + 1].broadcast_to([KD, 4, SEQ])).then_inc(s["final"][0], 16)

    for k in range(2):
        sp.wait_ge(s["ostored"][k], 16 * (PAIRS // 2 - k))
    denominators(0)
    store(ROUNDS - 1, RING - 1)
    sp.wait_ge(s["final"][0], 16 * HEADS)
    sp.wait_ge(s["ostored"][1], 16 * PAIRS // 2)
    denominators(1)
    for h in range(HEADS):
        rows = slice(h * KD, (h + 1) * KD)
        for b in range(BATCH):
            sp.dma_start(f.o4[rows, :, b * SEQ:(b + 1) * SEQ], scr_o[b, h, 0:KD]).then_inc(s["final"][1], 16)


MHA_SEMS = ("proj", "proj_read", "parts", "sent", "grouped", "ones", "stack0", "stack1", "stack2", "stack3",
            "s_made", "s_read", "maxima", "mneg", "mparts", "mstored", "mrow0", "mrow1", "st_made", "exped",
            "vcopied", "pv", "osum", "ostored0", "ostored1", "final0", "final1",
            "normed", "y")


def mha_setup(m):
    f = Memory()
    nc = m.d["nc"]
    v = lambda name: view(m.packs["l3"], "l3", name)
    f.wq, f.wk, f.wv, f.wo = v("wq"), v("wk"), v("wv"), v("wo")
    f.scr_parts = nc.dram_tensor("scr_parts", (2, 3, PAIRS * KD, SEQ), BF16).ap()
    f.scr_q = nc.dram_tensor("scr_q", (PAIRS, 5, KD, SEQ), BF16).ap()
    f.scr_k = nc.dram_tensor("scr_k", (PAIRS, 3, KD, SEQ), BF16).ap()
    f.scr_m = nc.dram_tensor("scr_m", (RING, 3, SEQ), BF16).ap()
    f.scr_o = nc.dram_tensor("scr_o", (PAIRS, 4 * 32, SEQ), F32).ap()
    a = Carver(m.arena, DEEP_AT // 2)
    f.qst = [a.bf16(SEQ) for _ in range(RING)]
    f.kst = [a.bf16(SEQ) for _ in range(RING)]
    f.vst = [a.take(BT * 32).rearrange("p (a b) -> p a b", b=32) for _ in range(RING)]
    f.vflat = a.take(TOK)
    f.v = f.vflat.rearrange("p (b h t v) -> p b h t v", b=BATCH, h=HEADS, t=BT)
    f.osum = [a.take(SEQ) for _ in range(2)]
    f.mp, f.mcol = a.take(2 * BT), a.take(BT)
    f.mneg, f.zeros = a.take(P)[0:BT, :], a.take(P)[0:BT, :]
    f.mparts = a.bf16(3 * P + 128)[0:BT, 0:3 * P].rearrange("p (s t) -> p s t", s=3)
    early = Carver(m.arena, a.at)
    f.q, f.k = early.take(TOK), early.take(TOK)
    f.qp, f.kp = (early.bf16(3 * TOK).rearrange("p (s t) -> p s t", s=3) for _ in range(2))
    main = Carver(m.arena, a.at)
    f.prob = main.take(BT * SEQ).rearrange("p (a b) -> p a b", a=BT)
    late = Carver(m.arena, a.at)
    f.o4, f.denom4 = (late.take(4 * TOK).rearrange("p (a b) -> p a b", b=TOK) for _ in range(2))
    f.oT, f.denom = f.o4[:, 2, :], f.denom4[:, 2, :]
    f.tmp = late.take(2 * BLK).rearrange("p (a b) -> p a b", a=2)
    return f


DH = 64
LH = 16
INNER = LH * DH
QB = INNER // P
WIN = 32
HALF = P // 2
SPAN = WIN + HALF
KEYS = WIN + P
FRONT = WIN + 1
ORDER = [h for h in range(0, LH, 2)] + [h for h in range(1, LH, 2)]
GROUP = 4
NORM_SHIFT = 2.0 ** 20
GUARD = 1e-24
FF = 341
FF_ROWS = [P, P, FF - 2 * P]
LOOPED = BT - 1


class Ring:

    def __init__(self, made, freed, start, tile, last):
        self.made, self.freed = made, freed
        self.jobs = {"start": start, "tile": tile, "last0": last[0], "last1": last[1]}
        n = len(tile)
        self.at = {"start": 0, "tile": len(start), "last0": len(start) + 2 * LOOPED * n}
        self.at["last1"] = self.at["last0"] + len(last[0])
        self.total = self.at["last1"] + len(last[1])
        assert self.total % 2 == 0

    def position(self, where, name):
        rnd, kind, c, b = where
        if kind == "last":
            kind = f"last{b}"
        i = self.at[kind] + self.jobs[kind].index(name)
        before = rnd * (self.total // 2)
        if kind == "tile":
            n = len(self.jobs["tile"])
            i += n * b
            before = before + n * c
        return i % 2, before + i // 2

    def place(self, where, name):
        return self.position(where, name)[0]

    def before_fill(self, eng, where, name):
        place, before = self.position(where, name)
        eng.wait_ge(self.freed[place], before)

    def before_read(self, eng, where, name):
        place, before = self.position(where, name)
        eng.wait_ge(self.made[place], before + 1)

    def after_read(self, eng, where, name):
        place, before = self.position(where, name)
        eng.wait_ge(self.freed[place], before + 1)


def deep_rings(s):
    wide = Ring(s["wide_made"], s["wide_freed"], start=["q0", "k0", "q1", "k1", "v0", "v1"],
                tile=["q", "p0", "k", "p1", "v0", "heads", "v1"],
                last=(["p0", "p1", "v0", "heads", "v1"], ["p0", "p1", "heads"]))
    tile = ["t0", "t1", "o0", "o1", "t2", "t3", "y"]
    turn = Ring(s["turn_made"], s["turn_freed"], start=["t0", "t1", "t2", "t3"], tile=tile, last=(tile, ["o0", "o1", "y"]))
    groups = [f"s{j}" for j in range(LH // GROUP)]
    score = Ring(s["score_made"], s["score_freed"], start=[], tile=groups, last=(groups, groups))
    return wide, score, turn


def deep_rounds(eng, start, tile, ffn):
    with eng.Fori(0, DEPTH // 2) as dd:
        for par in range(2):
            rnd = 2 * dd + par
            start(rnd, dd, par)
            with eng.Fori(0, LOOPED) as c:
                for b in range(BATCH):
                    tile((rnd, "tile", c, b), 16 * rnd + 2 * c + b, c, b, par, True, True)
            for b in range(BATCH):
                tile((rnd, "last", LOOPED, b), 16 * rnd + 2 * LOOPED + b, LOOPED, b, par, False, b == 0)
            if ffn is not None:
                ffn(rnd, par)


def deep_tensor(nc, pe, m, s, f):
    T = nc.tensor
    wide, score, turn = deep_rings(s)
    pe.wait_ge(s["ready"], 1)

    def project(w, where, name, j, b, rows):
        wide.before_fill(pe, where, name)
        at = 2 * wide.place(where, name)
        for half in range(2):
            last = T.matmul(m.ps[0:rows.stop - rows.start, at + half, :], f.xs[b][:, rows],
                            w.wqkv[:, j * INNER + half * BLK:j * INNER + (half + 1) * BLK], start=True, stop=True)
        last.then_inc(wide.made[wide.place(where, name)], 1)

    def values(w, where, b, half):
        project(w, where, f"v{half}", 2, b, slice(HALF * half, HALF * half + SPAN))

    def turned(where, name, src, k0):
        turn.before_fill(pe, where, name)
        place = turn.place(where, name)
        for i in range(4):
            last = T.transpose(m.ps[:, 6 + place, i * P:(i + 1) * P], src[:, (k0 + i) * P:(k0 + i + 1) * P], m.ident)
        last.then_inc(turn.made[place], 1)

    def start(rnd, dd, par):
        where, w = (rnd, "start", 0, 0), f.w[par]
        for b in range(BATCH):
            pe.wait_ge(s["staged"], 16 * rnd + b + 1)
            pe.wait_ge(s["weights"][par], 16 * dd + 16)
            project(w, where, f"q{b}", 0, b, slice(WIN, KEYS))
            project(w, where, f"k{b}", 1, b, slice(WIN, KEYS))
        values(w, where, 0, 0)
        values(w, where, 0, 1)
        pe.wait_ge(s["rotated"], 16 * rnd + 1)
        for j in range(4):
            turned(where, f"t{j}", f.rot[0], 4 * j)

    def tile(where, t, c, b, par, ahead2, ahead1):
        w = f.w[par]

        def scores(j):
            name = f"s{j}"
            score.before_fill(pe, where, name)
            bank = 4 + score.place(where, name)
            T.matmul(m.ps[:, bank, 0:GROUP * SPAN], f.identb,
                     f.bands[:, bass.ds(c, 1), :].broadcast_to([P, GROUP, SPAN]), start=True, stop=False,
                     skip_group_check=True)
            for i, h in enumerate(ORDER[GROUP * j:GROUP * (j + 1)]):
                rows = slice(DH * (h % 2), DH * (h % 2) + DH)
                for half in range(2):
                    last = T.matmul(m.ps[HALF * half:HALF * (half + 1), bank, i * SPAN:(i + 1) * SPAN],
                                    f.qT[rows, h // 2, HALF * half:HALF * (half + 1)],
                                    f.kT[b][rows, h // 2, HALF * half:HALF * half + SPAN], start=False, stop=True,
                                    skip_group_check=True)
            last.then_inc(score.made[score.place(where, name)], 1)

        def probs(j):
            name = f"p{j}"
            score.after_read(pe, where, f"s{2 * j}")
            score.after_read(pe, where, f"s{2 * j + 1}")
            wide.before_fill(pe, where, name)
            place = wide.place(where, name)
            for i in range(8):
                last = T.transpose(m.ps[0:SPAN, 2 * place + i // 4, (i % 4) * P:(i % 4 + 1) * P],
                                   f.prob[:, 8 * j + i, :], m.ident)
            last.then_inc(wide.made[place], 1)

        pe.wait_ge(s["turned"], t + 1)
        scores(0)
        scores(1)
        if ahead2:
            pe.wait_ge(s["staged"], t + 3)
            project(w, where, "q", 0, b, slice(WIN, KEYS))
        scores(2)
        scores(3)
        probs(0)
        if ahead2:
            project(w, where, "k", 1, b, slice(WIN, KEYS))
        probs(1)
        if ahead1:
            values(w, where, 1 - b, 0)
        wide.before_fill(pe, where, "heads")
        wide.after_read(pe, where, "p0")
        wide.after_read(pe, where, "p1")
        pe.wait_ge(s["v0_copied"], t + 1)
        pe.wait_ge(s["v1_copied"], t + 1)
        at = 2 * wide.place(where, "heads")
        for p, h in enumerate(ORDER):
            col = (h % 8) * DH
            for half in range(2):
                last = T.matmul(m.ps[HALF * half:HALF * (half + 1), at + h // 8, col:col + DH],
                                f.pT[0:SPAN, p, HALF * half:HALF * (half + 1)], f.v[0:SPAN, half, h * DH:(h + 1) * DH],
                                start=True, stop=True)
        last.then_inc(wide.made[wide.place(where, "heads")], 1)
        if ahead1:
            pe.wait_ge(s["rotated"], t + 2)
            turned(where, "t0", f.rot[1 - b], 0)
            turned(where, "t1", f.rot[1 - b], 4)
            values(w, where, 1 - b, 1)
        pe.wait_ge(s["normed"], t + 1)
        turned(where, "o0", f.o, 0)
        turned(where, "o1", f.o, 4)
        if ahead1:
            turned(where, "t2", f.rot[1 - b], 8)
            turned(where, "t3", f.rot[1 - b], 12)
        turn.before_fill(pe, where, "y")
        turn.after_read(pe, where, "o0")
        turn.after_read(pe, where, "o1")
        place = turn.place(where, "y")
        for k in range(QB):
            last = T.matmul(m.ps[:, 6 + place, 0:P], w.wo[:, k, :], f.oT[:, k, :], start=k == 0, stop=k == QB - 1)
        last.then_inc(turn.made[place], 1)

    def ffn(rnd, par):
        w = f.w[par]
        for i in range(NBLK):
            pe.wait_ge(s["shifted"], NBLK * rnd + i + 1)
            T.matmul(m.ps[:, i, :], f.mean, f.g.xc[:, i, :], start=True, stop=True).then_inc(s["mean"], 1)
        for i in range(NBLK):
            pe.wait_ge(s["squared"], NBLK * rnd + i + 1)
            T.matmul(m.ps[:, 4 + i, :], f.mean, f.g.sq[:, i, :], start=True, stop=True).then_inc(s["var"], 1)

        def second(i):
            pe.wait_ge(s["glu"], 12 * rnd + 3 * i + 3)
            if i == 0:
                pe.wait_ge(s["rstd"], NBLK * rnd + 4)
            if i >= 2:
                pe.wait_ge(s["added"], NBLK * rnd + i - 1)
            for k, rows in enumerate(FF_ROWS):
                last = T.matmul(m.ps[:, 6 + i % 2, :], w.w2[0:rows, k, :], f.g.u[i % 2][0:rows, k, :], start=k == 0,
                                stop=k == 2)
            last.then_inc(s["second"], 1)

        for i in range(NBLK):
            for k, rows in enumerate(FF_ROWS):
                p = 3 * i + k
                if k == 0:
                    pe.wait_ge(s["hn"], NBLK * rnd + i + 1)
                if p == 2:
                    pe.wait_ge(s["rstd"], NBLK * rnd + 2)
                if p >= 3:
                    pe.wait_ge(s["glu"], 12 * rnd + p - 2)
                for e in range(2):
                    at = e * FF + k * P
                    last = T.matmul(m.ps[0:rows, 2 * (p % 3) + e, :], w.w1[:, at:at + rows], m.hT[:, i * BLK:(i + 1) * BLK],
                                    start=True, stop=True)
                last.then_inc(s["first"], 1)
            if i > 0:
                second(i - 1)
        second(NBLK - 1)

    deep_rounds(pe, start, tile, ffn)

    pe.wait_ge(s["added"], NBLK * DEPTH)
    for t in range(TILES):
        b, c = divmod(t, BT)
        last = T.transpose(m.ps[:, t // 4, (t % 4) * P:(t % 4 + 1) * P],
                           f.xa[:, b, FRONT + c * P:FRONT + (c + 1) * P], m.ident)
        if t % 4 == 3:
            last.then_inc(s["final"], 1)


def deep_scalar(nc, act, m, s, f):
    A = nc.scalar.activation
    wide, score, turn = deep_rings(s)
    act.wait_ge(s["ready"], 1)

    def raw(where, name, j, b, square=False):
        wide.before_read(act, where, name)
        place = wide.place(where, name)
        A(f.raw[b][:, j * INNER:(j + 1) * INNER].rearrange("p (a b) -> p a b", a=2),
          m.ps[:, 2 * place:2 * place + 2, :], ACT.Copy).then_inc(wide.freed[place], 1)
        if square:
            act.drain()
            A(f.sq[b][:, j * INNER:(j + 1) * INNER], f.raw[b][:, j * INNER:(j + 1) * INNER], ACT.Square)
        if j == 1:
            act.drain().then_inc(s["raw"], 1)

    def values(where):
        wide.before_read(act, where, "v0")
        place = wide.place(where, "v0")
        A(f.v[0:SPAN, 0, :].rearrange("p (a b) -> p a b", a=2), m.ps[0:SPAN, 2 * place:2 * place + 2, :], ACT.Copy)\
            .then_inc(wide.freed[place], 1)
        act.drain().then_inc(s["v0_copied"], 1)

    def stage(t, c, b):
        A(f.xs[b][0:64, :], f.xa[0:64, b, bass.ds(1 + c * P, KEYS)], ACT.Copy)
        A(f.xs[b][64:P, :], f.xa[64:P, b, bass.ds(c * P, KEYS)], ACT.Copy)
        act.drain().then_inc(s["staged"], 1)

    def norms(t, b):
        act.wait_ge(s["sumsq"], t + 1)
        A(f.ss[b], f.ss[b], ACT.Ln, scale=NORM_SHIFT)
        act.drain()
        A(f.ss[b], f.ss[b], ACT.Exp, scale=-0.5).then_inc(s["rnorm"], 1)

    def turned(where, name, dst):
        turn.before_read(act, where, name)
        place = turn.place(where, name)
        A(dst, m.ps[:, 6 + place, :].rearrange("p (a b) -> p a b", a=4), ACT.Copy).then_inc(turn.freed[place], 1)

    def queries(where):
        turned(where, "t0", f.qT[:, 0:4, :])
        turned(where, "t1", f.qT[:, 4:8, :])

    def keys(where, b):
        turned(where, "t2", f.kT[b][:, 0:4, WIN:KEYS])
        turned(where, "t3", f.kT[b][:, 4:8, WIN:KEYS])
        act.drain().then_inc(s["turned"], 1)

    def carry(where, b):
        turn.before_read(act, where, "t0")
        A(f.kT[b][:, :, 0:WIN], f.kT[b][:, :, P:KEYS], ACT.Copy)
        act.drain()

    def start(rnd, dd, par):
        where = (rnd, "start", 0, 0)
        act.wait_ge(s["weights"][par], 16 * dd + 16)
        A(f.spare, f.eps, ACT.Copy)
        act.preload_act_table_set(EXP_LN)
        act.wait_ge(s["ready"], rnd + 2)
        for b in range(BATCH):
            stage(16 * rnd + b, 0, b)
        for b in range(BATCH):
            raw(where, f"q{b}", 0, b, square=b == 0)
            raw(where, f"k{b}", 1, b, square=b == 0)
        values(where)
        norms(16 * rnd, 0)
        carry(where, 0)
        queries(where)
        keys(where, 0)

    def tile(where, t, c, b, par, ahead2, ahead1):
        def exponentials(j):
            act.wait_ge(s["maxima"], 4 * t + j + 1)
            place = score.place(where, f"s{j}")
            for i in range(GROUP):
                p = GROUP * j + i
                last = A(f.prob[:, p, :], m.ps[:, 4 + place, i * SPAN:(i + 1) * SPAN], ACT.Exp,
                         bias=f.nmax[b][:, p:p + 1], accum_out=f.rsum[b][:, ORDER[p]:ORDER[p] + 1])
            last.then_inc(score.freed[place], 1)

        if ahead2:
            act.wait_ge(s["v1_copied"], t + 1)
            stage(t + 2, c + 1, b)
        if ahead1:
            norms(t + 1, 1 - b)
        exponentials(0)
        exponentials(1)
        if ahead2:
            act.wait_ge(s["rotated"], t + 1)
            raw(where, "q", 0, b)
        exponentials(2)
        exponentials(3)
        if ahead2:
            raw(where, "k", 1, b)
        wide.before_read(act, where, "p1")
        place = wide.place(where, "p1")
        A(f.pT[0:SPAN, 8:16, :], m.ps[0:SPAN, 2 * place:2 * place + 2, :].rearrange("p a (i b) -> p (a i) b", b=P),
          ACT.Copy).then_inc(wide.freed[place], 1)
        if ahead1:
            wide.before_read(act, where, "heads")
            values(where)
            carry(where, 1 - b)
            queries(where)
        turned(where, "o0", f.oT[:, 0:4, :])
        if ahead1:
            keys(where, 1 - b)

    def ffn(rnd, par):
        w = f.w[par]
        for i in range(NBLK):
            act.wait_ge(s["centred"], NBLK * rnd + i + 1)
            A(f.g.sq[:, i, :], f.g.xc[:, i, :], ACT.Square).then_inc(s["squared"], 1)
        for i in range(NBLK):
            act.wait_ge(s["var"], NBLK * rnd + i + 1)
            A(f.g.sq[:, i, :], m.ps[:, 4 + i, :], ACT.Ln, bias=f.eps)
            act.drain()
            A(f.g.sq[:, i, :], f.g.sq[:, i, :], ACT.Exp, scale=-0.5).then_inc(s["rstd"], 1)
        for p in range(3 * NBLK):
            k = p % 3
            rows = FF_ROWS[k]
            act.wait_ge(s["first"], 12 * rnd + p + 1)
            if p >= 2:
                act.wait_ge(s["glu"], 12 * rnd + p - 1)
            A(f.g.gl[0:rows, p % 2, :], m.ps[0:rows, 2 * (p % 3) + 1, :], ACT.Gelu,
              bias=w.b1[0:rows, 3 + k:4 + k]).then_inc(s["gelu"], 1)

    deep_rounds(act, start, tile, ffn)


def deep_vector(nc, dve, m, s, f):
    V = nc.vector
    wide, score, turn = deep_rings(s)
    for x in (f.xa, f.xb):
        V.memset(x[:, :, 0:FRONT], 0.0)
    V.tensor_copy(f.xa[:, :, FRONT:FRONT + SEQ], m.hT[:, :].rearrange("p (b t) -> p b t", b=BATCH))
    V.memset(f.mean, 1.0 / P)
    V.memset(f.eps, EPS)
    V.tensor_copy(f.identb, m.ident)
    V.tensor_copy(f.bands[:, 0, :], f.band0)
    V.tensor_copy(f.bands[:, 1:BT, :], repeat(f.band, BT - 1))
    dve.drain().then_inc(s["ready"], 1)

    def values(where):
        wide.before_read(dve, where, "v1")
        place = wide.place(where, "v1")
        V.tensor_copy(f.v[0:SPAN, 1, :].rearrange("p (a b) -> p a b", a=2), m.ps[0:SPAN, 2 * place:2 * place + 2, :])\
            .then_inc(wide.freed[place], 1)
        dve.drain().then_inc(s["v1_copied"], 1)

    def cosines(c, b):
        for j in range(2):
            V.tensor_tensor(f.rot[b][:, j * INNER:(j + 1) * INNER].rearrange("p (h d) -> p h d", d=DH),
                            f.raw[b][:, j * INNER:(j + 1) * INNER].rearrange("p (h d) -> p h d", d=DH),
                            f.tab[:, bass.ds(c, 1), 2 * j, :].broadcast_to([P, LH, DH]), ALU.mult)

    def norms(b):
        V.tensor_reduce(f.ss[b], f.sq[b].rearrange("p (h d) -> p h d", d=DH), AX, ALU.add)
        dve.drain()
        V.tensor_scalar(f.ss[b], f.ss[b], GUARD, None, ALU.max).then_inc(s["sumsq"], 1)

    def sines(c, b, js=(0, 1)):
        for j in js:
            raw = f.raw[b][:, j * INNER:(j + 1) * INNER].rearrange("p (h d) -> p h d", d=DH)
            to = f.sq[b][:, j * INNER:(j + 1) * INNER].rearrange("p (h d) -> p h d", d=DH)
            for e in range(2):
                here, there = slice(32 * e, 32 * e + 32), slice(32 - 32 * e, 64 - 32 * e)
                V.tensor_tensor(to[:, :, here], raw[:, :, there],
                                f.tab[:, bass.ds(c, 1), 2 * j + 1, here].broadcast_to([P, LH, 32]), ALU.mult)

    def rotate(t, b):
        dve.drain()
        V.tensor_tensor(f.rot[b], f.rot[b], f.sq[b], ALU.add)
        dve.drain()
        dve.wait_ge(s["rnorm"], t + 1)
        r = f.rot[b].rearrange("p (h d) -> p h d", d=DH)
        V.tensor_tensor(r, r, spread(f.ss[b], DH), ALU.mult).then_inc(s["rotated"], 1)

    def start(rnd, dd, par):
        where = (rnd, "start", 0, 0)
        for b in range(BATCH):
            V.memset(f.kT[b][:, :, P:KEYS], 0.0)
        dve.drain().then_inc(s["ready"], 1)
        dve.wait_ge(s["tables"], rnd + 1)
        dve.wait_ge(s["raw"], 16 * rnd + 1)
        norms(0)
        cosines(0, 0)
        sines(0, 0)
        rotate(16 * rnd, 0)
        values(where)
        dve.wait_ge(s["cosines"], 15 * rnd + 1)
        norms(1)

    def tile(where, t, c, b, par, ahead2, ahead1):
        def maxima(j):
            name = f"s{j}"
            score.before_read(dve, where, name)
            bank = 4 + score.place(where, name)
            V.tensor_reduce(f.nmax[b][:, GROUP * j:GROUP * (j + 1)],
                            m.ps[:, bank, 0:GROUP * SPAN].rearrange("p (h k) -> p h k", h=GROUP), AX, ALU.max,
                            negate=True).then_inc(s["maxima"], 1)

        maxima(0)
        maxima(1)
        if ahead1:
            sines(c + b, 1 - b, (0,))
        maxima(2)
        maxima(3)
        wide.before_read(dve, where, "p0")
        place = wide.place(where, "p0")
        V.tensor_copy(f.pT[0:SPAN, 0:8, :],
                      m.ps[0:SPAN, 2 * place:2 * place + 2, :].rearrange("p a (i b) -> p (a i) b", b=P))\
            .then_inc(wide.freed[place], 1)
        if ahead1:
            sines(c + b, 1 - b, (1,))
            rotate(t + 1, 1 - b)
        score.after_read(dve, where, "s2")
        score.after_read(dve, where, "s3")
        V.reciprocal(f.rsum[b], f.rsum[b])
        dve.drain()
        wide.before_read(dve, where, "heads")
        place = wide.place(where, "heads")
        V.tensor_tensor(f.o.rearrange("p (h d) -> p h d", d=DH),
                        m.ps[:, 2 * place:2 * place + 2, :].rearrange("p a (h d) -> p (a h) d", d=DH),
                        spread(f.rsum[b], DH), ALU.mult).then_inc(wide.freed[place], 1)
        dve.drain().then_inc(s["normed"], 1)
        turn.before_read(dve, where, "o1")
        place = turn.place(where, "o1")
        V.tensor_copy(f.oT[:, 4:8, :], m.ps[:, 6 + place, :].rearrange("p (a b) -> p a b", a=4))\
            .then_inc(turn.freed[place], 1)
        if ahead1:
            values(where)
        if ahead2:
            dve.wait_ge(s["cosines"], 15 * where[0] + 2 * c + b + 2)
            norms(b)
        turn.before_read(dve, where, "y")
        place = turn.place(where, "y")
        here = bass.ds(FRONT + c * P, P)
        V.tensor_tensor(f.xb[:, b, here], m.ps[:, 6 + place, 0:P], f.xa[:, b, here], ALU.add)\
            .then_inc(turn.freed[place], 1)

    def ffn(rnd, par):
        w = f.w[par]
        dve.drain()
        for i in range(NBLK):
            b, half = divmod(i, 2)
            at = half * BLK
            V.tensor_copy(f.g.xc[0:64, i, :], f.xb[0:64, b, FRONT + at:FRONT + at + BLK])
            V.tensor_copy(f.g.xc[64:P, i, :], f.xb[64:P, b, FRONT + at - 1:FRONT + at - 1 + BLK]).then_inc(s["shifted"], 1)
        for i in range(NBLK):
            dve.wait_ge(s["mean"], NBLK * rnd + i + 1)
            V.tensor_tensor(f.g.xc[:, i, :], f.g.xc[:, i, :], m.ps[:, i, :], ALU.subtract).then_inc(s["centred"], 1)
        for i in range(NBLK):
            dve.wait_ge(s["rstd"], NBLK * rnd + i + 1)
            V.tensor_tensor(f.g.xc[:, i, :], f.g.xc[:, i, :], f.g.sq[:, i, :], ALU.mult)
            dve.drain()
            V.tensor_scalar(m.hT[:, i * BLK:(i + 1) * BLK], f.g.xc[:, i, :], w.lng, w.lnb, ALU.mult, ALU.add)\
                .then_inc(s["hn"], 1)

        def add(i):
            b, half = divmod(i, 2)
            here = slice(FRONT + half * BLK, FRONT + (half + 1) * BLK)
            dve.wait_ge(s["second"], NBLK * rnd + i + 1)
            V.scalar_tensor_tensor(f.xa[:, b, here], m.ps[:, 6 + i % 2, :], w.b2, f.xb[:, b, here], ALU.add,
                                   ALU.add).then_inc(s["added"], 1)

        for i in range(NBLK):
            for k, rows in enumerate(FF_ROWS):
                p = 3 * i + k
                dve.wait_ge(s["gelu"], 12 * rnd + p + 1)
                if i >= 2 and k == 0:
                    dve.wait_ge(s["second"], NBLK * rnd + i - 1)
                V.scalar_tensor_tensor(f.g.u[i % 2][0:rows, k, :], m.ps[0:rows, 2 * (p % 3), :],
                                       w.b1[0:rows, k:k + 1], f.g.gl[0:rows, p % 2, :], ALU.add, ALU.mult)\
                    .then_inc(s["glu"], 1)
            if i > 0:
                add(i - 1)
        add(NBLK - 1)

    deep_rounds(dve, start, tile, ffn)
    for i in range(NBLK):
        dve.wait_ge(s["final"], i + 1)
        add_gated(nc, dve, m, m.ps[:, i, :].rearrange("p (a b) -> p a b", a=4), 4 * i, 4,
                  repeat(gate_row(m, 3, FFN, i // 2), 4), f.g.gl[:, i % 2, :].rearrange("p (a b) -> p a b", a=4))


def deep_gpsimd(nc, pool, m, s, f):
    G = nc.gpsimd
    pool.wait_ge(s["ready"], 1)

    def squares(t, c, b):
        pool.wait_ge(s["raw"], t + 1)
        G.tensor_tensor(f.sq[b], f.raw[b], f.raw[b], ALU.mult)
        for j in range(2):
            last = G.tensor_tensor(f.rot[b][:, j * INNER:(j + 1) * INNER].rearrange("p (h d) -> p h d", d=DH),
                                   f.raw[b][:, j * INNER:(j + 1) * INNER].rearrange("p (h d) -> p h d", d=DH),
                                   f.tab[:, bass.ds(c, 1), 2 * j, :].broadcast_to([P, LH, DH]), ALU.mult)
        last.then_inc(s["cosines"], 1)

    def start(rnd, dd, par):
        pool.wait_ge(s["weights"][par], 16 * dd + 16)
        pool.wait_ge(s["rotary"], 16 * rnd + 16)
        w = f.w[par]
        for j, scale in ((0, w.qs), (1, w.qs), (2, w.ks), (3, w.ks)):
            if j % 2 == 0:
                G.tensor_tensor(f.tab[:, :, j, :], f.tab[:, :, j, :], repeat(scale, BT), ALU.mult)
            else:
                for e in range(2):
                    here, there = slice(32 * e, 32 * e + 32), slice(32 - 32 * e, 64 - 32 * e)
                    G.tensor_tensor(f.tab[:, :, j, here], f.tab[:, :, j, here], repeat(scale[:, there], BT), ALU.mult)
        pool.drain().then_inc(s["tables"], 1)
        squares(16 * rnd + 1, 0, 1)

    def tile(where, t, c, b, par, ahead2, ahead1):
        if ahead2:
            pool.wait_ge(s["turned"], t + 1)
            squares(t + 2, c + 1, b)

    deep_rounds(pool, start, tile, None)


def deep_sync(nc, sp, m, s, f):
    def rotary():
        sp.dma_start(f.tab_flat, m.d["rotary"]).then_inc(s["rotary"], 16)

    def attended(rnd):
        sp.wait_ge(s["rotated"], 16 * (rnd + 1))
        rotary()

    rotary()
    for par in range(2):
        sp.dma_start(f.wbuf[par], m.d["deep"][par]).then_inc(s["weights"][par], 16)
    with sp.Fori(0, DEPTH // 2 - 1) as dd:
        for par in range(2):
            attended(2 * dd + par)
            sp.wait_ge(s["added"], NBLK * (2 * dd + par + 1))
            sp.dma_start(f.wbuf[par], m.d["deep"][bass.ds(2 * dd + par + 2, 1)].rearrange("a p n -> (a p) n"))\
                .then_inc(s["weights"][par], 16)
    attended(DEPTH - 2)
    sp.wait_ge(s["rotary"], 16 * DEPTH)


EXP_LN = "natural_log_exp_and_others"
DEEP_SEMS = ("rotary", "weights0", "weights1", "ready", "staged", "wide_made0", "wide_made1", "wide_freed0",
             "wide_freed1", "score_made0", "score_made1", "score_freed0", "score_freed1", "turn_made0", "turn_made1",
             "turn_freed0", "turn_freed1", "raw", "tables", "cosines", "sumsq", "rnorm", "rotated", "turned", "maxima",
             "v0_copied", "v1_copied", "normed", "shifted", "mean", "centred", "squared", "var", "rstd", "hn", "first",
             "gelu", "glu", "second", "added", "final")


def deep_setup(m):
    f = Memory()
    f.band, f.band0 = view(m.packs["const"], "const", "band"), view(m.packs["const"], "const", "band0")
    n = columns("deep")
    assert 2 * n <= DEEP_AT
    f.wbuf = [m.arena[:, par * n:(par + 1) * n] for par in range(2)]
    f.w = []
    for buf in f.wbuf:
        w = Memory()
        w.wqkv, w.w1, w.b1, w.b2, w.qs, w.ks, w.lng, w.lnb = (
            view(buf, "deep", name) for name in ("wqkv", "w1", "b1", "b2", "qs", "ks", "lng", "lnb"))
        w.wo = view(buf, "deep", "wo").rearrange("p (a b) -> p a b", a=QB)
        w.w2 = view(buf, "deep", "w2").rearrange("p (a b) -> p a b", a=3)
        f.w.append(w)
    old = Carver(m.packs["tern"])
    f.xa, f.xb = (old.take(BATCH * (FRONT + SEQ)).rearrange("p (b t) -> p b t", b=BATCH) for _ in range(2))
    f.oT = old.take(INNER).rearrange("p (a b) -> p a b", b=P)
    f.o = m.packs["l1"][:, 0:INNER]
    f.qT = m.packs["mole"][:, 0:INNER].rearrange("p (a b) -> p a b", b=P)
    a = Carver(m.arena, DEEP_AT)
    f.raw = [m.hT[:, :], a.take(2 * INNER)]
    f.rot = [a.take(2 * INNER) for _ in range(2)]
    f.sq = [a.take(2 * INNER) for _ in range(2)]
    f.pT = a.take(LH * P).rearrange("p (a b) -> p a b", b=P)
    f.v = a.take(2 * INNER).rearrange("p (a b) -> p a b", a=2)
    f.prob = a.take(LH * SPAN).rearrange("p (a b) -> p a b", b=SPAN)
    f.kT = [a.take(QB * KEYS).rearrange("p (a b) -> p a b", b=KEYS) for _ in range(2)]
    f.xs = [a.take(KEYS) for _ in range(2)]
    f.tab_flat = a.take(BT * 4 * DH)
    f.tab = f.tab_flat.rearrange("p (c j d) -> p c j d", c=BT, j=4)
    f.bands = a.bf16(BT * SPAN).rearrange("p (c k) -> p c k", k=SPAN)
    f.identb = a.bf16(P)
    f.mean = a.take(P)
    f.eps, f.spare = a.take(1), a.take(1)
    f.ss = [a.take(2 * LH) for _ in range(2)]
    f.nmax = [a.take(LH) for _ in range(2)]
    f.rsum = [a.take(LH) for _ in range(2)]
    g = Memory()
    b = Carver(m.arena, DEEP_AT)
    four = lambda: b.take(TOK).rearrange("p (a b) -> p a b", b=BLK)
    g.xc, g.sq = four(), four()
    g.gl = b.take(2 * BLK).rearrange("p (a b) -> p a b", b=BLK)
    g.u = [b.take(3 * BLK).rearrange("p (a b) -> p a b", b=BLK) for _ in range(2)]
    f.g = g
    return f


def build(nc, d, out):
    with ExitStack() as ctx:
        def sb(name, shape, dt=F32):
            return ctx.enter_context(nc.sbuf_tensor(name, shape, dt))

        def sem(name):
            return ctx.enter_context(nc.semaphore(name))

        m = Memory()
        m.d = d
        m.ps = ctx.enter_context(nc.psum_tensor("ps", [P, 8, BLK], F32))
        m.x = sb("x", [P, TILES, P])
        m.hT = sb("hT", [P, TOK])
        m.masks = sb("masks", [P, (FINE + 1) * BLOCK])
        m.packs = {k: sb("pack_" + k, [P, columns(k)]) for k in ("const", "l0", "tern", "l1", "mole", "l2", "l3")}
        m.arena = sb("arena", [P, ARENA])
        m.sc = sb("sc", [P, 2 * LAYERS])
        m.modc = sb("modc", [P, 8 * LAYERS])
        m.grow = sb("grow", [P, LAYERS, 4 * P])
        m.stats = sb("stats", [P, TILES, 6])
        m.mv = sb("mv", [P, TILES, 2])
        m.rstd = sb("rstd", [P, TILES])
        m.nhalf = sb("nhalf", [P, 64])
        m.ident = view(m.packs["const"], "const", "ident")
        m.cT = view(m.packs["const"], "const", "cT")
        first = Carver(m.arena)
        wmod = first.take(columns("mod"))
        m.wmod = wmod.rearrange("p (l a b) -> p l a b", l=LAYERS, a=6)
        m.scwide = first.take(2 * LAYERS * P).rearrange("p (a b) -> p a b", b=P)
        m.gtmp = first.take(LAYERS * BLK).rearrange("p (a b) -> p a b", b=BLK)
        m.xn = m.arena[:, ARENA - TOK:ARENA].rearrange("p (a b) -> p a b", b=P)

        m.loaded = {k: sem("loaded_" + k) for k in list(m.packs) + ["mod", "x"]}
        m.stage_done = sem("stage_done")
        m.out_written = sem("out_written")


        def sems(stage, names):
            s = {n: sem(f"{stage}_{n}") for n in names}
            for n in [n[:-1] for n in names if n.endswith("0")]:
                s[n] = [s[f"{n}{i}"] for i in range(4) if f"{n}{i}" in names]
            return s

        mod, ln, tern = sems("mod", MOD_SEMS), sems("ln", LN_SEMS), sems("tern", TERN_SEMS)
        attn_s = [sems("gla0", GLA_SEMS), sems("gla1", GLA_SEMS), sems("ssm", SSM_SEMS), sems("mha", MHA_SEMS)]
        attn_m = [gla_setup(m, 0), gla_setup(m, 1), ssm_setup(m), mha_setup(m)]
        ffn_s = [tern, sems("mole", MOLE_SEMS), tern, sems("deep", DEEP_SEMS)]
        ffn_m = [tern_setup(m, 0), mole_setup(m), tern_setup(m, 2), deep_setup(m)]

        block = ctx.enter_context(nc.Block())

        @block.sync
        def _(sp):
            sp.dma_start(m.packs["const"][:, :], d["const"]).then_inc(m.loaded["const"], 16)
            sp.dma_start(wmod, d["mod"]).then_inc(m.loaded["mod"], 16)
            sp.dma_start(m.x[:, :, :], d["x"].rearrange("b (t p) f -> p (b t) f", p=P)).then_inc(m.loaded["x"], 16)
            sp.dma_start(m.masks[:, :], d["masks"]).then_inc(m.loaded["x"], 16)
            for k in ("l0", "tern", "l1", "mole", "l2", "l3"):
                sp.dma_start(m.packs[k][:, :], d[k]).then_inc(m.loaded[k], 16)
            sp.wait_ge(m.stage_done, ENGINES * 5)
            sp.dma_start(m.packs["tern"][:, :], d["tern2"]).then_inc(m.loaded["tern"], 16)
            sp.wait_ge(m.stage_done, ENGINES * 14)
            mha_sync(nc, sp, m, attn_s[3], attn_m[3])
            sp.wait_ge(m.stage_done, ENGINES * 16)
            deep_sync(nc, sp, m, ffn_s[3], ffn_m[3])
            sp.wait_ge(m.stage_done, ENGINES * 17)
            sp.dma_start(out.rearrange("b (t p) f -> p (b t) f", p=P), m.x[:, :, :]).then_inc(m.out_written, 16)
            sp.wait_ge(m.out_written, 16)
            for name, loaded in m.loaded.items():
                sp.wait_ge(loaded, 32 if name in ("tern", "x") else 16)

        @block.tensor
        def _(pe):
            mod_tensor(nc, pe, m, mod)
            finish_stage(pe, m, 0)
            for l in range(LAYERS):
                ln_tensor(nc, pe, m, ln, 2 * l)
                finish_stage(pe, m, 1 + 4 * l)
                (gla_tensor, gla_tensor, ssm_tensor, mha_tensor)[l](nc, pe, m, attn_s[l], attn_m[l])
                finish_stage(pe, m, 2 + 4 * l)
                ln_tensor(nc, pe, m, ln, 2 * l + 1)
                finish_stage(pe, m, 3 + 4 * l)
                (tern_tensor, mole_tensor, tern_tensor, deep_tensor)[l](nc, pe, m, ffn_s[l], ffn_m[l])
                finish_stage(pe, m, 4 + 4 * l)

        @block.scalar
        def _(act):
            mod_scalar(nc, act, m, mod)
            finish_stage(act, m, 0)
            for l in range(LAYERS):
                ln_scalar(nc, act, m, ln, 2 * l, l, ATTN)
                finish_stage(act, m, 1 + 4 * l)
                (gla_scalar, gla_scalar, ssm_scalar, mha_scalar)[l](nc, act, m, attn_s[l], attn_m[l])
                finish_stage(act, m, 2 + 4 * l)
                ln_scalar(nc, act, m, ln, 2 * l + 1, l, FFN)
                finish_stage(act, m, 3 + 4 * l)
                (tern_scalar, mole_scalar, tern_scalar, deep_scalar)[l](nc, act, m, ffn_s[l], ffn_m[l])
                finish_stage(act, m, 4 + 4 * l)

        @block.vector
        def _(dve):
            dve.wait_ge(m.loaded["x"], 32)
            mod_vector(nc, dve, m, mod)
            finish_stage(dve, m, 0)
            for l in range(LAYERS):
                ln_vector(nc, dve, m, ln, 2 * l)
                finish_stage(dve, m, 1 + 4 * l)
                (gla_vector, gla_vector, ssm_vector, mha_vector)[l](nc, dve, m, attn_s[l], attn_m[l])
                finish_stage(dve, m, 2 + 4 * l)
                ln_vector(nc, dve, m, ln, 2 * l + 1)
                finish_stage(dve, m, 3 + 4 * l)
                (tern_vector, mole_vector, tern_vector, deep_vector)[l](nc, dve, m, ffn_s[l], ffn_m[l])
                finish_stage(dve, m, 4 + 4 * l)

        @block.gpsimd
        def _(pool):
            nc.gpsimd.memset(m.nhalf[:, :], -0.5)
            pool.drain()
            finish_stage(pool, m, 0)
            for l in range(LAYERS):
                ln_gpsimd(nc, pool, m, ln, 2 * l)
                finish_stage(pool, m, 1 + 4 * l)
                if l in (0, 1):
                    gla_gpsimd(nc, pool, m, attn_s[l], attn_m[l])
                if l == 3:
                    mha_gpsimd(nc, pool, m, attn_s[l], attn_m[l])
                finish_stage(pool, m, 2 + 4 * l)
                ln_gpsimd(nc, pool, m, ln, 2 * l + 1)
                finish_stage(pool, m, 3 + 4 * l)
                if l == 3:
                    deep_gpsimd(nc, pool, m, ffn_s[l], ffn_m[l])
                finish_stage(pool, m, 4 + 4 * l)


def pad(a, rows=P):
    a = a.reshape(a.shape[0], -1)
    out = np.zeros((rows, a.shape[1]), a.dtype)
    out[:a.shape[0]] = a
    return out


def by_rows(a):
    k = -(-a.shape[0] // P)
    a = pad(a, k * P)
    return a.reshape(k, P, -1).transpose(1, 0, 2).reshape(P, -1)


def col(v):
    return by_rows(v.reshape(-1, 1))


def rows_of(v):
    return np.broadcast_to(v.reshape(1, -1), (P, v.size))


def pack(name, parts):
    assert set(parts) == {n for n, _ in PACKS[name]}, name
    out = [pad(np.asarray(parts[n])) for n, _ in PACKS[name]]
    assert [a.shape[1] for a in out] == [c for _, c in PACKS[name]], [(n, a.shape) for (n, _), a in zip(PACKS[name], out)]
    return np.ascontiguousarray(np.concatenate(out, axis=1))


def level_masks():
    j, i = np.meshgrid(np.arange(P) % BLOCK, np.arange(BLOCK), indexing="ij")
    out = [((i >> lev) == (j >> lev) + 1) & ((j >> lev) % 2 == 0) for lev in range(FINE)] + [i == j]
    return np.ascontiguousarray(np.stack(out, axis=1).astype(np.float32).reshape(P, -1))


def rotary_tables():
    half = np.arange(0, 64, 2, dtype=np.float32)
    inv_freq = (np.float32(1.0) / np.float32(10000.0) ** (half / np.float32(64))).astype(np.float32)
    t = np.arange(SEQ, dtype=np.float32)
    freqs = np.concatenate([t[:, None] * inv_freq[None, :]] * 2, -1).astype(np.float32)
    base = ((half + np.float32(0.4 * 64)) / np.float32(1.4 * 64)).astype(np.float32)
    power = ((t - SEQ // 2) / np.float32(16)).astype(np.float32)
    scale = np.power(base[None, :], power[:, None]).astype(np.float32)
    scale = np.concatenate([scale, scale], -1)
    sign = np.concatenate([-np.ones(32), np.ones(32)]).astype(np.float32)
    cos, sin = np.cos(freqs).astype(np.float32), np.sin(freqs).astype(np.float32) * sign
    inv = np.float32(1.0) / scale
    tables = np.stack([8192 * cos * scale, 8192 * sin * scale, 1024 * cos * inv, 1024 * sin * inv], axis=1)
    return np.ascontiguousarray(tables.reshape(BT, P, 4, 64).transpose(1, 0, 2, 3).reshape(P, -1).astype(np.float32))


def band_masks():
    i, j = np.arange(P)[:, None], np.arange(96)[None, :] - 32
    seen = (j <= i % 64) & (j >= i % 64 - 32)
    first = seen & ((j >= 0) | (i >= 64))
    big = np.float32(-1e30)
    return np.where(seen, np.float32(0), big), np.where(first, np.float32(0), big)


def kernel(**inputs):
    import concourse.bacc as _bacc
    from concourse.bass_utils import run_bass_kernel_spmd as _run

    i = {k: np.asarray(v) for k, v in inputs.items()}
    band, band0 = band_masks()
    arrays = {
        "const": pack("const", {"ident": np.eye(P, dtype=np.float32), "band": band, "band0": band0,
                                "cT": np.concatenate([i[f"L{l}_c"].T for l in range(LAYERS)], axis=1)}),
        "masks": level_masks(),
        "rotary": rotary_tables(),
        "mod": pack("mod", {"wmod": np.concatenate([i[f"L{l}_wmod"] for l in range(LAYERS)], axis=1)}),
        "x": i["L0_attn_x"],
        "l0": pack("l0", {"wq": i["L0_attn_Wq"], "wk": i["L0_attn_Wk"], "wv": i["L0_attn_Wv"],
                          "g1": i["L0_attn_G1"], "g2": i["L0_attn_G2"], "wo": i["L0_attn_Wo"],
                          "delta": col(i["L0_attn_delta"]), "nw": col(i["L0_attn_norm_w"])}),
        "l1": pack("l1", {"wq": i["L1_attn_Wq"], "wk": i["L1_attn_Wk"], "wv": i["L1_attn_Wv"],
                          "wg": i["L1_attn_Wg"], "gk1": i["L1_attn_gk_w1"], "gk2": i["L1_attn_gk_w2"],
                          "b2": col(i["L1_attn_gk_b2"]),
                          "nw": col(np.concatenate([i["L1_attn_g_norm_w"]] * 2)), "wo": by_rows(i["L1_attn_Wo"])}),
        "mole": pack("mole", {
            "w1": i["L1_ffn_W1"], "w2": by_rows(i["L1_ffn_W2"]),
            "ar1": np.concatenate([i["L1_ffn_A1"].transpose(1, 0, 2).reshape(P, 24), i["L1_ffn_R1"]], axis=1),
            "b1": np.concatenate([i["L1_ffn_B1"].reshape(24, HID), i["L1_ffn_b1"].reshape(1, -1)]),
            "ar2": by_rows(np.concatenate([i["L1_ffn_A2"].transpose(1, 0, 2).reshape(HID, 24), i["L1_ffn_R2"]], axis=1)),
            "b2": np.concatenate([i["L1_ffn_B2"].reshape(24, P), i["L1_ffn_b2"].reshape(1, -1)])}),
        "l2": pack("l2", {"win": i["L2_attn_W_in"].T,
                          "cw": by_rows(i["L2_attn_conv_w"][:, 0, :]), "cb": col(i["L2_attn_conv_b"]),
                          "alog": by_rows(i["L2_attn_A_log"]), "d": col(i["L2_attn_D"]),
                          "wout": by_rows(i["L2_attn_W_out"].T)}),
        "l3": pack("l3", {"wq": i["L3_attn_W_query"].transpose(1, 0, 2).reshape(P, P),
                          "wk": i["L3_attn_W_key"].transpose(1, 0, 2).reshape(P, P),
                          "wv": i["L3_attn_W_val"].transpose(1, 0, 2).reshape(P, P),
                          "wo": i["L3_attn_W_out"].reshape(P, P)}),
    }
    for l, name in ((0, "tern"), (2, "tern2")):
        f = lambda k: i[f"L{l}_ffn_{k}"]
        arrays[name] = pack("tern", {
            "w1": f("w1_w").T, "w2": f("w2_w").T, "h1": by_rows(f("h1_w").T), "h2": by_rows(f("h2_w").T),
            "w3": by_rows(f("w3_w").T), "s1": col(f("w1_s")), "s2": col(f("w2_s")), "sh1": col(f("h1_s")),
            "sh2": col(f("h2_s")), "s3": rows_of(f("w3_s"))})
    g = lambda k: i[f"L3_ffn_{k}"]

    def halves(b):
        return np.concatenate([col(b[:341]), col(b[341:])], axis=1)

    arrays["deep"] = np.stack([pack("deep", {
        "wqkv": g("Wqkv")[r], "wo": by_rows(g("Wo")[r]), "w1": g("W1")[r], "w2": by_rows(g("W2")[r]),
        "b1": halves(g("b1")[r]), "b2": col(g("b2")[r]), "qs": rows_of(g("q_scale")[r]),
        "ks": rows_of(g("k_scale")[r]), "lng": col(g("ln_g")[r]), "lnb": col(g("ln_b")[r])}) for r in range(DEPTH)])

    nc = _bacc.Bacc("TRN2", target_bir_lowering=False, num_devices=1)
    feeds, drams = {}, {}
    for name, a in arrays.items():
        feeds["in_" + name] = np.ascontiguousarray(a)
        drams[name] = nc.dram_tensor("in_" + name, a.shape, mybir.dt.from_np(a.dtype), kind="ExternalInput").ap()
    out = nc.dram_tensor("out", (BATCH, SEQ, P), F32, kind="ExternalOutput").ap()
    drams["nc"] = nc
    build(nc, drams, out)
    return _run(nc, [feeds], core_ids=[0]).results[0]["out"]
```
